# Optimizing a Trainium2 kernel written in Bass

```python
import numpy as np
import jax
import jax.numpy as jnp

def _softmax(x, axis=-1):
    return jax.nn.softmax(x, axis=axis)

def _gelu(x):
    return jax.nn.gelu(x, approximate=True)

def _silu(x):
    return jax.nn.silu(x)

def _sigmoid(x):
    return jax.nn.sigmoid(x)

def _layernorm(x, axis=-1, eps=1e-05):
    m = jnp.mean(x, axis=axis, keepdims=True)
    v = jnp.var(x, axis=axis, keepdims=True)
    return (x - m) / jnp.sqrt(v + eps)

def _scatter_add(tgt, idx, src, axis=0):
    return tgt.at[idx].add(src)

def _segment_sum(src, seg, n):
    return jax.ops.segment_sum(src, seg, n)
kernel_name = 'mk_prb_d1_jaxref_r4_f7141c'

def setup_inputs(seed: int=0):
    np.random.seed(seed)
    _w = jnp.asarray

    def _L0_attn_setup():
        import jax, jax.numpy as jnp
        import numpy as np
        D_MODEL = 256
        STATE = 64
        HEADS = 8
        EXPAND = 2
        INNER = EXPAND * D_MODEL
        HEAD_DIM = INNER // HEADS
        PROJ_OUT = 2 * INNER + 2 * STATE + HEADS
        BATCH, SEQ = (2, 256)
        EPS = 1e-05

        def _layer_norm(x, gamma, beta):
            mu = jnp.mean(x, axis=-1, keepdims=True)
            xc = x - mu
            var = jnp.mean(xc * xc, axis=-1, keepdims=True)
            return xc * jax.lax.rsqrt(var + EPS) * gamma + beta

        def _mamba2(u, W_in, b_in, A_log, D_skip, dt_bias, W_out, b_out):
            B, L, _ = u.shape
            zxbcdt = u @ W_in + b_in
            z = zxbcdt[..., :INNER]
            xs = zxbcdt[..., INNER:2 * INNER].reshape(B, L, HEADS, HEAD_DIM)
            Bm = zxbcdt[..., 2 * INNER:2 * INNER + STATE]
            Cm = zxbcdt[..., 2 * INNER + STATE:2 * INNER + 2 * STATE]
            dt = jax.nn.softplus(zxbcdt[..., 2 * INNER + 2 * STATE:] + dt_bias)
            A = -jnp.exp(A_log)
            decay = jnp.exp(dt * A)
            dtx = dt[..., None] * xs

            def step(h, inp):
                dec_t, dtx_t, B_t, C_t = inp
                h = dec_t[:, :, None, None] * h + dtx_t[..., None] * B_t[:, None, None, :]
                y = jnp.einsum('bhpn,bn->bhp', h, C_t)
                return (h, y)
            h0 = jnp.zeros((B, HEADS, HEAD_DIM, STATE), u.dtype)
            scan_in = (jnp.moveaxis(decay, 1, 0), jnp.moveaxis(dtx, 1, 0), jnp.moveaxis(Bm, 1, 0), jnp.moveaxis(Cm, 1, 0))
            _, ys = jax.lax.scan(step, h0, scan_in)
            y = jnp.moveaxis(ys, 0, 1)
            y = y + D_skip[None, None, :, None] * xs
            y = y.reshape(B, L, INNER) * jax.nn.silu(z)
            return y @ W_out + b_out
        key = jax.random.key(seed)
        ks = jax.random.split(key, 6)
        g = lambda k, shape, sc: jax.random.normal(k, shape, jnp.float32) * sc
        return {'input_tensor': jax.random.normal(ks[0], (BATCH, SEQ, D_MODEL), jnp.float32), 'ln_gamma': jnp.ones((D_MODEL,), jnp.float32), 'ln_beta': jnp.zeros((D_MODEL,), jnp.float32), 'W_in': g(ks[1], (D_MODEL, PROJ_OUT), 0.02), 'b_in': jnp.zeros((PROJ_OUT,), jnp.float32), 'A_log': jnp.log(jnp.arange(1, HEADS + 1, dtype=jnp.float32)), 'D_skip': jnp.ones((HEADS,), jnp.float32), 'dt_bias': g(ks[2], (HEADS,), 0.1), 'W_out': g(ks[3], (INNER, D_MODEL), 0.02), 'b_out': jnp.zeros((D_MODEL,), jnp.float32)}
    _L0_attn_in = _L0_attn_setup()

    def _L0_ffn_setup():
        import jax, jax.numpy as jnp
        import numpy as np
        D_MODEL = 256
        N_HEAD = 16
        HEAD_DIM = D_MODEL // N_HEAD
        D_FF = 1024
        N_EXPERTS = 4
        EPS = 1e-05

        def _layer_norm(x, gamma, beta):
            mu = jnp.mean(x, axis=-1, keepdims=True)
            var = jnp.mean((x - mu) ** 2, axis=-1, keepdims=True)
            return (x - mu) / jnp.sqrt(var + EPS) * gamma + beta
        key = jax.random.key(seed)
        ks = jax.random.split(key, 20)
        f32 = jnp.float32
        sc = 1.0 / np.sqrt(D_MODEL)
        scf = 1.0 / np.sqrt(D_FF)
        return {'src': jax.random.normal(ks[0], (4, 128, D_MODEL), f32), 'Wq': jax.random.normal(ks[1], (D_MODEL, D_MODEL), f32) * sc, 'bq': jnp.zeros((D_MODEL,), f32), 'Wk': jax.random.normal(ks[2], (D_MODEL, D_MODEL), f32) * sc, 'bk': jnp.zeros((D_MODEL,), f32), 'Wv': jax.random.normal(ks[3], (D_MODEL, D_MODEL), f32) * sc, 'bv': jnp.zeros((D_MODEL,), f32), 'Wo': jax.random.normal(ks[4], (D_MODEL, D_MODEL), f32) * sc, 'bo': jnp.zeros((D_MODEL,), f32), 'router_w': jax.random.normal(ks[5], (D_MODEL, 1), f32) * 0.05, 'router_b': jnp.zeros((1,), f32), 'W1': jax.random.normal(ks[6], (N_EXPERTS, D_MODEL, D_FF), f32) * sc, 'b1': jnp.zeros((N_EXPERTS, D_FF), f32), 'W2': jax.random.normal(ks[7], (N_EXPERTS, D_FF, D_MODEL), f32) * scf, 'b2': jnp.zeros((N_EXPERTS, D_MODEL), f32), 'ln1_g': jnp.ones((D_MODEL,), f32), 'ln1_b': jnp.zeros((D_MODEL,), f32), 'ln2_g': jnp.ones((D_MODEL,), f32), 'ln2_b': jnp.zeros((D_MODEL,), f32)}
    _L0_ffn_in = _L0_ffn_setup()
    _d = {'L0_attn_input_tensor': _L0_attn_in['input_tensor'], 'L0_attn_ln_gamma': _L0_attn_in['ln_gamma'], 'L0_attn_ln_beta': _L0_attn_in['ln_beta'], 'L0_attn_W_in': _L0_attn_in['W_in'], 'L0_attn_b_in': _L0_attn_in['b_in'], 'L0_attn_A_log': _L0_attn_in['A_log'], 'L0_attn_D_skip': _L0_attn_in['D_skip'], 'L0_attn_dt_bias': _L0_attn_in['dt_bias'], 'L0_attn_W_out': _L0_attn_in['W_out'], 'L0_attn_b_out': _L0_attn_in['b_out'], 'L0_ffn_Wq': _L0_ffn_in['Wq'], 'L0_ffn_bq': _L0_ffn_in['bq'], 'L0_ffn_Wk': _L0_ffn_in['Wk'], 'L0_ffn_bk': _L0_ffn_in['bk'], 'L0_ffn_Wv': _L0_ffn_in['Wv'], 'L0_ffn_bv': _L0_ffn_in['bv'], 'L0_ffn_Wo': _L0_ffn_in['Wo'], 'L0_ffn_bo': _L0_ffn_in['bo'], 'L0_ffn_router_w': _L0_ffn_in['router_w'], 'L0_ffn_router_b': _L0_ffn_in['router_b'], 'L0_ffn_W1': _L0_ffn_in['W1'], 'L0_ffn_b1': _L0_ffn_in['b1'], 'L0_ffn_W2': _L0_ffn_in['W2'], 'L0_ffn_b2': _L0_ffn_in['b2'], 'L0_ffn_ln1_g': _L0_ffn_in['ln1_g'], 'L0_ffn_ln1_b': _L0_ffn_in['ln1_b'], 'L0_ffn_ln2_g': _L0_ffn_in['ln2_g'], 'L0_ffn_ln2_b': _L0_ffn_in['ln2_b']}
    _x0 = _d['L0_attn_input_tensor']
    _d['L0_attn_input_tensor'] = jax.random.normal(jax.random.fold_in(jax.random.key(seed), 1), (8, 512, 256), dtype=_x0.dtype)
    del _x0
    return _d

def reference(L0_attn_input_tensor, L0_attn_ln_gamma, L0_attn_ln_beta, L0_attn_W_in, L0_attn_b_in, L0_attn_A_log, L0_attn_D_skip, L0_attn_dt_bias, L0_attn_W_out, L0_attn_b_out, L0_ffn_Wq, L0_ffn_bq, L0_ffn_Wk, L0_ffn_bk, L0_ffn_Wv, L0_ffn_bv, L0_ffn_Wo, L0_ffn_bo, L0_ffn_router_w, L0_ffn_router_b, L0_ffn_W1, L0_ffn_b1, L0_ffn_W2, L0_ffn_b2, L0_ffn_ln1_g, L0_ffn_ln1_b, L0_ffn_ln2_g, L0_ffn_ln2_b):

    def _L0_attn_ref(input_tensor, ln_gamma, ln_beta, W_in, b_in, A_log, D_skip, dt_bias, W_out, b_out):
        import jax, jax.numpy as jnp
        import numpy as np
        D_MODEL = 256
        STATE = 64
        HEADS = 8
        EXPAND = 2
        INNER = EXPAND * D_MODEL
        HEAD_DIM = INNER // HEADS
        PROJ_OUT = 2 * INNER + 2 * STATE + HEADS
        BATCH, SEQ = (2, 256)
        EPS = 1e-05

        def _layer_norm(x, gamma, beta):
            mu = jnp.mean(x, axis=-1, keepdims=True)
            xc = x - mu
            var = jnp.mean(xc * xc, axis=-1, keepdims=True)
            return xc * jax.lax.rsqrt(var + EPS) * gamma + beta

        def _mamba2(u, W_in, b_in, A_log, D_skip, dt_bias, W_out, b_out):
            B, L, _ = u.shape
            zxbcdt = u @ W_in + b_in
            z = zxbcdt[..., :INNER]
            xs = zxbcdt[..., INNER:2 * INNER].reshape(B, L, HEADS, HEAD_DIM)
            Bm = zxbcdt[..., 2 * INNER:2 * INNER + STATE]
            Cm = zxbcdt[..., 2 * INNER + STATE:2 * INNER + 2 * STATE]
            dt = jax.nn.softplus(zxbcdt[..., 2 * INNER + 2 * STATE:] + dt_bias)
            A = -jnp.exp(A_log)
            decay = jnp.exp(dt * A)
            dtx = dt[..., None] * xs

            def step(h, inp):
                dec_t, dtx_t, B_t, C_t = inp
                h = dec_t[:, :, None, None] * h + dtx_t[..., None] * B_t[:, None, None, :]
                y = jnp.einsum('bhpn,bn->bhp', h, C_t)
                return (h, y)
            h0 = jnp.zeros((B, HEADS, HEAD_DIM, STATE), u.dtype)
            scan_in = (jnp.moveaxis(decay, 1, 0), jnp.moveaxis(dtx, 1, 0), jnp.moveaxis(Bm, 1, 0), jnp.moveaxis(Cm, 1, 0))
            _, ys = jax.lax.scan(step, h0, scan_in)
            y = jnp.moveaxis(ys, 0, 1)
            y = y + D_skip[None, None, :, None] * xs
            y = y.reshape(B, L, INNER) * jax.nn.silu(z)
            return y @ W_out + b_out
        normed = _layer_norm(input_tensor, ln_gamma, ln_beta)
        out = _mamba2(normed, W_in, b_in, A_log, D_skip, dt_bias, W_out, b_out)
        return input_tensor + out

    def _L0_ffn_ref(src, Wq, bq, Wk, bk, Wv, bv, Wo, bo, router_w, router_b, W1, b1, W2, b2, ln1_g, ln1_b, ln2_g, ln2_b):
        import jax, jax.numpy as jnp
        import numpy as np
        D_MODEL = 256
        N_HEAD = 16
        HEAD_DIM = D_MODEL // N_HEAD
        D_FF = 1024
        N_EXPERTS = 4
        EPS = 1e-05

        def _layer_norm(x, gamma, beta):
            mu = jnp.mean(x, axis=-1, keepdims=True)
            var = jnp.mean((x - mu) ** 2, axis=-1, keepdims=True)
            return (x - mu) / jnp.sqrt(var + EPS) * gamma + beta
        B, T, _ = src.shape
        q = (src @ Wq + bq).reshape(B, T, N_HEAD, HEAD_DIM)
        k = (src @ Wk + bk).reshape(B, T, N_HEAD, HEAD_DIM)
        v = (src @ Wv + bv).reshape(B, T, N_HEAD, HEAD_DIM)
        scale = HEAD_DIM ** (-0.5)
        scores = jnp.einsum('bqhd,bkhd->bhqk', q, k) * scale
        probs = jax.nn.softmax(scores, axis=-1)
        attn = jnp.einsum('bhqk,bkhd->bqhd', probs, v).reshape(B, T, D_MODEL)
        attn = attn @ Wo + bo
        x = _layer_norm(src + attn, ln1_g, ln1_b)
        keys = (x @ router_w + router_b)[..., 0]
        expert_idx = jnp.remainder(jnp.floor(keys).astype(jnp.int32), N_EXPERTS)
        ff_out = jnp.zeros_like(x)
        for e in range(N_EXPERTS):
            h = jax.nn.relu(x @ W1[e] + b1[e])
            y = h @ W2[e] + b2[e]
            ff_out = ff_out + jnp.where((expert_idx == e)[..., None], y, 0.0)
        return _layer_norm(x + ff_out, ln2_g, ln2_b)
    x = L0_attn_input_tensor
    xn = _layernorm(x, axis=-1)
    x = x + _L0_attn_ref(xn, L0_attn_ln_gamma, L0_attn_ln_beta, L0_attn_W_in, L0_attn_b_in, L0_attn_A_log, L0_attn_D_skip, L0_attn_dt_bias, L0_attn_W_out, L0_attn_b_out) + _L0_ffn_ref(xn, L0_ffn_Wq, L0_ffn_bq, L0_ffn_Wk, L0_ffn_bk, L0_ffn_Wv, L0_ffn_bv, L0_ffn_Wo, L0_ffn_bo, L0_ffn_router_w, L0_ffn_router_b, L0_ffn_W1, L0_ffn_b1, L0_ffn_W2, L0_ffn_b2, L0_ffn_ln1_g, L0_ffn_ln1_b, L0_ffn_ln2_g, L0_ffn_ln2_b)
    return x

_drawn_inputs = setup_inputs


def setup_inputs(seed=0):
    import zlib

    import numpy as np

    out = dict(_drawn_inputs(seed))
    spreads = {'L0_attn_ln_gamma': (1.0, 0.2),
     'L0_attn_ln_beta': (0.0, 0.1),
     'L0_attn_b_in': (0.0, 0.1),
     'L0_attn_D_skip': (1.0, 0.2),
     'L0_attn_b_out': (0.0, 0.1),
     'L0_ffn_bq': (0.0, 0.1),
     'L0_ffn_bk': (0.0, 0.1),
     'L0_ffn_bv': (0.0, 0.1),
     'L0_ffn_bo': (0.0, 0.1),
     'L0_ffn_b1': (0.0, 0.1),
     'L0_ffn_b2': (0.0, 0.1),
     'L0_ffn_ln1_g': (1.0, 0.2),
     'L0_ffn_ln1_b': (0.0, 0.1),
     'L0_ffn_ln2_g': (1.0, 0.2),
     'L0_ffn_ln2_b': (0.0, 0.1)}
    factors = {}
    for name, (base, spread) in spreads.items():
        noise = np.random.default_rng([zlib.crc32(name.encode()), seed]).standard_normal(out[name].shape)
        drawn = base * np.exp(spread * noise) if base else spread * noise
        out[name] = jnp.asarray(drawn.astype(out[name].dtype))
    for name, factor in factors.items():
        out[name] = (out[name] * factor).astype(out[name].dtype)
    return out
```

```python
import concourse.bass as bass
from concourse import mybir
from contextlib import ExitStack

FP32 = mybir.dt.float32
BF16 = mybir.dt.bfloat16
I32 = mybir.dt.int32
U32 = mybir.dt.uint32
ALU = mybir.AluOpType
ACT = mybir.ActivationFunctionType
AX = mybir.AxisListType

P = 128
B, T, D = 8, 512, 256
NT = T // P
TILES = B * NT
KD = D // P
H, HD = 16, 16
UH = P // HD
PARTS = 3
PAIRS_Q = (0, 0, 1, 1, 0, 2)
PAIRS_K = (0, 1, 0, 1, 2, 0)
KS = len(PAIRS_Q) * HD
KM = KS + PARTS
SCALE = HD ** -0.5
INNER, STATE, HEADS, PW = 512, 64, 8, 64
PROJ = 2 * INNER + 2 * STATE + HEADS
JI = INNER // P
E, FF = 4, 1024
ETILES = TILES + E - 1
EPS = 1e-5


def wait(eng, sem, value):
    if not isinstance(value, int) or value > 0:
        eng.wait_ge(sem, value)


def settle(core, eng):
    cell = core.pad[:, core.pads:core.pads + 1]
    core.pads += 1
    if eng is core.nc.vector:
        eng.memset(cell, 0.0)
    else:
        eng.tensor_tensor(cell, core.ones[0:1, 0:1], core.ones[0:1, 0:1], ALU.mult)


class Steps:

    def __init__(self, eng, sem, base):
        self.eng, self.sem, self.at = eng, sem, base

    def then(self, ins, core=None):
        ins.then_inc(self.sem, 1)
        self.at = self.at + 1
        self.eng.wait_ge(self.sem, self.at)
        if core:
            settle(core, core.nc.vector)


class Core:

    def __init__(self, nc, ctx, ins, out):
        self.nc, self.ctx, self.i, self.out = nc, ctx, ins, out
        self.psum = ctx.enter_context(nc.psum_tensor("psum", [P, 8, 512], FP32))
        self.bank = [self.psum[:, n] for n in range(8)]

        def dram(name, shape, dt=FP32):
            return nc.dram_tensor(name, shape, dt).ap()

        self.xn_dram = dram("xn_scratch", [B * T, D])
        self.nxT_dram = dram("nxT_scratch", [KD, P, B * T])
        self.parts_dram = dram("qk_parts", [2, B, 2, PARTS, P, T], BF16)
        self.rows_dram = dram("max_rows", [2, PARTS, UH * NT, P], BF16)
        self.v_dram = dram("v_scratch", [B * T, H * 2 * HD])
        self.x1_dram = dram("x1_scratch", [B * T, D])
        self.xg_dram = dram("x1_grouped", [ETILES * P, D])
        self.yg_dram = dram("y_grouped", [ETILES * P, D])
        self.r_dram = dram("other_branch", [B * T, D])
        self.pad, self.pads = self.sb("pad", [1, 128]), 0
        self.ident = self.sb("ident", [P, P])
        self.upper = self.sb("upper", [P, P])
        self.strict = self.sb("strict", [P, P])
        self.ones = self.sb("ones", [P, P])
        self.neg_half = self.sb("neg_half", [P, 8])
        self.dt_all = self.sb("dt_all", [P, TILES, HEADS])
        self.keys = self.sb("keys", [P, TILES])
        self.pos_i = self.sb("pos_i", [P, TILES], U32)
        self.which_i = self.sb("which_i", [P, ETILES], I32)

    def sb(self, name, shape, dt=FP32, ctx=None):
        return (ctx or self.ctx).enter_context(self.nc.sbuf_tensor(name, shape, dt))

    def sem(self, name, ctx=None):
        return (ctx or self.ctx).enter_context(self.nc.semaphore(name))


def row(vector):
    return vector.unsqueeze(0).to_broadcast([P, vector.shape[0]])


def constants(core):
    nc, c = core.nc, core
    with ExitStack() as ctx:
        filled = core.sem("filled", ctx)
        selected = core.sem("selected", ctx)
        zeroed = core.sem("zeroed", ctx)
        zeros = core.sb("zeros", [P, ETILES // 5, D], ctx=ctx)
        block = ctx.enter_context(nc.Block())

        @block.vector
        def _(dve):
            nc.vector.memset(zeros[:], 0.0).then_inc(zeroed, 1)

        @block.sync
        def _(sp):
            sp.wait_ge(zeroed, 1)
            for n in range(5):
                sp.dma_start(c.xg_dram.rearrange("(n t p) d -> n p t d", n=5, p=P)[n], zeros[:]).then_inc(zeroed, 16)
            sp.wait_ge(zeroed, 1 + 5 * 16)

        @block.gpsimd
        def _(pool):
            nc.gpsimd.memset(c.ident[:], 0.0)
            nc.gpsimd.memset(c.upper[:], 1.0)
            nc.gpsimd.memset(c.strict[:], 1.0)
            nc.gpsimd.memset(c.ones[:], 1.0)
            nc.gpsimd.memset(c.neg_half[:], -0.5).then_inc(filled, 1)
            pool.wait_ge(filled, 1)
            nc.gpsimd.affine_select(out=c.ident[:], in_=c.ident[:], compare_op=ALU.not_equal, fill=1.0,
                                    base=0, pattern=[[-1, P]], channel_multiplier=1).then_inc(selected, 1)
            nc.gpsimd.affine_select(out=c.upper[:], in_=c.upper[:], compare_op=ALU.is_ge, fill=0.0,
                                    base=0, pattern=[[1, P]], channel_multiplier=-1).then_inc(selected, 1)
            nc.gpsimd.affine_select(out=c.strict[:], in_=c.strict[:], compare_op=ALU.is_ge, fill=0.0,
                                    base=-1, pattern=[[-1, P]], channel_multiplier=1).then_inc(selected, 1)
            pool.wait_ge(selected, 3)


def project(core):
    nc, c, d = core.nc, core, core.i
    with ExitStack() as ctx:
        sb = lambda name, shape, dt=FP32: core.sb(name, shape, dt, ctx)
        sem = lambda name: core.sem(name, ctx)
        x = sb("x", [P, 2, NT, D])
        xn = sb("xn", [P, 2, NT, D])
        nx = sb("nx", [P, 2, NT, D])
        xnT = sb("xnT", [P, KD, T])
        nxT = sb("nxT", [P, 2, KD, T])
        wq, wk, wv = (sb(n, [P, KD, D]) for n in ("wq", "wk", "wv"))
        wdt = sb("wdt", [P, KD, HEADS])
        bq, bk, g_ln = (sb(n, [P, KD]) for n in ("bq", "bk", "g_ln"))
        bv = sb("bv", [P, D])
        full = sb("qk_full", [P, 4, T])
        rest = sb("qk_rest", [P, 4, T])
        parts = sb("qk_parts_sb", [P, 4, PARTS, T], BF16)
        v = sb("v_padded", [P, NT, H, 2 * HD])
        stats = sb("stats", [P, 2, NT, 6])
        mv = sb("mv", [P, 2, NT, 2])
        ve = sb("ve", [P, 2, NT])
        rstd = sb("rstd", [P, 2, NT])

        w_in = sem("w_in")
        x_in = [sem("x_in0"), sem("x_in1")]
        ln_var = sem("ln_var")
        ln_rstd = sem("ln_rstd")
        xn_ready = sem("xn_ready")
        nx_ready = sem("nx_ready")
        xn_out = [sem("xn_out0"), sem("xn_out1")]
        t_ready = sem("t_ready")
        t_taken = sem("t_taken")
        tn_taken = sem("tn_taken")
        nxT_out = [sem("nxT_out0"), sem("nxT_out1")]
        qk_ready = sem("qk_ready")
        full_ready = sem("full_ready")
        rest_ready = sem("rest_ready")
        mid_ready = sem("mid_ready")
        low_ready = sem("low_ready")
        parts_out = [sem(f"parts_out{j}") for j in range(4)]
        v_ready = sem("v_ready")
        v_taken = sem("v_taken")
        v_out = sem("v_out")
        dt_ready = sem("dt_ready")
        dt_taken = sem("dt_taken")
        dve_step = sem("dve_step")
        block = ctx.enter_context(nc.Block())
        x_tiles = d["L0_attn_input_tensor"].rearrange("b (t p) d -> b p t d", p=P)
        xn_tiles = c.xn_dram.rearrange("(b t p) d -> b p t d", t=NT, p=P)
        v_tiles = c.v_dram.rearrange("(b t p) e -> b p t e", t=NT, p=P)
        dv = d["L0_attn_W_in"]
        WEIGHTS = 9 * 16

        @block.sync
        def _(sp):
            sp.dma_start(x[:, 0], x_tiles[0]).then_inc(x_in[0], 16)
            for dst, src in ((wq, "Wq"), (wk, "Wk"), (wv, "Wv")):
                sp.dma_start(dst[:], d["L0_ffn_" + src].rearrange("(k p) n -> p k n", p=P)).then_inc(w_in, 16)
            with nc.allow_non_contiguous_dma(reason="small vectors"):
                sp.dma_start(wdt[:], dv[:, PROJ - HEADS:PROJ].rearrange("(k p) n -> p k n", p=P)).then_inc(w_in, 16)
                sp.dma_start(bq[:], d["L0_ffn_bq"].rearrange("(k p) -> p k", p=P)).then_inc(w_in, 16)
                sp.dma_start(bk[:], d["L0_ffn_bk"].rearrange("(k p) -> p k", p=P)).then_inc(w_in, 16)
                sp.dma_start(g_ln[:], d["L0_attn_ln_gamma"].rearrange("(k p) -> p k", p=P)).then_inc(w_in, 16)
            sp.dma_start(bv[:], row(d["L0_ffn_bv"])).then_inc(w_in, 16)
            sp.dma_start(x[:, 1], x_tiles[1]).then_inc(x_in[1], 16)

            def batch(b, i, p):
                sp.wait_ge(xn_ready, b + 1)
                sp.dma_start(xn_tiles[b], xn[:, p]).then_inc(xn_out[p], 16)
                sp.wait_ge(tn_taken, 2 * b + 2)
                sp.dma_start(c.nxT_dram[:, :, bass.ts(b, T)].rearrange("k p t -> p k t"),
                             nxT[:, p]).then_inc(nxT_out[p], 16)
                for j in range(4):
                    sp.wait_ge(low_ready, 4 * b + j + 1)
                    sp.dma_start(c.parts_dram[j % 2, b, j // 2].rearrange("a p t -> p a t"),
                                 parts[:, j]).then_inc(parts_out[j], 16)
                sp.wait_ge(v_taken, 2 * b + 2)
                sp.dma_start(v_tiles[b], v[:].rearrange("p t h e -> p t (h e)")).then_inc(v_out, 16)

            def prefetch(b, p):
                sp.wait_ge(xn_ready, b - 1)
                sp.dma_start(x[:, p], x_tiles[b]).then_inc(x_in[p], 16)

            batch(0, 0, 0)
            prefetch(2, 0)
            with sp.Fori(0, B // 2 - 2) as i:
                batch(2 * i + 1, i, 1)
                prefetch(2 * i + 3, 1)
                batch(2 * i + 2, i + 1, 0)
                prefetch(2 * i + 4, 0)
            batch(B - 3, B // 2 - 2, 1)
            prefetch(B - 1, 1)
            for p in range(2):
                batch(B - 2 + p, B // 2 - 1, p)
            for p in range(2):
                sp.wait_ge(xn_out[p], 16 * B // 2)
                sp.wait_ge(nxT_out[p], 16 * B // 2)
            for j in range(4):
                sp.wait_ge(parts_out[j], 16 * B)
            sp.wait_ge(v_out, 16 * B)

        @block.vector
        def _(dve):
            nc.vector.memset(v[:, :, :, HD:2 * HD], 1.0)
            dve.wait_ge(w_in, WEIGHTS - 16)
            STEPS = 6
            for k in range(KD):
                ins = nc.vector.tensor_scalar(wdt[:, k], wdt[:, k], g_ln[:, k:k + 1], None, ALU.mult)
            ins.then_inc(w_in, 16)

            def batch(b, i, p):
                step = Steps(dve, dve_step, STEPS * b)
                dve.wait_ge(x_in[p], 16 * (i + 1))
                for half, (src, dst) in enumerate(((x, xn), (xn, nx))):
                    for t in range(NT):
                        ins = nc.vector.bn_stats(stats[:, half, t], src[:, p, t])
                    step.then(ins, core)
                    for t in range(NT):
                        ins = nc.vector.bn_aggr(mv[:, half, t], stats[:, half, t])
                    step.then(ins)
                    nc.vector.tensor_scalar(ve[:, half], mv[:, half, :, 1], EPS, None, ALU.add).then_inc(ln_var, 1)
                    dve.wait_ge(ln_rstd, 2 * b + half + 1)
                    if half == 0:
                        wait(dve, xn_out[p], 16 * i)
                    else:
                        wait(dve, t_ready, 4 * b - 4)
                    for t in range(NT):
                        ins = nc.vector.tensor_scalar(dst[:, p, t], src[:, p, t], mv[:, half, t, 0:1],
                                                      rstd[:, half, t:t + 1], ALU.subtract, ALU.mult)
                    step.then(ins)
                    nc.vector.tensor_copy(ve[:, half, 0:1], ve[:, half, 0:1]).then_inc(xn_ready if half == 0 else nx_ready, 1)

            def rests(b):
                for j in range(4):
                    dve.wait_ge(full_ready, 4 * b + j + 1)
                    wait(dve, parts_out[j], 16 * b)
                    nc.vector.tensor_copy(parts[:, j, 0], full[:, j]).then_inc(rest_ready, 1)
                    dve.wait_ge(rest_ready, 8 * b + 2 * j + 1)
                    nc.vector.tensor_tensor(rest[:, j], full[:, j], parts[:, j, 0], ALU.subtract).then_inc(rest_ready, 1)
                    dve.wait_ge(rest_ready, 8 * b + 2 * j + 2)
                    nc.vector.tensor_copy(parts[:, j, 1], rest[:, j]).then_inc(mid_ready, 1)
                for half in range(2):
                    dve.wait_ge(v_ready, 2 * b + half + 1)
                    if half == 0:
                        wait(dve, v_out, 16 * b)
                    nc.vector.tensor_tensor(
                        v[:, 2 * half:2 * half + 2, :, 0:HD],
                        c.bank[6 + half][:].rearrange("p (t h e) -> p t h e", t=2, h=H),
                        bv[:].rearrange("p (h e) -> p h e", h=H).unsqueeze(1).to_broadcast([P, 2, H, HD]),
                        ALU.add).then_inc(v_taken, 1)

            batch(0, 0, 0)
            with dve.Fori(0, B // 2 - 1) as i:
                batch(2 * i + 1, i, 1)
                rests(2 * i)
                batch(2 * i + 2, i + 1, 0)
                rests(2 * i + 1)
            batch(B - 1, B // 2 - 1, 1)
            rests(B - 2)
            rests(B - 1)

        @block.gpsimd
        def _(pool):
            def powers(b):
                for half in range(2):
                    pool.wait_ge(ln_var, 2 * b + half + 1)
                    nc.gpsimd.tensor_tensor(rstd[:, half], ve[:, half], c.neg_half[:, 0:NT], ALU.pow).then_inc(ln_rstd, 1)

            def lows(b):
                for j in range(4):
                    pool.wait_ge(mid_ready, 4 * b + j + 1)
                    nc.gpsimd.tensor_tensor(parts[:, j, 2], rest[:, j], parts[:, j, 1], ALU.subtract).then_inc(low_ready, 1)

            powers(0)
            with pool.Fori(0, B - 1) as b:
                powers(b + 1)
                lows(b)
            lows(B - 1)

        @block.tensor
        def _(pe):
            pe.wait_ge(w_in, WEIGHTS)

            def batch(b, p):
                for n, src in enumerate((xn, nx)):
                    pe.wait_ge((xn_ready, nx_ready)[n], b + 1)
                    for k in range(KD):
                        if n == 0:
                            wait(pe, dt_taken, b)
                        else:
                            pe.wait_ge(t_taken, 2 * b + 1 + k)
                        for t in range(NT):
                            ins = nc.tensor.transpose(c.bank[k][:, bass.ts(t, P)], src[:, p, t, bass.ts(k, P)], c.ident[:])
                        ins.then_inc(t_ready, 1)
                pe.wait_ge(t_taken, 2 * b + 2)
                for j in range(4):
                    w = (wq, wk)[j % 2]
                    wait(pe, full_ready, 4 * b - 3 + j)
                    for k in range(KD):
                        ins = nc.tensor.matmul(c.bank[2 + j][:], w[:, k, bass.ts(j // 2, P)], xnT[:, k],
                                               start=k == 0, stop=k == KD - 1)
                    ins.then_inc(qk_ready, 1)
                for half in range(2):
                    wait(pe, v_taken, 2 * b - 1 + half)
                    for t in (2 * half, 2 * half + 1):
                        for k in range(KD):
                            ins = nc.tensor.matmul(c.bank[6 + half][:, bass.ts(t % 2, D)], xnT[:, k, bass.ts(t, P)],
                                                   wv[:, k], start=k == 0, stop=k == KD - 1)
                    ins.then_inc(v_ready, 1)
                pe.wait_ge(tn_taken, 2 * b + 2)
                for t in range(NT):
                    for k in range(KD):
                        ins = nc.tensor.matmul(c.bank[0][:, bass.ts(t, HEADS)], nxT[:, p, k, bass.ts(t, P)],
                                               wdt[:, k], start=k == 0, stop=k == KD - 1)
                ins.then_inc(dt_ready, 1)

            batch(0, 0)
            with pe.Fori(0, B // 2 - 1) as i:
                batch(2 * i + 1, 1)
                batch(2 * i + 2, 0)
            batch(B - 1, 1)

        @block.scalar
        def _(act):
            act.wait_ge(w_in, WEIGHTS)

            def batch(b, i, p):
                for n in range(2):
                    for k in range(KD):
                        act.wait_ge(t_ready, 4 * b + 2 * n + k + 1)
                        if n == 0:
                            if k == 0:
                                wait(act, v_ready, 2 * b)
                            nc.scalar.copy(xnT[:, k], c.bank[k][:]).then_inc(t_taken, 1)
                        else:
                            if k == 0:
                                wait(act, nxT_out[p], 16 * i)
                                wait(act, dt_ready, b - 1)
                            nc.scalar.copy(nxT[:, p, k], c.bank[k][:]).then_inc(tn_taken, 1)
                for j in range(4):
                    act.wait_ge(qk_ready, 4 * b + j + 1)
                    wait(act, rest_ready, 8 * b - 6 + 2 * j)
                    nc.scalar.activation(full[:, j], c.bank[2 + j][:], ACT.Identity,
                                         bias=(bq, bk)[j % 2][:, j // 2:j // 2 + 1]).then_inc(full_ready, 1)
                act.wait_ge(dt_ready, b + 1)
                nc.scalar.copy(c.dt_all[:, bass.ts(b, NT)], c.bank[0][:, 0:NT * HEADS].rearrange("p (t h) -> p t h", t=NT)).then_inc(dt_taken, 1)

            batch(0, 0, 0)
            with act.Fori(0, B // 2 - 1) as i:
                batch(2 * i + 1, i, 1)
                batch(2 * i + 2, i + 1, 0)
            batch(B - 1, B // 2 - 1, 1)


JOBS = {1: ["OT3-"], 3: ["aT0-"], 4: ["aT1-", "neg1"], 5: ["OT0"], 7: ["Wo0-"], 8: ["Wo1-"], 9: ["OT1"],
        12: ["neg0+"], 13: ["OT2"]}
STEPS_B = 16


class Jobs:

    def __init__(self, b, first=False, last=False, tail=False):
        kept = [(s, j) for s, js in JOBS.items() for j in js
                if not (first and j[-1] == "-") and not (last and j[-1] == "+") and not (tail and j[-1] != "-")]
        start = 1 if first else 10 * b - 4
        if tail:
            start = 10 * B - 5
        self.of = {s: [(j, start + n) for n, (s2, j) in enumerate(kept) if s2 == s] for s in range(STEPS_B)}


def attend(core):
    nc, c, d = core.nc, core, core.i
    with ExitStack() as ctx:
        sb = lambda name, shape, dt=FP32: core.sb(name, shape, dt, ctx)
        sem = lambda name: core.sem(name, ctx)
        qs = sb("q_stack", [P, 4, UH, T], BF16)
        ks = sb("k_stack", [P, 4, UH, T], BF16)
        v = sb("v_tiles", [P, 2, NT, H * 2 * HD])
        probs = sb("probs", [P, 2, 4, T])
        nmax = sb("nmax", [P, 2, UH * NT])
        nrow = sb("nrow", [UH * NT, P])
        nrest = sb("nrest", [UH * NT, P])
        nparts = sb("nparts", [UH * NT, PARTS, P], BF16)
        oT = sb("oT", [P, 2, T])
        rsum = sb("rsum", [P, NT, 4])
        attn = sb("attn", [P, NT, D])
        aT = sb("aT", [P, KD, T])
        wo = sb("wo", [P, KD, D])
        bo, g1, b1, rw = (sb(n, [P, D]) for n in ("bo", "g1", "b1", "rw"))
        rb = sb("rb", [P, 1])
        xnb = sb("xnb", [P, 2, NT, D])
        res = sb("res", [P, NT, D])
        norm = sb("norm", [P, NT, D])
        x1 = sb("x1", [P, NT, D])
        stats = sb("stats1", [P, NT, 6])
        mv = sb("mv1", [P, NT, 2])
        ve = sb("ve1", [P, NT])
        rstd = sb("rstd1", [P, NT])
        kt = sb("kt", [P, NT])
        junk = sb("junk", [1, 2])
        product = sb("product", [P, NT, D])

        w_in = sem("w_in1")
        set_up = sem("set_up")
        stack_in = [sem(f"stack_in{n}") for n in range(4)]
        v_in = [sem(f"v_in{n}") for n in range(2)]
        xn_in = [sem(f"xn_in{n}") for n in range(2)]
        rows_in = [sem(f"rows_in{n}") for n in range(2)]
        s1_ready = sem("s1_ready")
        max_done = sem("max_done")
        s2_ready = sem("s2_ready")
        exp_done = sem("exp_done")
        pv_done = sem("pv_done")
        oT_ready = sem("oT_ready")
        job_ready = sem("job_ready")
        job_taken = sem("job_taken")
        group_done = sem("group_done")
        aT_ready = sem("aT_ready")
        nrow_ready = sem("nrow_ready")
        pool_step = sem("pool_step1")
        rows_made = sem("rows_made")
        rows_out = sem("rows_out")
        xnb_ready = sem("xnb_ready")
        res_done = sem("res_done")
        ve_ready = sem("ve_ready")
        rstd_ready = sem("rstd_ready")
        norm_ready = sem("norm_ready")
        x1_ready = sem("x1_ready")
        x1_out = sem("x1_out")
        keys_done = sem("keys_done")
        recip_done = sem("recip_done")
        dve_step = sem("dve_step1")
        block = ctx.enter_context(nc.Block())
        xn_tiles = c.xn_dram.rearrange("(b t p) d -> b p t d", t=NT, p=P)
        x1_tiles = c.x1_dram.rearrange("(b t p) d -> b p t d", t=NT, p=P)
        v_tiles = c.v_dram.rearrange("(b t p) e -> b p t e", t=NT, p=P)
        LOADS = 2 * len(PAIRS_Q) * 16
        last_ord = 10 * B

        @block.sync
        def _(sp):
            def stack(b, hf, p):
                for dst, pairs, n in ((qs, PAIRS_Q, 0), (ks, PAIRS_K, 1)):
                    for r, part in enumerate(pairs):
                        sp.dma_start(dst[HD * r:HD * r + HD, 2 * p + hf],
                                     c.parts_dram[n, b, hf, part].rearrange("(h e) t -> e h t", e=HD)
                                     ).then_inc(stack_in[2 * p + hf], 16)

            def rest(b, p):
                sp.dma_start(v[:, p], v_tiles[b]).then_inc(v_in[p], 16)
                sp.dma_start(xnb[:, p], xn_tiles[b]).then_inc(xn_in[p], 16)

            stack(0, 0, 0)
            sp.dma_start(wo[:], d["L0_ffn_Wo"].rearrange("(k p) n -> p k n", p=P)).then_inc(w_in, 16)
            for dst, name in ((bo, "bo"), (g1, "ln1_g"), (b1, "ln1_b")):
                sp.dma_start(dst[:], row(d["L0_ffn_" + name])).then_inc(w_in, 16)
            sp.dma_start(rw[:], row(d["L0_ffn_router_w"].rearrange("d o -> (d o)"))).then_inc(w_in, 16)
            with nc.allow_non_contiguous_dma(reason="one number"):
                sp.dma_start(rb[:], row(d["L0_ffn_router_b"])).then_inc(w_in, 16)
            stack(0, 1, 0)
            rest(0, 0)

            def body(b, p):
                wait(sp, s2_ready, 32 * b - 16)
                stack(b + 1, 0, 1 - p)
                wait(sp, s2_ready, 32 * b)
                stack(b + 1, 1, 1 - p)
                wait(sp, res_done, 2 * b)
                rest(b + 1, 1 - p)

            body(0, 0)
            with sp.Fori(0, (B - 2) // 2) as i:
                body(2 * i + 1, 1)
                body(2 * i + 2, 0)

        @block.tensor
        def _(pe):
            pe.wait_ge(w_in, 6 * 16)

            def s1(b, hf, p, q, head):
                n = (2 * b + hf) * UH * NT + head * NT
                if head == 0:
                    pe.wait_ge(stack_in[2 * p + hf], LOADS * (q + 1))
                for t in range(NT):
                    wait(pe, max_done, n + t - 1)
                    nc.tensor.matmul(c.bank[t % 2], qs[0:KS, 2 * p + hf, head, bass.ts(t, P)],
                                     ks[0:KS, 2 * p + hf, head], start=True, stop=True).then_inc(s1_ready, 1)

            def s2(b, p, s):
                hf, g, k = s // 8, s // 4 % 2, s % 4
                if s % 8 == 0:
                    pe.wait_ge(rows_in[hf], 16 * (b + 1))
                    pe.wait_ge(set_up, 2)
                for pair in range(2):
                    wait(pe, exp_done, 2 * (16 * b + s) + pair - 1)
                    for j in (2 * pair, 2 * pair + 1):
                        ins = nc.tensor.matmul(c.bank[2 + j], ks[0:KM, 2 * p + hf, 4 * g + j, bass.ts(k, P)],
                                               qs[0:KM, 2 * p + hf, 4 * g + j], start=True, stop=True)
                    ins.then_inc(s2_ready, 1)

            def pv(b, p, q, s):
                k = s % 4
                pe.wait_ge(exp_done, 2 * (16 * b + s) + 2)
                if s == 0:
                    pe.wait_ge(v_in[p], 16 * (q + 1))
                if k == 0:
                    wait(pe, oT_ready, 4 * b + s // 4)
                for j in range(4):
                    ins = nc.tensor.matmul(c.bank[6][32 * j:32 * j + 32], v[:, p, k, bass.ts(s // 4 * 4 + j, 32)],
                                           probs[:, s % 2, j], start=k == 0, stop=k == 3)
                ins.then_inc(pv_done, 1)

            def job(name, n, b):
                wait(pe, job_taken, n)
                if name[:2] == "OT":
                    g = 4 * b + int(name[2]) - (4 if name[-1] == "-" else 0)
                    pe.wait_ge(oT_ready, g + 1)
                    for t in range(NT):
                        ins = nc.tensor.transpose(c.bank[7][:, bass.ts(t, P)], oT[:, int(name[2]) % 2, bass.ts(t, P)], c.ident[:])
                elif name[:2] == "aT":
                    k = int(name[2])
                    pe.wait_ge(group_done, 4 * b)
                    for t in range(NT):
                        ins = nc.tensor.transpose(c.bank[7][:, bass.ts(t, P)], attn[:, t, bass.ts(k, P)], c.ident[:])
                elif name[:2] == "Wo":
                    half = int(name[2])
                    pe.wait_ge(aT_ready, 2 * b)
                    for t in (2 * half, 2 * half + 1):
                        for k in range(KD):
                            ins = nc.tensor.matmul(c.bank[7][:, bass.ts(t % 2, D)], aT[:, k, bass.ts(t, P)], wo[:, k],
                                                   start=k == 0, stop=k == KD - 1)
                else:
                    hf = int(name[3])
                    u = 2 * b + 1 if hf else 2 * b + 2
                    pe.wait_ge(max_done, UH * NT * (u + 1))
                    ins = nc.tensor.transpose(c.bank[7][0:UH * NT, 0:P], nmax[:, hf], c.ident[:])
                ins.then_inc(job_ready, 1)

            for head in range(UH):
                s1(0, 0, 0, 0, head)
            job("neg0+", 0, -1)
            for head in range(4):
                s1(0, 1, 0, 0, head)

            def body(b, p, q, first=False, last=False):
                jobs = Jobs(b, first, last)
                for s in range(STEPS_B):
                    s2(b, p, s)
                    if s < 4:
                        s1(b, 1, p, q, 4 + s)
                    elif not last:
                        w = s - 4
                        s1(b + 1, w // UH, 1 - p, q + p, w % UH)
                    if s == 0 and not first:
                        pv(b - 1, 1 - p, q - (1 - p), STEPS_B - 1)
                    elif s > 0:
                        pv(b, p, q, s - 1)
                    for name, n in jobs.of[s]:
                        job(name, n, b)

            body(0, 0, 0, first=True)
            with pe.Fori(0, (B - 2) // 2) as i:
                body(2 * i + 1, 1, i)
                body(2 * i + 2, 0, i + 1)
            body(B - 1, 1, B // 2 - 1, last=True)
            pv(B - 1, 1, B // 2 - 1, STEPS_B - 1)
            jobs = Jobs(B, tail=True)
            for s in range(STEPS_B):
                for name, n in jobs.of[s]:
                    job(name, n, B)

        @block.scalar
        def _(act):
            def job(name, n, b):
                if name[:2] in ("OT", "Wo"):
                    return
                act.wait_ge(job_ready, n + 1)
                if name[:2] == "aT":
                    nc.scalar.copy(aT[:, int(name[2])], c.bank[7][:]).then_inc(job_taken, 1)
                    act.wait_ge(job_taken, n + 1)
                    nc.scalar.copy(junk[0:1, 0:1], junk[0:1, 0:1]).then_inc(aT_ready, 1)
                else:
                    u = 2 * b + 1 if name[3] == "1" else 2 * b + 2
                    wait(act, rows_made, u)
                    nc.scalar.copy(nrow[:], c.bank[7][0:UH * NT, 0:P]).then_inc(job_taken, 1)

            def out_copy(g, half):
                act.wait_ge(pv_done, 4 * (g + 1))
                wait(act, group_done, g - 1)
                nc.scalar.copy(oT[:, half], c.bank[6][:]).then_inc(oT_ready, 1)

            act.wait_ge(set_up, 2)
            job("neg0+", 0, -1)

            def body(b, first=False, last=False):
                jobs = Jobs(b, first, last)
                for s in range(STEPS_B):
                    wait(act, pv_done, 16 * b + s - 1)
                    for pair in range(2):
                        act.wait_ge(s2_ready, 2 * (16 * b + s) + pair + 1)
                        nc.scalar.activation(probs[:, s % 2, 2 * pair:2 * pair + 2], c.psum[:, 2 + 2 * pair:4 + 2 * pair],
                                             ACT.Exp, scale=SCALE).then_inc(exp_done, 1)
                    if s % 4 == 0 and not (first and s == 0):
                        out_copy(4 * b + s // 4 - 1, (s // 4 - 1) % 2)
                    for name, n in jobs.of[s]:
                        job(name, n, b)

            body(0, first=True)
            with act.Fori(0, (B - 2) // 2) as i:
                body(2 * i + 1)
                body(2 * i + 2)
            body(B - 1, last=True)
            out_copy(4 * B - 1, 1)
            jobs = Jobs(B, tail=True)
            for s in range(STEPS_B):
                for name, n in jobs.of[s]:
                    job(name, n, B)

        @block.vector
        def _(dve):
            nc.vector.memset(junk[:], 0.0).then_inc(set_up, 1)
            dve.wait_ge(w_in, 6 * 16)

            def maxima(b, hf, head):
                n = (2 * b + hf) * UH * NT + head * NT
                for t in range(NT):
                    dve.wait_ge(s1_ready, n + t + 1)
                    nc.vector.tensor_reduce(nmax[:, hf, head * NT + t:head * NT + t + 1], c.bank[t % 2], axis=AX.X,
                                            op=ALU.max, negate=True).then_inc(max_done, 1)

            def group(name, n, b):
                g = int(name[2])
                dve.wait_ge(job_ready, n + 1)
                o = c.bank[7].rearrange("p (t j e) -> p t j e", t=NT, j=4)
                nc.vector.reciprocal(rsum[:], o[:, :, :, HD]).then_inc(recip_done, 1)
                dve.wait_ge(recip_done, 4 * b + g + 1 - (4 if name[-1] == "-" else 0))
                nc.vector.tensor_tensor(
                    attn[:, :, bass.ts(g, 4 * HD)].rearrange("p t (j e) -> p t j e", j=4),
                    o[:, :, :, 0:HD], rsum[:].unsqueeze(3).to_broadcast([P, NT, 4, HD]), ALU.mult).then_inc(job_taken, 1)
                dve.wait_ge(job_taken, n + 1)
                nc.vector.tensor_copy(junk[0:1, 0:1], junk[0:1, 0:1]).then_inc(group_done, 1)

            def job(name, n, b, p):
                if name[:2] == "OT":
                    group(name, n, b)
                elif name[:2] == "Wo":
                    half = int(name[2])
                    dve.wait_ge(job_ready, n + 1)
                    dve.wait_ge(xnb_ready, b)
                    nc.vector.tensor_tensor(res[:, 2 * half:2 * half + 2], c.bank[7].rearrange("p (t e) -> p t e", t=2),
                                            xnb[:, 1 - p, 2 * half:2 * half + 2], ALU.add).then_inc(job_taken, 1)
                    dve.wait_ge(job_taken, n + 1)
                    nc.vector.tensor_copy(junk[0:1, 0:1], junk[0:1, 0:1]).then_inc(res_done, 1)

            def finish(b, s):
                step = Steps(dve, dve_step, 3 * b)
                if s == 9:
                    dve.wait_ge(res_done, 2 * b + 2)
                    for t in range(NT):
                        ins = nc.vector.bn_stats(stats[:, t], res[:, t])
                    step.then(ins, core)
                    for t in range(NT):
                        ins = nc.vector.bn_aggr(mv[:, t], stats[:, t])
                    step.then(ins)
                    nc.vector.tensor_scalar(ve[:], mv[:, :, 1], EPS, None, ALU.add).then_inc(ve_ready, 1)
                if s == 10:
                    dve.wait_ge(rstd_ready, b + 1)
                    wait(dve, x1_ready, 2 * b)
                    for t in range(NT):
                        ins = nc.vector.tensor_scalar(norm[:, t], res[:, t], mv[:, t, 0:1], rstd[:, t:t + 1],
                                                      ALU.subtract, ALU.mult)
                    ins.then_inc(norm_ready, 1)
                if s == 14:
                    dve.wait_ge(x1_ready, 2 * b + 2)
                    for t in range(NT):
                        ins = nc.vector.tensor_tensor_reduce(out=product[:, t], in0=x1[:, t], in1=rw[:], scale=1.0, scalar=0.0,
                                                             op0=ALU.mult, op1=ALU.add, accum_out=kt[:, t:t + 1])
                    step.at = 3 * b + 2
                    step.then(ins)
                    nc.vector.tensor_scalar(c.keys[:, bass.ts(b, NT)], kt[:], rb[:], None, ALU.add).then_inc(keys_done, 1)

            for head in range(UH):
                maxima(0, 0, head)
            for head in range(4):
                maxima(0, 1, head)

            def body(b, p, first=False, last=False):
                jobs = Jobs(b, first, last)
                for s in range(STEPS_B):
                    if s < 4:
                        maxima(b, 1, 4 + s)
                    elif not last:
                        maxima(b + 1, (s - 4) // UH, (s - 4) % UH)
                    for name, n in jobs.of[s]:
                        job(name, n, b, p)
                    if not first:
                        finish(b - 1, s)

            body(0, 0, first=True)
            with dve.Fori(0, (B - 2) // 2) as i:
                body(2 * i + 1, 1)
                body(2 * i + 2, 0)
            body(B - 1, 1, last=True)
            jobs = Jobs(B, tail=True)
            for s in range(STEPS_B):
                for name, n in jobs.of[s]:
                    job(name, n, B, 0)
                finish(B - 1, s)
            dve.wait_ge(keys_done, B)

        @block.gpsimd
        def _(pool):
            nc.gpsimd.memset(ks[KS:KM], 1.0).then_inc(set_up, 1)
            pool.wait_ge(w_in, 6 * 16)

            def rows(u, b, hf, p):
                step = Steps(pool, pool_step, 3 * u)
                ord_ = 0 if isinstance(b, int) and b == 0 and hf == 0 else (10 * b - 4 + (3 if hf else -2))
                if isinstance(b, int) and b == 0 and hf == 1:
                    ord_ = 1
                if isinstance(b, int) and b == 1 and hf == 0:
                    ord_ = 4
                pool.wait_ge(job_taken, ord_ + 1)
                wait(pool, rows_in[hf], 16 * b)
                step.then(nc.gpsimd.tensor_tensor(nparts[:, 0], nrow[:], c.ones[0:UH * NT], ALU.mult))
                step.then(nc.gpsimd.tensor_tensor(nrest[:], nrow[:], nparts[:, 0], ALU.subtract))
                step.then(nc.gpsimd.tensor_tensor(nparts[:, 1], nrest[:], c.ones[0:UH * NT], ALU.mult))
                nc.gpsimd.tensor_tensor(nparts[:, 2], nrest[:], nparts[:, 1], ALU.subtract).then_inc(rows_made, 1)
                pool.wait_ge(rows_made, u + 1)
                settle(core, nc.gpsimd)
                pool.dma_start(c.rows_dram[hf].rearrange("a r q -> r a q"), nparts[:]).then_inc(rows_out, 16)
                pool.wait_ge(rows_out, 16 * (u + 1))
                settle(core, nc.gpsimd)
                pool.dma_start(qs[KS:KM, 2 * p + hf].rearrange("a h t -> a (h t)"),
                               c.rows_dram[hf].rearrange("a r q -> a (r q)")).then_inc(rows_in[hf], 16)

            def add_bias(b, p, q):
                pool.wait_ge(xn_in[p], 16 * (q + 1))
                nc.gpsimd.tensor_tensor(xnb[:, p], xnb[:, p], bo[:].unsqueeze(1).to_broadcast([P, NT, D]),
                                        ALU.add).then_inc(xnb_ready, 1)

            def finish(b):
                pool.wait_ge(ve_ready, b + 1)
                nc.gpsimd.tensor_tensor(rstd[:], ve[:], c.neg_half[:, 0:NT], ALU.pow).then_inc(rstd_ready, 1)
                pool.wait_ge(norm_ready, b + 1)
                wait(pool, x1_out, 16 * b)
                wait(pool, keys_done, b)
                nc.gpsimd.tensor_tensor(x1[:], norm[:], g1[:].unsqueeze(1).to_broadcast([P, NT, D]), ALU.mult).then_inc(x1_ready, 1)
                pool.wait_ge(x1_ready, 2 * b + 1)
                nc.gpsimd.tensor_tensor(x1[:], x1[:], b1[:].unsqueeze(1).to_broadcast([P, NT, D]), ALU.add).then_inc(x1_ready, 1)
                pool.wait_ge(x1_ready, 2 * b + 2)
                settle(core, nc.gpsimd)
                pool.dma_start(x1_tiles[b], x1[:]).then_inc(x1_out, 16)

            rows(0, 0, 0, 0)

            def body(b, p, q, first=False, last=False):
                rows(2 * b + 1, b, 1, p)
                add_bias(b, p, q)
                if not first:
                    finish(b - 1)
                if not last:
                    rows(2 * b + 2, b + 1, 0, 1 - p)

            body(0, 0, 0, first=True)
            with pool.Fori(0, (B - 2) // 2) as i:
                body(2 * i + 1, 1, i)
                body(2 * i + 2, 0, i + 1)
            body(B - 1, 1, B // 2 - 1, last=True)
            finish(B - 1)
            pool.wait_ge(x1_out, 16 * B)


def route(core):
    nc, c = core.nc, core
    with ExitStack() as ctx:
        sb = lambda name, shape, dt=FP32: core.sb(name, shape, dt, ctx)
        sem = lambda name: core.sem(name, ctx)
        whole = sb("whole", [P, TILES], I32)
        fl = sb("fl", [P, TILES])
        above = sb("above", [P, TILES])
        one_hot = sb("one_hot", [P, E, TILES])
        run = sb("run", [P, 2, E, TILES])
        at = sb("at", [P, E, TILES])
        caps = sb("caps", [P, E])
        caps_i = sb("caps_i", [P, E], I32)
        start = sb("start", [P, E])
        pos = sb("pos", [P, TILES])
        first_i = sb("first_i", [P, ETILES], I32)
        first = sb("first", [P, ETILES])
        past = sb("past", [P, E, ETILES])
        which = sb("which", [P, ETILES])
        x1 = sb("x1_rows", [P, 2, NT, D])
        idx = sb("idx", [P, NT], U32)
        step_sem = sem("step_r")
        iota_done = sem("iota_done")
        hot = sem("hot")
        counted = sem("counted")
        pos_ready = sem("pos_ready")
        x1_in = [sem("x1_in0"), sem("x1_in1")]
        idx_done = sem("idx_done")
        scattered = [sem("scattered0"), sem("scattered1")]
        block = ctx.enter_context(nc.Block())
        x1_tiles = c.x1_dram.rearrange("(b t p) d -> b p t d", t=NT, p=P)

        @block.vector
        def _(dve):
            step = Steps(dve, step_sem, 0)
            step.then(nc.vector.tensor_copy(whole[:], c.keys[:]))
            step.then(nc.vector.tensor_copy(fl[:], whole[:]))
            step.then(nc.vector.tensor_tensor(above[:], fl[:], c.keys[:], ALU.is_gt))
            step.then(nc.vector.tensor_tensor(fl[:], fl[:], above[:], ALU.subtract))
            step.then(nc.vector.tensor_copy(whole[:], fl[:]))
            step.then(nc.vector.tensor_scalar(whole[:], whole[:], E - 1, None, ALU.bitwise_and))
            step.then(nc.vector.tensor_copy(fl[:], whole[:]))
            for e in range(E):
                ins = nc.vector.tensor_scalar(one_hot[:, e], fl[:], float(e), None, ALU.is_equal)
            ins.then_inc(hot, 1)
            dve.wait_ge(counted, 1)
            within = c.bank[0][:, 0:E * TILES].rearrange("p (e t) -> p e t", e=E)
            totals = c.bank[1][:, 0:E * TILES].rearrange("p (e t) -> p e t", e=E)
            step.then(nc.vector.tensor_copy(run[:, 0], totals))
            a, shift = 0, 1
            while shift < TILES:
                nc.vector.tensor_copy(run[:, 1 - a, :, 0:shift], run[:, a, :, 0:shift])
                step.then(nc.vector.tensor_tensor(run[:, 1 - a, :, shift:], run[:, a, :, shift:],
                                                  run[:, a, :, 0:TILES - shift], ALU.add))
                a, shift = 1 - a, 2 * shift
            step.then(nc.vector.tensor_scalar(caps[:], run[:, a, :, TILES - 1], float(P - 1), None, ALU.add))
            step.then(nc.vector.tensor_copy(caps_i[:], caps[:]))
            step.then(nc.vector.tensor_scalar(caps_i[:], caps_i[:], -P, None, ALU.bitwise_and))
            step.then(nc.vector.tensor_copy(caps[:], caps_i[:]))
            step.then(nc.vector.memset(start[:], 0.0))
            for e in range(1, E):
                step.then(nc.vector.tensor_tensor(start[:, e:e + 1], start[:, e - 1:e], caps[:, e - 1:e], ALU.add))
            step.then(nc.vector.tensor_tensor(run[:, 1 - a], run[:, a], totals, ALU.subtract))
            step.then(nc.vector.tensor_tensor(at[:], within, run[:, 1 - a], ALU.add))
            step.then(nc.vector.tensor_tensor(at[:], at[:], start[:].unsqueeze(2).to_broadcast([P, E, TILES]), ALU.add))
            step.then(nc.vector.tensor_tensor(at[:], at[:], one_hot[:], ALU.mult))
            step.then(nc.vector.tensor_reduce(pos[:], at[:].rearrange("p e t -> p t e"), axis=AX.X, op=ALU.add))
            step.then(nc.vector.tensor_scalar(pos[:], pos[:], -1.0, None, ALU.add))
            nc.vector.tensor_copy(c.pos_i[:], pos[:]).then_inc(pos_ready, 1)
            dve.wait_ge(iota_done, 1)
            step.then(nc.vector.tensor_copy(first[:], first_i[:]))
            for e in range(1, E):
                ins = nc.vector.tensor_scalar(past[:, e], first[:], start[:, e:e + 1], None, ALU.is_ge)
            step.then(ins)
            step.then(nc.vector.tensor_reduce(which[:], past[:, 1:E].rearrange("p e t -> p t e"), axis=AX.X, op=ALU.add))
            step.then(nc.vector.tensor_copy(c.which_i[:], which[:]))

        @block.tensor
        def _(pe):
            pe.wait_ge(hot, 1)
            nc.tensor.matmul(c.bank[0][:, 0:E * TILES], c.upper[:], one_hot[:].rearrange("p e t -> p (e t)"), start=True, stop=True)
            nc.tensor.matmul(c.bank[1][:, 0:E * TILES], c.ones[:], one_hot[:].rearrange("p e t -> p (e t)"), start=True,
                             stop=True).then_inc(counted, 1)

        @block.sync
        def _(sp):
            def load(b, p):
                sp.dma_start(x1[:, p], x1_tiles[b]).then_inc(x1_in[p], 16)

            load(0, 0)
            load(1, 1)
            with sp.Fori(0, B // 2 - 1) as i:
                for p in range(2):
                    sp.wait_ge(scattered[p], 16 * NT * (i + 1))
                    load(2 * i + 2 + p, p)

        @block.gpsimd
        def _(pool):
            nc.gpsimd.iota(first_i[:], pattern=[[P, ETILES]], base=0, channel_multiplier=0).then_inc(iota_done, 1)
            pool.wait_ge(pos_ready, 1)

            def scatter(b, i, p):
                if p == 0:
                    wait(pool, scattered[1], 16 * NT * i)
                else:
                    pool.wait_ge(scattered[0], 16 * NT * (i + 1))
                settle(core, nc.gpsimd)
                nc.gpsimd.tensor_copy(idx[:], c.pos_i[:, bass.ts(b, NT)]).then_inc(idx_done, 1)
                pool.wait_ge(idx_done, b + 1)
                pool.wait_ge(x1_in[p], 16 * (i + 1))
                settle(core, nc.gpsimd)
                for t in range(NT):
                    pool.indirect_dma_start(c.xg_dram, bass.IndirectOffsetOnAxis(ap=idx[:, t:t + 1], axis=0),
                                            x1[:, p, t], None).then_inc(scattered[p], 16)

            scatter(0, 0, 0)
            scatter(1, 0, 1)
            with pool.Fori(1, B // 2) as i:
                for p in range(2):
                    scatter(2 * i + p, i, p)
            for p in range(2):
                pool.wait_ge(scattered[p], 16 * NT * B // 2)


def experts(core):
    nc, c, d = core.nc, core, core.i
    with ExitStack() as ctx:
        sb = lambda name, shape, dt=FP32: core.sb(name, shape, dt, ctx)
        sem = lambda name: core.sem(name, ctx)
        NH, KF = FF // 512, FF // P
        w1 = sb("w1", [P, E, KD, FF])
        w2 = sb("w2", [P, E, KF, D])
        b1 = sb("b1e", [P, E, FF])
        b2 = sb("b2e", [P, E, D])
        g2, be2 = sb("g2", [P, D]), sb("be2", [P, D])
        xg = sb("xg", [P, 4, D])
        xgT = sb("xgT", [P, 2, KD, P])
        h = sb("h", [P, FF])
        hT = sb("hT", [P, KF, P])
        res = sb("res_e", [P, D])
        sum_ = sb("sum_e", [P, D])
        stats, mv = sb("stats_e", [P, 6]), sb("mv_e", [P, 2])
        ve, rstd = sb("ve_e", [P, 1]), sb("rstd_e", [P, 1])
        norm = sb("norm_e", [P, 2, D])
        y = sb("y_e", [P, 2, D])
        w_in = sem("w_in_e")
        xg_in = [sem(f"xg_in{n}") for n in range(4)]
        x_t, x_tk = sem("x_t"), sem("x_tk")
        h_mm, h_sb = sem("h_mm"), sem("h_sb")
        h_t, h_tk = sem("h_t"), sem("h_tk")
        y_mm, y_tk = sem("y_mm"), sem("y_tk")
        dve_step = sem("step_e")
        ve_r, rstd_r, norm_r, y_r = sem("ve_r"), sem("rstd_r"), sem("norm_r"), sem("y_r")
        y_out = [sem("y_out0"), sem("y_out1")]
        block = ctx.enter_context(nc.Block())
        xg_t = c.xg_dram.rearrange("(i p) d -> i p d", p=P)
        yg_t = c.yg_dram.rearrange("(i p) d -> i p d", p=P)
        LAST = ETILES - 1
        UN = 4

        def loop(eng, body):
            for i in range(UN):
                body(i, i, 0)
            with eng.Fori(1, (ETILES - 3) // UN) as j:
                for n in range(UN):
                    body(UN * j + n, n, j)
            for i in range((ETILES - 3) // UN * UN, ETILES):
                body(i, i % UN, i // UN)

        @block.sync
        def _(sp):
            def load(i, n):
                sp.dma_start(xg[:, n], xg_t[i]).then_inc(xg_in[n], 16)

            for i in range(3):
                load(i, i)
            for e in range(E):
                sp.dma_start(w1[:, e], d["L0_ffn_W1"][e].rearrange("(k p) n -> p k n", p=P)).then_inc(w_in, 16)
                sp.dma_start(w2[:, e], d["L0_ffn_W2"][e].rearrange("(k p) n -> p k n", p=P)).then_inc(w_in, 16)
                sp.dma_start(b1[:, e], row(d["L0_ffn_b1"][e])).then_inc(w_in, 16)
                sp.dma_start(b2[:, e], row(d["L0_ffn_b2"][e])).then_inc(w_in, 16)
            sp.dma_start(g2[:], row(d["L0_ffn_ln2_g"])).then_inc(w_in, 16)
            sp.dma_start(be2[:], row(d["L0_ffn_ln2_b"])).then_inc(w_in, 16)

            def body(i, n, j):
                if not isinstance(i, int) or i + 3 < ETILES:
                    wait(sp, dve_step, 4 * i - 3)
                    load(i + 3, (n + 3) % UN)
                sp.wait_ge(y_r, 2 * i + 2)
                sp.dma_start(yg_t[i], y[:, n % 2]).then_inc(y_out[n % 2], 16)

            loop(sp, body)
            sp.wait_ge(y_out[0], 16 * ((ETILES + 1) // 2))
            sp.wait_ge(y_out[1], 16 * (ETILES // 2))

        @block.tensor
        def _(pe):
            def x_transposed(i, n, j):
                pe.wait_ge(xg_in[n], 16 * (j + 1))
                wait(pe, x_tk, i)
                for k in range(KD):
                    ins = nc.tensor.transpose(c.bank[0][:, bass.ts(k, P)], xg[:, n, bass.ts(k, P)], c.ident[:])
                ins.then_inc(x_t, 1)

            def up(i, n):
                e = pe.value_load(c.which_i[0:1, bass.ds(i, 1)], min_val=0, max_val=E - 1)
                pe.wait_ge(x_tk, i + 1)
                wait(pe, h_sb, 2 * i)
                for m in range(NH):
                    for k in range(KD):
                        ins = nc.tensor.matmul(c.bank[1 + m], xgT[:, n % 2, k], w1[:, bass.ds(e, 1), k, bass.ts(m, 512)],
                                               start=k == 0, stop=k == KD - 1)
                    ins.then_inc(h_mm, 1)

            def h_transposed(i):
                for m in range(2):
                    pe.wait_ge(h_sb, 2 * i + 1 + m)
                    wait(pe, h_tk, 2 * i - 1 + m)
                    for k in range(4):
                        ins = nc.tensor.transpose(c.bank[3 + m][:, bass.ts(k, P)], h[:, bass.ts(4 * m + k, P)], c.ident[:])
                    ins.then_inc(h_t, 1)

            def down(i):
                e = pe.value_load(c.which_i[0:1, bass.ds(i, 1)], min_val=0, max_val=E - 1)
                pe.wait_ge(h_tk, 2 * i + 2)
                wait(pe, y_tk, i)
                for k in range(KF):
                    ins = nc.tensor.matmul(c.bank[5][:, 0:D], hT[:, k], w2[:, bass.ds(e, 1), k], start=k == 0, stop=k == KF - 1)
                ins.then_inc(y_mm, 1)

            pe.wait_ge(w_in, 16 * 18)
            x_transposed(0, 0, 0)
            up(0, 0)
            x_transposed(1, 1, 0)

            def body(i, n, j):
                h_transposed(i)
                if not isinstance(i, int) or i + 1 < ETILES:
                    up(i + 1, n + 1)
                if not isinstance(i, int) or i + 2 < ETILES:
                    x_transposed(i + 2, (n + 2) % UN, j + (n + 2) // UN)
                down(i)

            loop(pe, body)

        @block.scalar
        def _(act):
            act.wait_ge(w_in, 16 * 18)

            def x_copy(i, n):
                act.wait_ge(x_t, i + 1)
                wait(act, h_mm, 2 * i - 2)
                nc.scalar.copy(xgT[:, n % 2], c.bank[0][:, 0:KD * P].rearrange("p (k q) -> p k q", k=KD)).then_inc(x_tk, 1)

            x_copy(0, 0)

            def body(i, n, j):
                if not isinstance(i, int) or i + 1 < ETILES:
                    x_copy(i + 1, n + 1)
                for m in range(2):
                    act.wait_ge(h_t, 2 * i + 1 + m)
                    wait(act, y_mm, i)
                    nc.scalar.activation(hT[:, 4 * m:4 * m + 4], c.bank[3 + m].rearrange("p (k q) -> p k q", k=4),
                                         ACT.Relu).then_inc(h_tk, 1)

            loop(act, body)

        @block.vector
        def _(dve):
            dve.wait_ge(w_in, 16 * 18)

            def bias(i):
                e = dve.value_load(c.which_i[0:1, bass.ds(i, 1)], min_val=0, max_val=E - 1)
                for m in range(NH):
                    dve.wait_ge(h_mm, 2 * i + 1 + m)
                    wait(dve, h_t, 2 * i - 1 + m)
                    nc.vector.tensor_tensor(h[:, bass.ts(m, 512)].unsqueeze(1), c.bank[1 + m].unsqueeze(1),
                                            b1[:, bass.ds(e, 1), bass.ts(m, 512)], ALU.add).then_inc(h_sb, 1)

            def tail(i, n):
                e = dve.value_load(c.which_i[0:1, bass.ds(i, 1)], min_val=0, max_val=E - 1)
                step = Steps(dve, dve_step, 4 * i)
                dve.wait_ge(y_mm, i + 1)
                nc.vector.tensor_tensor(sum_[:].unsqueeze(1), c.bank[5][:, 0:D].unsqueeze(1), b2[:, bass.ds(e, 1)],
                                        ALU.add).then_inc(y_tk, 1)
                dve.wait_ge(y_tk, i + 1)
                step.then(nc.vector.tensor_tensor(res[:], sum_[:], xg[:, n], ALU.add))
                step.then(nc.vector.bn_stats(stats[:], res[:]), core)
                step.then(nc.vector.bn_aggr(mv[:], stats[:]))
                nc.vector.tensor_scalar(ve[:], mv[:, 1:2], EPS, None, ALU.add).then_inc(ve_r, 1)
                dve.wait_ge(rstd_r, i + 1)
                wait(dve, y_r, 2 * i - 2)
                step.then(nc.vector.tensor_scalar(norm[:, n % 2], res[:], mv[:, 0:1], rstd[:], ALU.subtract, ALU.mult))

            bias(0)

            def body(i, n, j):
                if not isinstance(i, int) or i + 1 < ETILES:
                    bias(i + 1)
                tail(i, n)

            loop(dve, body)

        @block.gpsimd
        def _(pool):
            pool.wait_ge(w_in, 16 * 18)

            def body(i, n, j):
                pool.wait_ge(ve_r, i + 1)
                nc.gpsimd.tensor_tensor(rstd[:], ve[:], c.neg_half[:, 0:1], ALU.pow).then_inc(rstd_r, 1)
                pool.wait_ge(dve_step, 4 * i + 4)
                wait(pool, y_out[n % 2], 16 * (2 * j + n // 2))
                nc.gpsimd.tensor_tensor(y[:, n % 2], norm[:, n % 2], g2[:], ALU.mult).then_inc(y_r, 1)
                pool.wait_ge(y_r, 2 * i + 1)
                nc.gpsimd.tensor_tensor(y[:, n % 2], y[:, n % 2], be2[:], ALU.add).then_inc(y_r, 1)

            loop(pool, body)


def collect(core):
    nc, c = core.nc, core
    with ExitStack() as ctx:
        sb = lambda name, shape, dt=FP32: core.sb(name, shape, dt, ctx)
        sem = lambda name: core.sem(name, ctx)
        y = sb("y_c", [P, 2, NT, D])
        r = sb("r_c", [P, 2, NT, D])
        o = sb("o_c", [P, 2, NT, D])
        idx = sb("idx_c", [P, 2, NT], U32)
        gathered = [sem("gathered0"), sem("gathered1")]
        r_in = [sem("r_in0"), sem("r_in1")]
        idx_done, added = sem("idx_done_c"), sem("added")
        out_done = [sem("out_done0"), sem("out_done1")]
        block = ctx.enter_context(nc.Block())
        r_tiles = c.r_dram.rearrange("(b t p) d -> b p t d", t=NT, p=P)
        out_tiles = c.out.rearrange("b (t p) d -> b p t d", p=P)

        def loop(eng, body):
            for b in range(2):
                body(b, b, 0)
            with eng.Fori(1, B // 2) as i:
                for p in range(2):
                    body(2 * i + p, p, i)

        @block.gpsimd
        def _(pool):
            def body(b, p, i):
                wait(pool, gathered[p], 16 * NT * i)
                wait(pool, added, b - 1)
                settle(core, nc.gpsimd)
                nc.gpsimd.tensor_copy(idx[:, p], c.pos_i[:, bass.ts(b, NT)]).then_inc(idx_done, 1)
                pool.wait_ge(idx_done, b + 1)
                settle(core, nc.gpsimd)
                for t in range(NT):
                    pool.indirect_dma_start(y[:, p, t], None, c.yg_dram,
                                            bass.IndirectOffsetOnAxis(ap=idx[:, p, t:t + 1], axis=0)).then_inc(gathered[p], 16)

            loop(pool, body)

        @block.vector
        def _(dve):
            def body(b, p, i):
                dve.wait_ge(gathered[p], 16 * NT * (i + 1))
                dve.wait_ge(r_in[p], 16 * (i + 1))
                wait(dve, out_done[p], 16 * i)
                nc.vector.tensor_tensor(o[:, p], y[:, p], r[:, p], ALU.add).then_inc(added, 1)

            loop(dve, body)

        @block.scalar
        def _(act):
            def body(b, p, i):
                act.wait_ge(added, b + 1)
                act.dma_start(out_tiles[b], o[:, p]).then_inc(out_done[p], 16)

            loop(act, body)
            for p in range(2):
                act.wait_ge(out_done[p], 16 * B // 2)

        @block.sync
        def _(sp):
            def body(b, p, i):
                wait(sp, added, b - 1)
                sp.dma_start(r[:, p], r_tiles[b]).then_inc(r_in[p], 16)

            loop(sp, body)


def mamba(core):
    nc, c, d = core.nc, core, core.i
    with ExitStack() as ctx:
        sb = lambda name, shape, dt=FP32: core.sb(name, shape, dt, ctx)
        sem = lambda name: core.sem(name, ctx)
        Z0, X0, B0, C0, DT0 = 0, INNER, 2 * INNER, 2 * INNER + STATE, 2 * INNER + 2 * STATE
        win = sb("win", [P, KD, PROJ])
        wc2 = sb("wc2", [P, KD, 2 * STATE])
        wout = sb("wout", [P, JI, D])
        g_ln, be_ln = sb("g_lnm", [P, KD]), sb("be_lnm", [P, KD])
        be_wide = sb("be_wide", [P, KD, P])
        b_row = sb("b_row", [P, INNER + STATE])
        b_in_row = sb("b_in_row", [P, PROJ - INNER])
        dtb = sb("dtb", [P, HEADS])
        dtb_in = sb("dtb_in", [P, HEADS])
        bz, bz_in = sb("bz", [P, JI]), sb("bz_in", [P, JI])
        bB, bB_in = sb("bB", [STATE, 1]), sb("bB_in", [STATE, 1])
        bC, bC_in = sb("bC", [P, 1]), sb("bC_in", [P, 1])
        b_out = sb("b_out_row", [P, D])
        d_row = sb("d_row", [P, HEADS])
        a_row = sb("a_row", [P, HEADS])
        sp_a, sp_b, sp_c, sp_d, sp_e = (sb(f"sp{n}", [P, TILES, HEADS]) for n in range(5))
        a_all = sb("a_all", [P, TILES, HEADS])
        nxT = sb("nxT_m", [P, 2, KD, P])
        xr = sb("xr", [P, 2, 2, D])
        resid = sb("resid", [P, 2, D])
        aU = sb("aU", [P, 2, HEADS, P])
        xs = sb("xs", [P, INNER])
        Bs = sb("Bs", [P, 2, STATE])
        BT = sb("BT", [STATE, P])
        CT = sb("CT", [P, 2, P])
        z = sb("z", [P, JI, P])
        th = sb("th", [P, JI, P])
        gate = sb("gate", [P, 2, JI, P])
        L = sb("L", [P, 2, HEADS, P])
        E2 = sb("E2", [P, 2, JI, P])
        Gm = sb("Gm", [P, P])
        M = sb("M", [P, 2, HEADS, P])
        CE = sb("CE", [P, 2, JI, P])
        dtx = sb("dtx", [P, 2, HEADS, PW])
        wdtx = sb("wdtx", [P, 2, HEADS, PW])
        xsD = sb("xsD", [P, 2, HEADS, PW])
        Hs = sb("Hs", [P, JI, PW])
        HB = sb("HB", [P, JI, P])
        yg = sb("yg", [P, JI, P])
        r = sb("r_m", [P, 2, D])

        w_in, set_step, set_act, set_done = sem("w_in_m"), sem("set_step"), sem("set_act"), sem("set_done")
        bias_mm = sem("bias_mm")
        nx_in = [sem("nx_in0"), sem("nx_in1")]
        xr_in = [sem("xr_in0"), sem("xr_in1")]
        aU_r, resid_r, resid_s, wdtx_r, xsD_r = (sem(n) for n in ("aU_r", "resid_r", "resid_s", "wdtx_r", "xsD_r"))
        xs_mm, bc_mm, z_mm, cum_mm, e_mm, g_mm, y_mm, st_mm, out_mm = (
            sem(n) for n in ("xs_mm", "bc_mm", "z_mm", "cum_mm", "e_mm", "g_mm", "y_mm_m", "st_mm", "out_mm"))
        xs_r, bc_r, dtx_r, gate_r, Gm_r, M_r, CE_r, yg_r, h_step, h_r, r_r = (
            sem(n) for n in ("xs_r", "bc_r", "dtx_r", "gate_r", "Gm_r", "M_r", "CE_r", "yg_r", "h_step", "h_r", "r_r"))
        z_r, th_r, L_r, E_r, HB_r = (sem(n) for n in ("z_r", "th_r", "L_r", "E_r", "HB_r"))
        r_out = [sem("r_out0"), sem("r_out1")]
        block = ctx.enter_context(nc.Block())
        W_LOADS = 17
        x_t = d["L0_attn_input_tensor"].rearrange("b (t p) d -> (b t) p d", p=P)
        xn_t = c.xn_dram.rearrange("(i p) d -> i p d", p=P)
        r_t = c.r_dram.rearrange("(i p) d -> i p d", p=P)

        def chunks(eng, body):
            for n in range(NT):
                body(n, 0, n)
            with eng.Fori(1, B - 1) as b:
                for n in range(NT):
                    body(NT * b + n, b, n)
            for n in range(NT):
                body(NT * (B - 1) + n, B - 1, n)

        @block.sync
        def _(sp):
            ld = lambda dst, src: sp.dma_start(dst, src).then_inc(w_in, 16)
            ld(win[:], d["L0_attn_W_in"].rearrange("(k p) n -> p k n", p=P))
            b_in = d["L0_attn_b_in"]
            with nc.allow_non_contiguous_dma(reason="small vectors"):
                ld(g_ln[:], d["L0_attn_ln_gamma"].rearrange("(k p) -> p k", p=P))
                ld(be_ln[:], d["L0_attn_ln_beta"].rearrange("(k p) -> p k", p=P))
                ld(bz_in[:], b_in[Z0:Z0 + INNER].rearrange("(k p) -> p k", p=P))
                ld(bB_in[:], b_in[B0:B0 + STATE].rearrange("(p o) -> p o", o=1))
                for half in range(2):
                    ld(bC_in[STATE * half:STATE * half + STATE], b_in[C0:C0 + STATE].rearrange("(p o) -> p o", o=1))
            for k in range(2):
                ld(wc2[:, :, bass.ts(k, STATE)], d["L0_attn_W_in"][:, C0:C0 + STATE].rearrange("(k p) n -> p k n", p=P))
            ld(b_in_row[:], row(b_in[INNER:PROJ]))
            ld(dtb_in[:], row(d["L0_attn_dt_bias"]))
            ld(a_row[:], row(d["L0_attn_A_log"]))
            ld(d_row[:], row(d["L0_attn_D_skip"]))
            ld(b_out[:], row(d["L0_attn_b_out"]))
            ld(wout[:], d["L0_attn_W_out"].rearrange("(j p) n -> p j n", p=P))
            sp.dma_start(dtb[:], row(b_in[DT0:PROJ])).then_inc(w_in, 16)
            assert W_LOADS == 17

            def load(i, p):
                sp.dma_start(nxT[:, p], c.nxT_dram[:, :, bass.ts(i, P)].rearrange("k p t -> p k t")).then_inc(nx_in[p], 16)
                sp.dma_start(xr[:, p, 0], x_t[i]).then_inc(xr_in[p], 16)
                sp.dma_start(xr[:, p, 1], xn_t[i]).then_inc(xr_in[p], 16)

            load(0, 0)
            load(1, 1)

            def body(i, b, n):
                sp.wait_ge(r_r, i + 1)
                sp.dma_start(r_t[i], r[:, n % 2]).then_inc(r_out[n % 2], 16)
                if not isinstance(i, int) or i + 2 < TILES:
                    sp.wait_ge(z_mm, i + 1)
                    sp.wait_ge(resid_s, i + 1)
                    load(i + 2, n % 2)

            chunks(sp, body)
            for p in range(2):
                sp.wait_ge(r_out[p], 16 * TILES // 2)

        @block.tensor
        def _(pe):
            pe.wait_ge(w_in, 16 * (W_LOADS - 1))
            pe.wait_ge(set_step, 1)
            mm = nc.tensor.matmul
            for k in range(KD):
                mm(c.bank[0], be_wide[:, k], win[:, k, X0:X0 + INNER], start=k == 0, stop=k == 1)
            for k in range(KD):
                mm(c.bank[1][:, 0:STATE], be_wide[:, k], win[:, k, B0:B0 + STATE], start=k == 0, stop=k == 1)
            for k in range(KD):
                mm(c.bank[1][:, 64:64 + HEADS], be_wide[:, k], win[:, k, DT0:PROJ], start=k == 0, stop=k == 1)
            for j in range(JI):
                for k in range(KD):
                    mm(c.bank[2][:, j:j + 1], win[:, k, bass.ts(j, P)], be_ln[:, k:k + 1], start=k == 0, stop=k == 1)
            for k in range(KD):
                mm(c.bank[2][0:STATE, 8:9], win[:, k, B0:B0 + STATE], be_ln[:, k:k + 1], start=k == 0, stop=k == 1)
            for k in range(KD):
                ins = mm(c.bank[2][:, 9:10], wc2[:, k], be_ln[:, k:k + 1], start=k == 0, stop=k == 1)
            ins.then_inc(bias_mm, 1)
            pe.wait_ge(set_done, 1)

            def front(i, b, n):
                p = n % 2
                pe.wait_ge(nx_in[p], 16 * (2 * b + n // 2 + 1))
                wait(pe, xs_r, i)
                for k in range(KD):
                    ins = mm(c.bank[0], nxT[:, p, k], win[:, k, X0:X0 + INNER], start=k == 0, stop=k == 1)
                ins.then_inc(xs_mm, 1)
                wait(pe, bc_r, i)
                wait(pe, Gm_r, i)
                for k in range(KD):
                    mm(c.bank[1][:, 0:STATE], nxT[:, p, k], win[:, k, B0:B0 + STATE], start=k == 0, stop=k == 1)
                for k in range(KD):
                    mm(c.bank[1][0:STATE, P:2 * P], win[:, k, B0:B0 + STATE], nxT[:, p, k], start=k == 0, stop=k == 1)
                for k in range(KD):
                    ins = mm(c.bank[1][:, 2 * P:3 * P], wc2[:, k], nxT[:, p, k], start=k == 0, stop=k == 1)
                ins.then_inc(bc_mm, 1)
                wait(pe, z_r, i)
                for j in range(JI):
                    for k in range(KD):
                        ins = mm(c.bank[2][:, bass.ts(j, P)], win[:, k, bass.ts(j, P)], nxT[:, p, k], start=k == 0, stop=k == 1)
                ins.then_inc(z_mm, 1)
                pe.wait_ge(aU_r, i + 1)
                wait(pe, L_r, i)
                for half in range(2):
                    ins = mm(c.bank[4 + half], c.strict[:], aU[:, p, 4 * half:4 * half + 4], start=True, stop=True)
                ins.then_inc(cum_mm, 1)
                wait(pe, E_r, i)
                for odd in range(2):
                    ins = mm(c.bank[6][STATE * odd:STATE * odd + STATE], c.ones[:, 0:STATE], aU[:, p, odd:HEADS:2],
                             start=True, stop=True)
                ins.then_inc(e_mm, 1)

            def cb(i, n):
                pe.wait_ge(bc_r, i + 1)
                mm(c.bank[1][:, 3 * P:4 * P], BT[:], CT[0:STATE, n % 2], start=True, stop=True).then_inc(g_mm, 1)

            def back(i, b, n):
                p = n % 2
                pe.wait_ge(xsD_r, i + 1)
                pe.wait_ge(M_r, i + 1)
                pe.wait_ge(CE_r, i + 1)
                wait(pe, yg_r, i)
                if n > 0:
                    pe.wait_ge(HB_r, 2 * (3 * b + n))
                for j in range(JI):
                    out = c.bank[7][:, bass.ts(j, P)]
                    mm(out, xsD[:, p, 2 * j:2 * j + 2].rearrange("p h e -> p (h e)"), c.ident[:], start=True, stop=False)
                    if n > 0:
                        mm(out, HB[:, j], CE[:, p, j], start=False, stop=False)
                    for odd in range(2):
                        ins = mm(c.bank[7][PW * odd:PW * odd + PW, bass.ts(j, P)], dtx[:, p, 2 * j + odd], M[:, p, 2 * j + odd],
                                 start=False, stop=True)
                ins.then_inc(y_mm, 1)
                if n < NT - 1:
                    pe.wait_ge(wdtx_r, i + 1)
                    wait(pe, r_r, i)
                    for odd in range(2):
                        ins = mm(c.bank[3][STATE * odd:STATE * odd + STATE, 0:JI * PW], Bs[:, p],
                                 wdtx[:, p, odd:HEADS:2], start=True, stop=True)
                    ins.then_inc(st_mm, 1)

            def outs(i, b, n):
                pe.wait_ge(yg_r, i + 1)
                if n < NT - 1:
                    pe.wait_ge(h_r, 3 * b + n + 1)
                else:
                    wait(pe, r_r, i)
                for j in range(JI):
                    ins = mm(c.bank[3][:, D:2 * D], yg[:, j], wout[:, j], start=j == 0, stop=j == JI - 1)
                ins.then_inc(out_mm, 1)

            front(0, 0, 0)
            cb(0, 0)

            def body(i, b, n):
                more = not isinstance(i, int) or i + 1 < TILES
                if more:
                    front(i + 1, b + (n + 1) // NT, (n + 1) % NT)
                back(i, b, n)
                if more:
                    cb(i + 1, n + 1)
                outs(i, b, n)

            chunks(pe, body)

        @block.scalar
        def _(act):
            act.wait_ge(w_in, 16 * (W_LOADS - 1))
            nc.scalar.activation(a_row[:], a_row[:], ACT.Exp).then_inc(set_act, 1)
            act.wait_ge(set_step, 2)
            nc.scalar.activation(sp_b[:], sp_b[:], ACT.Exp).then_inc(set_act, 1)
            act.wait_ge(set_step, 3)
            nc.scalar.activation(sp_d[:], sp_c[:], ACT.Ln).then_inc(set_act, 1)
            act.wait_ge(set_done, 1)

            def front(i, n):
                p = n % 2
                act.wait_ge(z_mm, i + 1)
                wait(act, gate_r, i)
                for j in range(JI):
                    ins = nc.scalar.activation(z[:, j], c.bank[2][:, bass.ts(j, P)], ACT.Identity, bias=bz[:, j:j + 1])
                ins.then_inc(z_r, 1)
                act.wait_ge(z_r, i + 1)
                nc.scalar.activation(th[:], z[:], ACT.Tanh, scale=0.5).then_inc(th_r, 1)
                act.wait_ge(cum_mm, i + 1)
                wait(act, M_r, i - 1)
                wait(act, wdtx_r, i - 1)
                nc.scalar.activation(L[:, p], c.psum[:, 4:6].rearrange("p a (h t) -> p (a h) t", t=P), ACT.Exp).then_inc(L_r, 1)
                act.wait_ge(e_mm, i + 1)
                wait(act, CE_r, i - 1)
                wait(act, h_r, h_before)
                nc.scalar.activation(E2[:, p], c.bank[6].rearrange("p (j t) -> p j t", t=P), ACT.Exp).then_inc(E_r, 1)

            h_before = 0
            front(0, 0)

            def body(i, b, n):
                nonlocal h_before
                if not isinstance(i, int) or i + 1 < TILES:
                    h_before = 3 * b + n if n < NT - 1 else 3 * b + NT - 1
                    front(i + 1, (n + 1) % NT)
                if n < NT - 1:
                    act.wait_ge(h_r, 3 * b + n + 1)
                    act.wait_ge(y_mm, i + 1)
                    for odd in range(2):
                        rows = slice(STATE * odd, STATE * odd + STATE)
                        nc.scalar.copy(HB[rows, :, bass.ts(odd, PW)], Hs[rows]).then_inc(HB_r, 1)

            chunks(act, body)

        @block.vector
        def _(dve):
            dve.wait_ge(w_in, 16 * (W_LOADS - 1))
            v = nc.vector
            v.memset(HB[:], 0.0)
            v.tensor_copy(be_wide[:], be_ln[:].unsqueeze(2).to_broadcast([P, KD, P])).then_inc(set_step, 1)
            dve.wait_ge(bias_mm, 1)
            v.tensor_tensor(b_row[:, 0:INNER], c.bank[0], b_in_row[:, 0:INNER], ALU.add)
            v.tensor_tensor(b_row[:, INNER:], c.bank[1][:, 0:STATE], b_in_row[:, INNER:INNER + STATE], ALU.add)
            v.tensor_tensor(dtb[:], c.bank[1][:, 64:64 + HEADS], b_in_row[:, PROJ - INNER - HEADS:], ALU.add)
            v.tensor_tensor(bz[:], c.bank[2][:, 0:JI], bz_in[:], ALU.add)
            v.tensor_tensor(bB[:], c.bank[2][0:STATE, 8:9], bB_in[:], ALU.add)
            v.tensor_tensor(bC[:], c.bank[2][:, 9:10], bC_in[:], ALU.add)
            for k in range(KD):
                v.tensor_scalar(win[:, k], win[:, k], g_ln[:, k:k + 1], None, ALU.mult)
                v.tensor_scalar(wc2[:, k], wc2[:, k], g_ln[:, k:k + 1], None, ALU.mult)
            step = Steps(dve, h_step, 0)
            step.then(v.tensor_scalar(wout[:], wout[:], 0.5, None, ALU.mult))
            step.then(v.tensor_tensor(dtb[:], dtb[:], dtb_in[:], ALU.add))
            step.then(v.tensor_tensor(sp_a[:], c.dt_all[:], dtb[:].unsqueeze(1).to_broadcast([P, TILES, HEADS]), ALU.add))
            step.then(v.tensor_scalar(sp_b[:], sp_a[:], -1.0, None, ALU.mult))
            v.tensor_tensor(sp_b[:], sp_b[:], sp_a[:], ALU.min).then_inc(set_step, 1)
            dve.wait_ge(set_act, 2)
            v.tensor_scalar(sp_c[:], sp_b[:], 1.0, None, ALU.add).then_inc(set_step, 1)
            dve.wait_ge(set_act, 3)
            step.then(v.tensor_scalar(sp_c[:], sp_c[:], -1.0, None, ALU.add))
            step.then(v.tensor_scalar(sp_e[:], sp_c[:], 0.0, None, ALU.is_equal))
            step.then(v.tensor_tensor(sp_c[:], sp_c[:], sp_e[:], ALU.add))
            step.then(v.reciprocal(sp_c[:], sp_c[:]))
            step.then(v.tensor_tensor(sp_d[:], sp_d[:], sp_e[:], ALU.add))
            step.then(v.tensor_tensor(sp_d[:], sp_d[:], sp_c[:], ALU.mult))
            step.then(v.tensor_tensor(sp_d[:], sp_d[:], sp_b[:], ALU.mult))
            step.then(v.tensor_scalar(sp_a[:], sp_a[:], 0.0, None, ALU.max))
            step.then(v.tensor_tensor(c.dt_all[:], sp_a[:], sp_d[:], ALU.add))
            step.then(v.tensor_scalar(a_row[:], a_row[:], -1.0, None, ALU.mult))
            v.tensor_tensor(a_all[:], c.dt_all[:], a_row[:].unsqueeze(1).to_broadcast([P, TILES, HEADS]),
                            ALU.mult).then_inc(set_done, 1)
            H0 = step.at

            def front_a(i, n):
                p = n % 2
                dve.wait_ge(xs_mm, i + 1)
                wait(dve, xsD_r, i)
                v.tensor_tensor(xs[:], c.bank[0], b_row[:, 0:INNER], ALU.add).then_inc(xs_r, 1)
                dve.wait_ge(bc_mm, i + 1)
                wait(dve, st_mm, st_before)
                wait(dve, g_mm, i)
                v.tensor_tensor(Bs[:, p], c.bank[1][:, 0:STATE], b_row[:, INNER:], ALU.add)
                v.tensor_scalar(BT[:], c.bank[1][0:STATE, P:2 * P], bB[:], None, ALU.add)
                v.tensor_scalar(CT[:, p], c.bank[1][:, 2 * P:3 * P], bC[:], None, ALU.add).then_inc(bc_r, 1)
                dve.wait_ge(xs_r, i + 1)
                wait(dve, y_mm, i - 1)
                v.tensor_tensor(dtx[:, p], xs[:].rearrange("p (h e) -> p h e", h=HEADS),
                                c.dt_all[:, bass.ds(i, 1)].rearrange("p o h -> p (o h)").unsqueeze(2).to_broadcast([P, HEADS, PW]),
                                ALU.mult).then_inc(dtx_r, 1)

            def front_b(i, n):
                p = n % 2
                dve.wait_ge(g_mm, i + 1)
                v.tensor_tensor(Gm[:], c.bank[1][:, 3 * P:4 * P], c.upper[:], ALU.mult).then_inc(Gm_r, 1)
                dve.wait_ge(Gm_r, i + 1)
                dve.wait_ge(L_r, i + 1)
                v.tensor_tensor(M[:, p], L[:, p], Gm[:].unsqueeze(1).to_broadcast([P, HEADS, P]), ALU.mult).then_inc(M_r, 1)
                dve.wait_ge(E_r, i + 1)
                v.tensor_tensor(CE[:, p], E2[:, p], CT[:, p].unsqueeze(1).to_broadcast([P, JI, P]), ALU.mult).then_inc(CE_r, 1)
                dve.wait_ge(th_r, i + 1)
                v.scalar_tensor_tensor(out=gate[:, p], in0=th[:], scalar=1.0, in1=z[:], op0=ALU.add,
                                       op1=ALU.mult).then_inc(gate_r, 1)

            st_before = 0
            front_a(0, 0)
            front_b(0, 0)

            def body(i, b, n):
                nonlocal st_before
                more = not isinstance(i, int) or i + 1 < TILES
                if more:
                    st_before = 3 * b + n
                    front_a(i + 1, (n + 1) % NT)
                dve.wait_ge(y_mm, i + 1)
                dve.wait_ge(gate_r, i + 1)
                wait(dve, out_mm, i)
                v.tensor_tensor(yg[:], c.bank[7].rearrange("p (j t) -> p j t", t=P), gate[:, n % 2], ALU.mult).then_inc(yg_r, 1)
                if n < NT - 1:
                    own = c.bank[3][:, 0:JI * PW].rearrange("p (j e) -> p j e", j=JI)
                    wait(dve, HB_r, 2 * (3 * b + n))
                    dve.wait_ge(st_mm, 3 * b + n + 1)
                    if n == 0:
                        v.tensor_copy(Hs[:], own).then_inc(h_r, 1)
                    else:
                        v.tensor_tensor(Hs[:], Hs[:], E2[:, n % 2, :, P - 1:P].to_broadcast([P, JI, PW]),
                                        ALU.mult).then_inc(h_step, 1)
                        dve.wait_ge(h_step, H0 + 2 * b + n)
                        v.tensor_tensor(Hs[:], Hs[:], own, ALU.add).then_inc(h_r, 1)
                if more:
                    front_b(i + 1, (n + 1) % NT)
                dve.wait_ge(out_mm, i + 1)
                dve.wait_ge(resid_r, i + 1)
                wait(dve, r_out[n % 2], 16 * (2 * b + n // 2))
                v.tensor_tensor(r[:, n % 2], c.bank[3][:, D:2 * D], resid[:, n % 2], ALU.add).then_inc(r_r, 1)

            chunks(dve, body)

        @block.gpsimd
        def _(pool):
            pool.wait_ge(set_done, 1)
            g = nc.gpsimd

            def front(i, b, n):
                p = n % 2
                wait(pool, e_mm, i - 1)
                g.tensor_tensor(aU[:, p], c.upper[:].unsqueeze(1).to_broadcast([P, HEADS, P]),
                                a_all[:, bass.ds(i, 1)].rearrange("p o h -> p (o h)").unsqueeze(2).to_broadcast([P, HEADS, P]),
                                ALU.mult).then_inc(aU_r, 1)
                pool.wait_ge(xs_r, i + 1)
                wait(pool, y_mm, i - 1)
                g.tensor_tensor(xsD[:, p], xs[:].rearrange("p (h e) -> p h e", h=HEADS),
                                d_row[:].unsqueeze(2).to_broadcast([P, HEADS, PW]), ALU.mult).then_inc(xsD_r, 1)
                pool.wait_ge(dtx_r, i + 1)
                pool.wait_ge(L_r, i + 1)
                g.tensor_tensor(wdtx[:, p], dtx[:, p], L[:, p, :, P - 1:P].to_broadcast([P, HEADS, PW]), ALU.mult).then_inc(wdtx_r, 1)
                pool.wait_ge(xr_in[p], 32 * (2 * b + n // 2 + 1))
                wait(pool, r_r, i - 1)
                g.tensor_tensor(resid[:, p], xr[:, p, 0], xr[:, p, 1], ALU.add).then_inc(resid_s, 1)
                pool.wait_ge(resid_s, i + 1)
                g.tensor_tensor(resid[:, p], resid[:, p], b_out[:], ALU.add).then_inc(resid_r, 1)

            front(0, 0, 0)

            def body(i, b, n):
                if not isinstance(i, int) or i + 1 < TILES:
                    front(i + 1, b + (n + 1) // NT, (n + 1) % NT)

            chunks(pool, body)


def build(nc, ins, out):
    with ExitStack() as ctx:
        core = Core(nc, ctx, ins, out)
        constants(core)
        project(core)
        attend(core)
        route(core)
        mamba(core)
        experts(core)
        collect(core)


_INS = ['L0_attn_input_tensor', 'L0_attn_ln_gamma', 'L0_attn_ln_beta', 'L0_attn_W_in', 'L0_attn_b_in',
        'L0_attn_A_log', 'L0_attn_D_skip', 'L0_attn_dt_bias', 'L0_attn_W_out', 'L0_attn_b_out', 'L0_ffn_Wq',
        'L0_ffn_bq', 'L0_ffn_Wk', 'L0_ffn_bk', 'L0_ffn_Wv', 'L0_ffn_bv', 'L0_ffn_Wo', 'L0_ffn_bo',
        'L0_ffn_router_w', 'L0_ffn_router_b', 'L0_ffn_W1', 'L0_ffn_b1', 'L0_ffn_W2', 'L0_ffn_b2',
        'L0_ffn_ln1_g', 'L0_ffn_ln1_b', 'L0_ffn_ln2_g', 'L0_ffn_ln2_b']


def kernel(**inputs):
    import numpy as np
    import concourse.bacc as bacc
    from concourse.bass_utils import run_bass_kernel_spmd

    nc = bacc.Bacc("TRN2", target_bir_lowering=False, num_devices=1)
    arrays, ins = {}, {}
    for name in _INS:
        a = np.ascontiguousarray(inputs[name])
        arrays["in_" + name] = a
        ins[name] = nc.dram_tensor("in_" + name, a.shape, mybir.dt.from_np(a.dtype), kind="ExternalInput").ap()
    out = nc.dram_tensor("out_0", (B, T, D), FP32, kind="ExternalOutput").ap()
    build(nc, ins, out)
    result = run_bass_kernel_spmd(nc, [arrays], core_ids=[0])
    return result.results[0]["out_0"]
```

```python
import concourse.bass as bass
from concourse import mybir
from contextlib import ExitStack

FP32 = mybir.dt.float32
BF16 = mybir.dt.bfloat16
I32 = mybir.dt.int32
U32 = mybir.dt.uint32
ALU = mybir.AluOpType
ACT = mybir.ActivationFunctionType
AX = mybir.AxisListType

P = 128
B, T, D = 8, 512, 256
NT = T // P
TILES = B * NT
KD = D // P
H, HD = 16, 16
UH = P // HD
PARTS = 3
PAIRS_Q = (0, 0, 1, 1, 0, 2)
PAIRS_K = (0, 1, 0, 1, 2, 0)
KS = len(PAIRS_Q) * HD
KM = KS + PARTS
SCALE = HD ** -0.5
INNER, STATE, HEADS, PW = 512, 64, 8, 64
PROJ = 2 * INNER + 2 * STATE + HEADS
JI = INNER // P
E, FF = 4, 1024
ETILES = TILES + E - 1
TAIL = E * P
REGION = B * T + TAIL
EPS = 1e-5


def wait(eng, sem, value):
    if not isinstance(value, int) or value > 0:
        eng.wait_ge(sem, value)


def settle(core, eng):
    cell = core.pad[:, core.pads:core.pads + 1]
    core.pads += 1
    if eng is core.nc.vector:
        eng.memset(cell, 0.0)
    else:
        eng.tensor_tensor(cell, core.ones[0:1, 0:1], core.ones[0:1, 0:1], ALU.mult)


class Steps:

    def __init__(self, eng, sem, base):
        self.eng, self.sem, self.at = eng, sem, base

    def then(self, ins, core=None):
        ins.then_inc(self.sem, 1)
        self.at = self.at + 1
        self.eng.wait_ge(self.sem, self.at)
        if core:
            settle(core, core.nc.vector)


class Core:

    def __init__(self, nc, ctx, ins, out):
        self.nc, self.ctx, self.i, self.out = nc, ctx, ins, out
        self.psum = ctx.enter_context(nc.psum_tensor("psum", [P, 8, 512], FP32))
        self.bank = [self.psum[:, n] for n in range(8)]

        def dram(name, shape, dt=FP32):
            return nc.dram_tensor(name, shape, dt).ap()

        self.xn_dram = dram("xn_scratch", [B * T, D])
        self.nxT_dram = dram("nxT_scratch", [KD, P, B * T])
        self.parts_dram = dram("qk_parts", [2, B, 2, PARTS, P, T], BF16)
        self.rows_dram = dram("max_rows", [2, PARTS, UH * NT, P], BF16)
        self.v_dram = dram("v_scratch", [B * T, H * 2 * HD])
        self.xg_dram = dram("x1_grouped", [E * REGION, D])
        self.yg_dram = dram("y_grouped", [ETILES * P, D])
        self.pad, self.pads = self.sb("pad", [1, 128]), 0
        self.ident = self.sb("ident", [P, P])
        self.upper = self.sb("upper", [P, P])
        self.strict = self.sb("strict", [P, P])
        self.ones = self.sb("ones", [P, P])
        self.neg_half = self.sb("neg_half", [P, 8])
        self.dt_all = self.sb("dt_all", [P, TILES, HEADS])
        self.e_i = self.sb("e_i", [P, E], I32)
        self.e_num = self.sb("e_num", [P, E])
        self.e_row = self.sb("e_row", [P, E])
        self.seen = self.sb("seen", [P, NT + 1, E])
        self.pos_i = self.sb("pos_i", [P, TILES], U32)
        self.pos_y = self.sb("pos_y", [P, TILES], U32)
        self.which_i = self.sb("which_i", [P, ETILES], I32)
        self.row_i = self.sb("row_i", [P, ETILES], I32)

    def sb(self, name, shape, dt=FP32, ctx=None):
        return (ctx or self.ctx).enter_context(self.nc.sbuf_tensor(name, shape, dt))

    def sem(self, name, ctx=None):
        return (ctx or self.ctx).enter_context(self.nc.semaphore(name))


def row(vector):
    return vector.unsqueeze(0).to_broadcast([P, vector.shape[0]])


def constants(core):
    nc, c = core.nc, core
    with ExitStack() as ctx:
        filled = core.sem("filled", ctx)
        made = core.sem("made", ctx)
        numbered = core.sem("numbered", ctx)
        block = ctx.enter_context(nc.Block())

        @block.vector
        def _(dve):
            nc.vector.memset(c.seen[:], 0.0)
            dve.wait_ge(numbered, 1)
            nc.vector.tensor_copy(c.e_num[:], c.e_i[:]).then_inc(made, 1)
            dve.wait_ge(made, 1)
            nc.vector.tensor_scalar(c.e_row[:], c.e_num[:], float(REGION), None, ALU.mult)

        @block.gpsimd
        def _(pool):
            nc.gpsimd.iota(c.e_i[:], pattern=[[1, E]], base=0, channel_multiplier=0).then_inc(numbered, 1)
            nc.gpsimd.memset(c.ident[:], 0.0)
            nc.gpsimd.memset(c.upper[:], 1.0)
            nc.gpsimd.memset(c.strict[:], 1.0)
            nc.gpsimd.memset(c.ones[:], 1.0)
            nc.gpsimd.memset(c.neg_half[:], -0.5).then_inc(filled, 1)
            pool.wait_ge(filled, 1)
            nc.gpsimd.affine_select(out=c.ident[:], in_=c.ident[:], compare_op=ALU.not_equal, fill=1.0,
                                    base=0, pattern=[[-1, P]], channel_multiplier=1)
            nc.gpsimd.affine_select(out=c.upper[:], in_=c.upper[:], compare_op=ALU.is_ge, fill=0.0,
                                    base=0, pattern=[[1, P]], channel_multiplier=-1)
            nc.gpsimd.affine_select(out=c.strict[:], in_=c.strict[:], compare_op=ALU.is_ge, fill=0.0,
                                    base=-1, pattern=[[-1, P]], channel_multiplier=1)


def project(core):
    nc, c, d = core.nc, core, core.i
    with ExitStack() as ctx:
        sb = lambda name, shape, dt=FP32: core.sb(name, shape, dt, ctx)
        sem = lambda name: core.sem(name, ctx)
        x = sb("x", [P, 2, NT, D])
        xn = sb("xn", [P, 2, NT, D])
        nx = sb("nx", [P, 2, NT, D])
        xnT = sb("xnT", [P, KD, T])
        nxT = sb("nxT", [P, 2, KD, T])
        wq, wk, wv = (sb(n, [P, KD, D]) for n in ("wq", "wk", "wv"))
        wdt = sb("wdt", [P, KD, HEADS])
        bq, bk, g_ln = (sb(n, [P, KD]) for n in ("bq", "bk", "g_ln"))
        bv = sb("bv", [P, D])
        full = sb("qk_full", [P, 4, T])
        rest = sb("qk_rest", [P, 4, T])
        parts = sb("qk_parts_sb", [P, 4, PARTS, T], BF16)
        v = sb("v_padded", [P, NT, H, 2 * HD])
        stats = sb("stats", [P, 2, NT, 6])
        mv = sb("mv", [P, 2, NT, 2])
        ve = sb("ve", [P, 2, NT])
        rstd = sb("rstd", [P, 2, NT])

        w_in = sem("w_in")
        x_in = [sem("x_in0"), sem("x_in1")]
        ln_var = sem("ln_var")
        ln_rstd = sem("ln_rstd")
        xn_ready = sem("xn_ready")
        nx_ready = sem("nx_ready")
        xn_out = [sem("xn_out0"), sem("xn_out1")]
        t_ready = sem("t_ready")
        t_taken = sem("t_taken")
        tn_taken = sem("tn_taken")
        nxT_out = [sem("nxT_out0"), sem("nxT_out1")]
        qk_ready = sem("qk_ready")
        full_ready = sem("full_ready")
        rest_ready = sem("rest_ready")
        mid_ready = sem("mid_ready")
        low_ready = sem("low_ready")
        parts_out = [sem(f"parts_out{j}") for j in range(4)]
        v_ready = sem("v_ready")
        v_taken = sem("v_taken")
        v_out = sem("v_out")
        dt_ready = sem("dt_ready")
        dt_taken = sem("dt_taken")
        dve_step = sem("dve_step")
        block = ctx.enter_context(nc.Block())
        x_tiles = d["L0_attn_input_tensor"].rearrange("b (t p) d -> b p t d", p=P)
        xn_tiles = c.xn_dram.rearrange("(b t p) d -> b p t d", t=NT, p=P)
        v_tiles = c.v_dram.rearrange("(b t p) e -> b p t e", t=NT, p=P)
        dv = d["L0_attn_W_in"]
        WEIGHTS = 9 * 16

        @block.sync
        def _(sp):
            sp.dma_start(x[:, 0], x_tiles[0]).then_inc(x_in[0], 16)
            sp.dma_start(x[:, 1], x_tiles[1]).then_inc(x_in[1], 16)
            for dst, src in ((wq, "Wq"), (wk, "Wk"), (wv, "Wv")):
                sp.dma_start(dst[:], d["L0_ffn_" + src].rearrange("(k p) n -> p k n", p=P)).then_inc(w_in, 16)
            with nc.allow_non_contiguous_dma(reason="small vectors"):
                sp.dma_start(wdt[:], dv[:, PROJ - HEADS:PROJ].rearrange("(k p) n -> p k n", p=P)).then_inc(w_in, 16)
                sp.dma_start(bq[:], d["L0_ffn_bq"].rearrange("(k p) -> p k", p=P)).then_inc(w_in, 16)
                sp.dma_start(bk[:], d["L0_ffn_bk"].rearrange("(k p) -> p k", p=P)).then_inc(w_in, 16)
                sp.dma_start(g_ln[:], d["L0_attn_ln_gamma"].rearrange("(k p) -> p k", p=P)).then_inc(w_in, 16)
            sp.dma_start(bv[:], row(d["L0_ffn_bv"])).then_inc(w_in, 16)

            def batch(b, i, p):
                sp.wait_ge(xn_ready, b + 1)
                sp.dma_start(xn_tiles[b], xn[:, p]).then_inc(xn_out[p], 16)
                if not isinstance(b, int) or b + 2 < B:
                    sp.dma_start(x[:, p], x_tiles[b + 2]).then_inc(x_in[p], 16)
                sp.wait_ge(tn_taken, 2 * b + 2)
                sp.dma_start(c.nxT_dram[:, :, bass.ts(b, T)].rearrange("k p t -> p k t"),
                             nxT[:, p]).then_inc(nxT_out[p], 16)
                for j in range(4):
                    sp.wait_ge(low_ready, 4 * b + j + 1)
                    sp.dma_start(c.parts_dram[j % 2, b, j // 2].rearrange("a p t -> p a t"),
                                 parts[:, j]).then_inc(parts_out[j], 16)
                sp.wait_ge(v_taken, 2 * b + 2)
                sp.dma_start(v_tiles[b], v[:].rearrange("p t h e -> p t (h e)")).then_inc(v_out, 16)

            batch(0, 0, 0)
            with sp.Fori(0, B // 2 - 2) as i:
                batch(2 * i + 1, i, 1)
                batch(2 * i + 2, i + 1, 0)
            batch(B - 3, B // 2 - 2, 1)
            for p in range(2):
                batch(B - 2 + p, B // 2 - 1, p)
            for p in range(2):
                sp.wait_ge(xn_out[p], 16 * B // 2)
                sp.wait_ge(nxT_out[p], 16 * B // 2)
            for j in range(4):
                sp.wait_ge(parts_out[j], 16 * B)
            sp.wait_ge(v_out, 16 * B)

        @block.vector
        def _(dve):
            nc.vector.memset(v[:, :, :, HD:2 * HD], 1.0)
            dve.wait_ge(w_in, WEIGHTS - 16)
            STEPS = 6
            for k in range(KD):
                ins = nc.vector.tensor_scalar(wdt[:, k], wdt[:, k], g_ln[:, k:k + 1], None, ALU.mult)
            ins.then_inc(w_in, 16)

            def batch(b, i, p):
                step = Steps(dve, dve_step, STEPS * b)
                dve.wait_ge(x_in[p], 16 * (i + 1))
                for half, (src, dst) in enumerate(((x, xn), (xn, nx))):
                    for t in range(NT):
                        ins = nc.vector.bn_stats(stats[:, half, t], src[:, p, t])
                    step.then(ins, core)
                    for t in range(NT):
                        ins = nc.vector.bn_aggr(mv[:, half, t], stats[:, half, t])
                    step.then(ins)
                    nc.vector.tensor_scalar(ve[:, half], mv[:, half, :, 1], EPS, None, ALU.add).then_inc(ln_var, 1)
                    dve.wait_ge(ln_rstd, 2 * b + half + 1)
                    if half == 0:
                        wait(dve, xn_out[p], 16 * i)
                    else:
                        wait(dve, t_ready, 4 * b - 4)
                    for t in range(NT):
                        ins = nc.vector.tensor_scalar(dst[:, p, t], src[:, p, t], mv[:, half, t, 0:1],
                                                      rstd[:, half, t:t + 1], ALU.subtract, ALU.mult)
                    step.then(ins)
                    nc.vector.tensor_copy(ve[:, half, 0:1], ve[:, half, 0:1]).then_inc(xn_ready if half == 0 else nx_ready, 1)

            def rests(b):
                for j in range(4):
                    dve.wait_ge(full_ready, 4 * b + j + 1)
                    wait(dve, parts_out[j], 16 * b)
                    nc.vector.tensor_copy(parts[:, j, 0], full[:, j]).then_inc(rest_ready, 1)
                    dve.wait_ge(rest_ready, 8 * b + 2 * j + 1)
                    nc.vector.tensor_tensor(rest[:, j], full[:, j], parts[:, j, 0], ALU.subtract).then_inc(rest_ready, 1)
                    dve.wait_ge(rest_ready, 8 * b + 2 * j + 2)
                    nc.vector.tensor_copy(parts[:, j, 1], rest[:, j]).then_inc(mid_ready, 1)
                for half in range(2):
                    dve.wait_ge(v_ready, 2 * b + half + 1)
                    if half == 0:
                        wait(dve, v_out, 16 * b)
                    nc.vector.tensor_tensor(
                        v[:, 2 * half:2 * half + 2, :, 0:HD],
                        c.bank[6 + half][:].rearrange("p (t h e) -> p t h e", t=2, h=H),
                        bv[:].rearrange("p (h e) -> p h e", h=H).unsqueeze(1).to_broadcast([P, 2, H, HD]),
                        ALU.add).then_inc(v_taken, 1)

            batch(0, 0, 0)
            with dve.Fori(0, B // 2 - 1) as i:
                batch(2 * i + 1, i, 1)
                rests(2 * i)
                batch(2 * i + 2, i + 1, 0)
                rests(2 * i + 1)
            batch(B - 1, B // 2 - 1, 1)
            rests(B - 2)
            rests(B - 1)

        @block.gpsimd
        def _(pool):
            def powers(b):
                for half in range(2):
                    pool.wait_ge(ln_var, 2 * b + half + 1)
                    nc.gpsimd.tensor_tensor(rstd[:, half], ve[:, half], c.neg_half[:, 0:NT], ALU.pow).then_inc(ln_rstd, 1)

            def lows(b):
                for j in range(4):
                    pool.wait_ge(mid_ready, 4 * b + j + 1)
                    nc.gpsimd.tensor_tensor(parts[:, j, 2], rest[:, j], parts[:, j, 1], ALU.subtract).then_inc(low_ready, 1)

            powers(0)
            with pool.Fori(0, B - 1) as b:
                powers(b + 1)
                lows(b)
            lows(B - 1)

        @block.tensor
        def _(pe):
            pe.wait_ge(w_in, WEIGHTS)

            def batch(b, p):
                for n, src in enumerate((xn, nx)):
                    pe.wait_ge((xn_ready, nx_ready)[n], b + 1)
                    for k in range(KD):
                        if n == 0:
                            wait(pe, dt_taken, b)
                        else:
                            pe.wait_ge(t_taken, 2 * b + 1 + k)
                        for t in range(NT):
                            ins = nc.tensor.transpose(c.bank[k][:, bass.ts(t, P)], src[:, p, t, bass.ts(k, P)], c.ident[:])
                        ins.then_inc(t_ready, 1)
                pe.wait_ge(t_taken, 2 * b + 2)
                for j in range(4):
                    w = (wq, wk)[j % 2]
                    wait(pe, full_ready, 4 * b - 3 + j)
                    for k in range(KD):
                        ins = nc.tensor.matmul(c.bank[2 + j][:], w[:, k, bass.ts(j // 2, P)], xnT[:, k],
                                               start=k == 0, stop=k == KD - 1)
                    ins.then_inc(qk_ready, 1)
                for half in range(2):
                    wait(pe, v_taken, 2 * b - 1 + half)
                    for t in (2 * half, 2 * half + 1):
                        for k in range(KD):
                            ins = nc.tensor.matmul(c.bank[6 + half][:, bass.ts(t % 2, D)], xnT[:, k, bass.ts(t, P)],
                                                   wv[:, k], start=k == 0, stop=k == KD - 1)
                    ins.then_inc(v_ready, 1)
                pe.wait_ge(tn_taken, 2 * b + 2)
                for t in range(NT):
                    for k in range(KD):
                        ins = nc.tensor.matmul(c.bank[0][:, bass.ts(t, HEADS)], nxT[:, p, k, bass.ts(t, P)],
                                               wdt[:, k], start=k == 0, stop=k == KD - 1)
                ins.then_inc(dt_ready, 1)

            batch(0, 0)
            with pe.Fori(0, B // 2 - 1) as i:
                batch(2 * i + 1, 1)
                batch(2 * i + 2, 0)
            batch(B - 1, 1)

        @block.scalar
        def _(act):
            act.wait_ge(w_in, WEIGHTS)

            def batch(b, i, p):
                for n in range(2):
                    for k in range(KD):
                        act.wait_ge(t_ready, 4 * b + 2 * n + k + 1)
                        if n == 0:
                            if k == 0:
                                wait(act, v_ready, 2 * b)
                            nc.scalar.copy(xnT[:, k], c.bank[k][:]).then_inc(t_taken, 1)
                        else:
                            if k == 0:
                                wait(act, nxT_out[p], 16 * i)
                                wait(act, dt_ready, b - 1)
                            nc.scalar.copy(nxT[:, p, k], c.bank[k][:]).then_inc(tn_taken, 1)
                for j in range(4):
                    act.wait_ge(qk_ready, 4 * b + j + 1)
                    wait(act, rest_ready, 8 * b - 6 + 2 * j)
                    nc.scalar.activation(full[:, j], c.bank[2 + j][:], ACT.Identity,
                                         bias=(bq, bk)[j % 2][:, j // 2:j // 2 + 1]).then_inc(full_ready, 1)
                act.wait_ge(dt_ready, b + 1)
                nc.scalar.copy(c.dt_all[:, bass.ts(b, NT)], c.bank[0][:, 0:NT * HEADS].rearrange("p (t h) -> p t h", t=NT)).then_inc(dt_taken, 1)

            batch(0, 0, 0)
            with act.Fori(0, B // 2 - 1) as i:
                batch(2 * i + 1, i, 1)
                batch(2 * i + 2, i + 1, 0)
            batch(B - 1, B // 2 - 1, 1)


JOBS = {1: ["OT3-"], 3: ["aT0-"], 4: ["aT1-", "neg1"], 5: ["OT0"], 7: ["Wo0-"], 8: ["Wo1-"], 9: ["OT1"],
        12: ["neg0+"], 13: ["OT2"], 15: ["cnt-"]}
JOBS_B = sum(len(j) for j in JOBS.values())
STEPS_B = 16


class Jobs:

    def __init__(self, b, first=False, last=False, tail=False):
        kept = [(s, j) for s, js in JOBS.items() for j in js
                if not (first and j[-1] == "-") and not (last and j[-1] == "+") and not (tail and j[-1] != "-")]
        start = 1 if first else JOBS_B * (b - 1) + 6
        if tail:
            start = JOBS_B * (B - 1) + 5
        self.of = {s: [(j, start + n) for n, (s2, j) in enumerate(kept) if s2 == s] for s in range(STEPS_B)}


def attend(core):
    nc, c, d = core.nc, core, core.i
    with ExitStack() as ctx:
        sb = lambda name, shape, dt=FP32: core.sb(name, shape, dt, ctx)
        sem = lambda name: core.sem(name, ctx)
        qs = sb("q_stack", [P, 4, UH, T], BF16)
        ks = sb("k_stack", [P, 4, UH, T], BF16)
        v = sb("v_tiles", [P, 2, NT, H * 2 * HD])
        probs = sb("probs", [P, 2, 4, T])
        nmax = sb("nmax", [P, 2, UH * NT])
        nrow = sb("nrow", [UH * NT, P])
        nrest = sb("nrest", [UH * NT, P])
        nparts = sb("nparts", [UH * NT, PARTS, P], BF16)
        oT = sb("oT", [P, 2, T])
        rsum = sb("rsum", [P, NT, 4])
        attn = sb("attn", [P, NT, D])
        aT = sb("aT", [P, KD, T])
        wo = sb("wo", [P, KD, D])
        bo, g1, b1, rw = (sb(n, [P, D]) for n in ("bo", "g1", "b1", "rw"))
        rb = sb("rb", [P, 1])
        xnb = sb("xnb", [P, 2, NT, D])
        res = sb("res", [P, NT, D])
        norm = sb("norm", [P, NT, D])
        x1 = sb("x1", [P, NT, D])
        stats = sb("stats1", [P, NT, 6])
        mv = sb("mv1", [P, NT, 2])
        ve = sb("ve1", [P, NT])
        rstd = sb("rstd1", [P, NT])
        kt = sb("kt", [P, NT])
        keys, fl, above, pos = (sb(n, [P, NT]) for n in ("keys", "fl", "above", "pos"))
        whole = sb("whole", [P, NT], I32)
        hot = sb("hot", [P, NT, E])
        at = sb("at", [P, NT, E])
        idx = sb("idx", [P, NT], U32)
        junk = sb("junk", [1, 2])
        product = sb("product", [P, NT, D])

        w_in = sem("w_in1")
        set_up = sem("set_up")
        stack_in = [sem(f"stack_in{n}") for n in range(4)]
        v_in = [sem(f"v_in{n}") for n in range(2)]
        xn_in = [sem(f"xn_in{n}") for n in range(2)]
        rows_in = [sem(f"rows_in{n}") for n in range(2)]
        s1_ready = sem("s1_ready")
        max_done = sem("max_done")
        s2_ready = sem("s2_ready")
        exp_done = sem("exp_done")
        pv_done = sem("pv_done")
        oT_ready = sem("oT_ready")
        job_ready = sem("job_ready")
        job_taken = sem("job_taken")
        group_done = sem("group_done")
        aT_ready = sem("aT_ready")
        nrow_ready = sem("nrow_ready")
        pool_step = sem("pool_step1")
        rows_made = sem("rows_made")
        rows_out = sem("rows_out")
        xnb_ready = sem("xnb_ready")
        res_done = sem("res_done")
        ve_ready = sem("ve_ready")
        rstd_ready = sem("rstd_ready")
        norm_ready = sem("norm_ready")
        x1_ready = sem("x1_ready")
        hot_ready = sem("hot_ready")
        pos_ready = sem("pos_ready")
        idx_done = sem("idx_done")
        scattered = sem("scattered")
        recip_done = sem("recip_done")
        dve_step = sem("dve_step1")
        block = ctx.enter_context(nc.Block())
        xn_tiles = c.xn_dram.rearrange("(b t p) d -> b p t d", t=NT, p=P)
        v_tiles = c.v_dram.rearrange("(b t p) e -> b p t e", t=NT, p=P)
        LOADS = 2 * len(PAIRS_Q) * 16

        @block.sync
        def _(sp):
            def stack(b, hf, p):
                for dst, pairs, n in ((qs, PAIRS_Q, 0), (ks, PAIRS_K, 1)):
                    for r, part in enumerate(pairs):
                        sp.dma_start(dst[HD * r:HD * r + HD, 2 * p + hf],
                                     c.parts_dram[n, b, hf, part].rearrange("(h e) t -> e h t", e=HD)
                                     ).then_inc(stack_in[2 * p + hf], 16)

            def rest(b, p):
                sp.dma_start(v[:, p], v_tiles[b]).then_inc(v_in[p], 16)
                sp.dma_start(xnb[:, p], xn_tiles[b]).then_inc(xn_in[p], 16)

            stack(0, 0, 0)
            sp.dma_start(wo[:], d["L0_ffn_Wo"].rearrange("(k p) n -> p k n", p=P)).then_inc(w_in, 16)
            for dst, name in ((bo, "bo"), (g1, "ln1_g"), (b1, "ln1_b")):
                sp.dma_start(dst[:], row(d["L0_ffn_" + name])).then_inc(w_in, 16)
            sp.dma_start(rw[:], row(d["L0_ffn_router_w"].rearrange("d o -> (d o)"))).then_inc(w_in, 16)
            with nc.allow_non_contiguous_dma(reason="one number"):
                sp.dma_start(rb[:], row(d["L0_ffn_router_b"])).then_inc(w_in, 16)
            stack(0, 1, 0)
            rest(0, 0)

            def body(b, p):
                wait(sp, s2_ready, 32 * b - 16)
                stack(b + 1, 0, 1 - p)
                wait(sp, s2_ready, 32 * b)
                stack(b + 1, 1, 1 - p)
                wait(sp, res_done, 2 * b)
                rest(b + 1, 1 - p)

            body(0, 0)
            with sp.Fori(0, (B - 2) // 2) as i:
                body(2 * i + 1, 1)
                body(2 * i + 2, 0)

        @block.tensor
        def _(pe):
            pe.wait_ge(w_in, 6 * 16)

            def s1(b, hf, p, q, head):
                n = (2 * b + hf) * UH * NT + head * NT
                if head == 0:
                    pe.wait_ge(stack_in[2 * p + hf], LOADS * (q + 1))
                for t in range(NT):
                    wait(pe, max_done, n + t - 1)
                    nc.tensor.matmul(c.bank[t % 2], qs[0:KS, 2 * p + hf, head, bass.ts(t, P)],
                                     ks[0:KS, 2 * p + hf, head], start=True, stop=True).then_inc(s1_ready, 1)

            def s2(b, p, s):
                hf, g, k = s // 8, s // 4 % 2, s % 4
                if s % 8 == 0:
                    pe.wait_ge(rows_in[hf], 16 * (b + 1))
                    pe.wait_ge(set_up, 2)
                for pair in range(2):
                    wait(pe, exp_done, 2 * (16 * b + s) + pair - 1)
                    for j in (2 * pair, 2 * pair + 1):
                        ins = nc.tensor.matmul(c.bank[2 + j], ks[0:KM, 2 * p + hf, 4 * g + j, bass.ts(k, P)],
                                               qs[0:KM, 2 * p + hf, 4 * g + j], start=True, stop=True)
                    ins.then_inc(s2_ready, 1)

            def pv(b, p, q, s):
                k = s % 4
                pe.wait_ge(exp_done, 2 * (16 * b + s) + 2)
                if s == 0:
                    pe.wait_ge(v_in[p], 16 * (q + 1))
                if k == 0:
                    wait(pe, oT_ready, 4 * b + s // 4)
                for j in range(4):
                    ins = nc.tensor.matmul(c.bank[6][32 * j:32 * j + 32], v[:, p, k, bass.ts(s // 4 * 4 + j, 32)],
                                           probs[:, s % 2, j], start=k == 0, stop=k == 3)
                ins.then_inc(pv_done, 1)

            def job(name, n, b):
                wait(pe, job_taken, n)
                if name[:2] == "OT":
                    g = 4 * b + int(name[2]) - (4 if name[-1] == "-" else 0)
                    pe.wait_ge(oT_ready, g + 1)
                    for t in range(NT):
                        ins = nc.tensor.transpose(c.bank[7][:, bass.ts(t, P)], oT[:, int(name[2]) % 2, bass.ts(t, P)], c.ident[:])
                elif name[:2] == "aT":
                    k = int(name[2])
                    pe.wait_ge(group_done, 4 * b)
                    for t in range(NT):
                        ins = nc.tensor.transpose(c.bank[7][:, bass.ts(t, P)], attn[:, t, bass.ts(k, P)], c.ident[:])
                elif name[:2] == "Wo":
                    half = int(name[2])
                    pe.wait_ge(aT_ready, 2 * b)
                    for t in (2 * half, 2 * half + 1):
                        for k in range(KD):
                            ins = nc.tensor.matmul(c.bank[7][:, bass.ts(t % 2, D)], aT[:, k, bass.ts(t, P)], wo[:, k],
                                                   start=k == 0, stop=k == KD - 1)
                elif name == "cnt-":
                    pe.wait_ge(hot_ready, b)
                    rows = c.bank[7][:, 0:NT * E]
                    nc.tensor.matmul(rows, c.upper[:], hot[:].rearrange("p t e -> p (t e)"), start=True, stop=False)
                    ins = nc.tensor.matmul(rows, c.ones[:], c.seen[:, 0:NT].rearrange("p t e -> p (t e)"), start=False, stop=True)
                else:
                    hf = int(name[3])
                    u = 2 * b + 1 if hf else 2 * b + 2
                    pe.wait_ge(max_done, UH * NT * (u + 1))
                    ins = nc.tensor.transpose(c.bank[7][0:UH * NT, 0:P], nmax[:, hf], c.ident[:])
                ins.then_inc(job_ready, 1)

            for head in range(UH):
                s1(0, 0, 0, 0, head)
            job("neg0+", 0, -1)
            for head in range(4):
                s1(0, 1, 0, 0, head)

            def body(b, p, q, first=False, last=False):
                jobs = Jobs(b, first, last)
                for s in range(STEPS_B):
                    s2(b, p, s)
                    if s < 4:
                        s1(b, 1, p, q, 4 + s)
                    elif not last:
                        w = s - 4
                        s1(b + 1, w // UH, 1 - p, q + p, w % UH)
                    if s == 0 and not first:
                        pv(b - 1, 1 - p, q - (1 - p), STEPS_B - 1)
                    elif s > 0:
                        pv(b, p, q, s - 1)
                    for name, n in jobs.of[s]:
                        job(name, n, b)

            body(0, 0, 0, first=True)
            with pe.Fori(0, (B - 2) // 2) as i:
                body(2 * i + 1, 1, i)
                body(2 * i + 2, 0, i + 1)
            body(B - 1, 1, B // 2 - 1, last=True)
            pv(B - 1, 1, B // 2 - 1, STEPS_B - 1)
            jobs = Jobs(B, tail=True)
            for s in range(STEPS_B):
                for name, n in jobs.of[s]:
                    job(name, n, B)

        @block.scalar
        def _(act):
            def job(name, n, b):
                if name[:2] in ("OT", "Wo", "cn"):
                    return
                act.wait_ge(job_ready, n + 1)
                if name[:2] == "aT":
                    nc.scalar.copy(aT[:, int(name[2])], c.bank[7][:]).then_inc(job_taken, 1)
                    act.wait_ge(job_taken, n + 1)
                    nc.scalar.copy(junk[0:1, 0:1], junk[0:1, 0:1]).then_inc(aT_ready, 1)
                else:
                    u = 2 * b + 1 if name[3] == "1" else 2 * b + 2
                    wait(act, rows_made, u)
                    nc.scalar.copy(nrow[:], c.bank[7][0:UH * NT, 0:P]).then_inc(job_taken, 1)

            def out_copy(g, half):
                act.wait_ge(pv_done, 4 * (g + 1))
                wait(act, group_done, g - 1)
                nc.scalar.copy(oT[:, half], c.bank[6][:]).then_inc(oT_ready, 1)

            act.wait_ge(set_up, 2)
            job("neg0+", 0, -1)

            def body(b, first=False, last=False):
                jobs = Jobs(b, first, last)
                for s in range(STEPS_B):
                    wait(act, pv_done, 16 * b + s - 1)
                    for pair in range(2):
                        act.wait_ge(s2_ready, 2 * (16 * b + s) + pair + 1)
                        nc.scalar.activation(probs[:, s % 2, 2 * pair:2 * pair + 2], c.psum[:, 2 + 2 * pair:4 + 2 * pair],
                                             ACT.Exp, scale=SCALE).then_inc(exp_done, 1)
                    if s % 4 == 0 and not (first and s == 0):
                        out_copy(4 * b + s // 4 - 1, (s // 4 - 1) % 2)
                    for name, n in jobs.of[s]:
                        job(name, n, b)

            body(0, first=True)
            with act.Fori(0, (B - 2) // 2) as i:
                body(2 * i + 1)
                body(2 * i + 2)
            body(B - 1, last=True)
            out_copy(4 * B - 1, 1)
            jobs = Jobs(B, tail=True)
            for s in range(STEPS_B):
                for name, n in jobs.of[s]:
                    job(name, n, B)

        @block.vector
        def _(dve):
            nc.vector.memset(junk[:], 0.0).then_inc(set_up, 1)
            dve.wait_ge(w_in, 6 * 16)

            def maxima(b, hf, head):
                n = (2 * b + hf) * UH * NT + head * NT
                for t in range(NT):
                    dve.wait_ge(s1_ready, n + t + 1)
                    nc.vector.tensor_reduce(nmax[:, hf, head * NT + t:head * NT + t + 1], c.bank[t % 2], axis=AX.X,
                                            op=ALU.max, negate=True).then_inc(max_done, 1)

            def group(name, n, b):
                g = int(name[2])
                dve.wait_ge(job_ready, n + 1)
                o = c.bank[7].rearrange("p (t j e) -> p t j e", t=NT, j=4)
                nc.vector.reciprocal(rsum[:], o[:, :, :, HD]).then_inc(recip_done, 1)
                dve.wait_ge(recip_done, 4 * b + g + 1 - (4 if name[-1] == "-" else 0))
                nc.vector.tensor_tensor(
                    attn[:, :, bass.ts(g, 4 * HD)].rearrange("p t (j e) -> p t j e", j=4),
                    o[:, :, :, 0:HD], rsum[:].unsqueeze(3).to_broadcast([P, NT, 4, HD]), ALU.mult).then_inc(job_taken, 1)
                dve.wait_ge(job_taken, n + 1)
                nc.vector.tensor_copy(junk[0:1, 0:1], junk[0:1, 0:1]).then_inc(group_done, 1)

            def job(name, n, b, p):
                if name[:2] == "OT":
                    group(name, n, b)
                elif name[:2] == "Wo":
                    half = int(name[2])
                    dve.wait_ge(job_ready, n + 1)
                    dve.wait_ge(xnb_ready, b)
                    nc.vector.tensor_tensor(res[:, 2 * half:2 * half + 2], c.bank[7].rearrange("p (t e) -> p t e", t=2),
                                            xnb[:, 1 - p, 2 * half:2 * half + 2], ALU.add).then_inc(job_taken, 1)
                    dve.wait_ge(job_taken, n + 1)
                    nc.vector.tensor_copy(junk[0:1, 0:1], junk[0:1, 0:1]).then_inc(res_done, 1)
                elif name == "cnt-":
                    step = Steps(dve, dve_step, CHAIN * b - 4)
                    dve.wait_ge(job_ready, n + 1)
                    nc.vector.tensor_tensor(at[:], c.bank[7][:, 0:NT * E].rearrange("p (t e) -> p t e", t=NT),
                                            c.e_row[:].unsqueeze(1).to_broadcast([P, NT, E]), ALU.add).then_inc(job_taken, 1)
                    dve.wait_ge(job_taken, n + 1)
                    step.then(nc.vector.tensor_tensor(at[:], at[:], hot[:], ALU.mult))
                    step.then(nc.vector.tensor_reduce(pos[:], at[:], axis=AX.X, op=ALU.add))
                    step.then(nc.vector.tensor_scalar(pos[:], pos[:], -1.0, None, ALU.add))
                    nc.vector.tensor_copy(c.pos_i[:, bass.ds(NT * b - NT, NT)], pos[:]).then_inc(pos_ready, 1)
                    step.then(nc.vector.tensor_copy(c.seen[:, 0], c.seen[:, NT]))

            def finish(b, s):
                step = Steps(dve, dve_step, CHAIN * b)
                if s == 9:
                    dve.wait_ge(res_done, 2 * b + 2)
                    for t in range(NT):
                        ins = nc.vector.bn_stats(stats[:, t], res[:, t])
                    step.then(ins, core)
                    for t in range(NT):
                        ins = nc.vector.bn_aggr(mv[:, t], stats[:, t])
                    step.then(ins)
                    nc.vector.tensor_scalar(ve[:], mv[:, :, 1], EPS, None, ALU.add).then_inc(ve_ready, 1)
                if s == 10:
                    dve.wait_ge(rstd_ready, b + 1)
                    wait(dve, x1_ready, 2 * b)
                    for t in range(NT):
                        ins = nc.vector.tensor_scalar(norm[:, t], res[:, t], mv[:, t, 0:1], rstd[:, t:t + 1],
                                                      ALU.subtract, ALU.mult)
                    ins.then_inc(norm_ready, 1)
                if s == 12:
                    dve.wait_ge(x1_ready, 2 * b + 2)
                    for t in range(NT):
                        ins = nc.vector.tensor_tensor_reduce(out=product[:, t], in0=x1[:, t], in1=rw[:], scale=1.0, scalar=0.0,
                                                             op0=ALU.mult, op1=ALU.add, accum_out=kt[:, t:t + 1])
                    step.at = CHAIN * b + 2
                    step.then(ins)
                    step.then(nc.vector.tensor_scalar(keys[:], kt[:], rb[:], None, ALU.add))
                    step.then(nc.vector.tensor_copy(whole[:], keys[:]))
                    step.then(nc.vector.tensor_copy(fl[:], whole[:]))
                    step.then(nc.vector.tensor_tensor(above[:], fl[:], keys[:], ALU.is_gt))
                    step.then(nc.vector.tensor_tensor(fl[:], fl[:], above[:], ALU.subtract))
                    step.then(nc.vector.tensor_copy(whole[:], fl[:]))
                    step.then(nc.vector.tensor_scalar(whole[:], whole[:], E - 1, None, ALU.bitwise_and))
                    step.then(nc.vector.tensor_copy(fl[:], whole[:]))
                    step.then(nc.vector.tensor_tensor(hot[:], fl[:].unsqueeze(2).to_broadcast([P, NT, E]),
                                                      c.e_num[:].unsqueeze(1).to_broadcast([P, NT, E]), ALU.is_equal))
                    for t in range(NT):
                        step.then(nc.vector.tensor_tensor(c.seen[:, t + 1], c.seen[:, t], hot[:, t], ALU.add))
                    nc.vector.tensor_copy(junk[0:1, 0:1], junk[0:1, 0:1]).then_inc(hot_ready, 1)

            CHAIN = 2 + 10 + NT + 4
            for head in range(UH):
                maxima(0, 0, head)
            for head in range(4):
                maxima(0, 1, head)

            def body(b, p, first=False, last=False):
                jobs = Jobs(b, first, last)
                for s in range(STEPS_B):
                    if s < 4:
                        maxima(b, 1, 4 + s)
                    elif not last:
                        maxima(b + 1, (s - 4) // UH, (s - 4) % UH)
                    for name, n in jobs.of[s]:
                        job(name, n, b, p)
                    if not first:
                        finish(b - 1, s)

            body(0, 0, first=True)
            with dve.Fori(0, (B - 2) // 2) as i:
                body(2 * i + 1, 1)
                body(2 * i + 2, 0)
            body(B - 1, 1, last=True)
            jobs = Jobs(B, tail=True)
            for s in range(STEPS_B):
                for name, n in jobs.of[s]:
                    job(name, n, B, 0)
                finish(B - 1, s)

        @block.gpsimd
        def _(pool):
            nc.gpsimd.memset(ks[KS:KM], 1.0).then_inc(set_up, 1)
            pool.wait_ge(w_in, 6 * 16)

            def rows(u, b, hf, p):
                step = Steps(pool, pool_step, 3 * u)
                ord_ = 0 if isinstance(b, int) and b == 0 and hf == 0 else JOBS_B * (b - 1) + 6 + (3 if hf else 8 - JOBS_B)
                if isinstance(b, int) and b == 0 and hf == 1:
                    ord_ = 1
                if isinstance(b, int) and b == 1 and hf == 0:
                    ord_ = 4
                pool.wait_ge(job_taken, ord_ + 1)
                wait(pool, rows_in[hf], 16 * b)
                step.then(nc.gpsimd.tensor_tensor(nparts[:, 0], nrow[:], c.ones[0:UH * NT], ALU.mult))
                step.then(nc.gpsimd.tensor_tensor(nrest[:], nrow[:], nparts[:, 0], ALU.subtract))
                step.then(nc.gpsimd.tensor_tensor(nparts[:, 1], nrest[:], c.ones[0:UH * NT], ALU.mult))
                nc.gpsimd.tensor_tensor(nparts[:, 2], nrest[:], nparts[:, 1], ALU.subtract).then_inc(rows_made, 1)
                pool.wait_ge(rows_made, u + 1)
                settle(core, nc.gpsimd)
                pool.dma_start(c.rows_dram[hf].rearrange("a r q -> r a q"), nparts[:]).then_inc(rows_out, 16)
                pool.wait_ge(rows_out, 16 * (u + 1))
                settle(core, nc.gpsimd)
                pool.dma_start(qs[KS:KM, 2 * p + hf].rearrange("a h t -> a (h t)"),
                               c.rows_dram[hf].rearrange("a r q -> a (r q)")).then_inc(rows_in[hf], 16)

            def add_bias(b, p, q):
                pool.wait_ge(xn_in[p], 16 * (q + 1))
                nc.gpsimd.tensor_tensor(xnb[:, p], xnb[:, p], bo[:].unsqueeze(1).to_broadcast([P, NT, D]),
                                        ALU.add).then_inc(xnb_ready, 1)

            def finish(b):
                pool.wait_ge(ve_ready, b + 1)
                nc.gpsimd.tensor_tensor(rstd[:], ve[:], c.neg_half[:, 0:NT], ALU.pow).then_inc(rstd_ready, 1)
                pool.wait_ge(norm_ready, b + 1)
                wait(pool, scattered, 16 * NT * b)
                nc.gpsimd.tensor_tensor(x1[:], norm[:], g1[:].unsqueeze(1).to_broadcast([P, NT, D]), ALU.mult).then_inc(x1_ready, 1)
                pool.wait_ge(x1_ready, 2 * b + 1)
                nc.gpsimd.tensor_tensor(x1[:], x1[:], b1[:].unsqueeze(1).to_broadcast([P, NT, D]), ALU.add).then_inc(x1_ready, 1)

            def scatter(b):
                wait(pool, scattered, 16 * NT * b)
                pool.wait_ge(pos_ready, b + 1)
                settle(core, nc.gpsimd)
                nc.gpsimd.tensor_copy(idx[:], c.pos_i[:, bass.ts(b, NT)]).then_inc(idx_done, 1)
                pool.wait_ge(idx_done, b + 1)
                pool.wait_ge(x1_ready, 2 * b + 2)
                settle(core, nc.gpsimd)
                for t in range(NT):
                    pool.indirect_dma_start(c.xg_dram, bass.IndirectOffsetOnAxis(ap=idx[:, t:t + 1], axis=0),
                                            x1[:, t], None).then_inc(scattered, 16)

            rows(0, 0, 0, 0)

            def body(b, p, q, first=False, last=False):
                rows(2 * b + 1, b, 1, p)
                add_bias(b, p, q)
                if not first:
                    finish(b - 1)
                if not last:
                    rows(2 * b + 2, b + 1, 0, 1 - p)
                if not first:
                    scatter(b - 1)

            body(0, 0, 0, first=True)
            with pool.Fori(0, (B - 2) // 2) as i:
                body(2 * i + 1, 1, i)
                body(2 * i + 2, 0, i + 1)
            body(B - 1, 1, B // 2 - 1, last=True)
            finish(B - 1)
            scatter(B - 1)
            pool.wait_ge(scattered, 16 * NT * B)


def tables(core):
    nc, c = core.nc, core
    with ExitStack() as ctx:
        sb = lambda name, shape, dt=FP32: core.sb(name, shape, dt, ctx)
        sem = lambda name: core.sem(name, ctx)
        zeros = sb("zeros", [P, E, D])
        count = sb("count", [P, E])
        end_row = sb("end_row", [P, E])
        end_i = sb("end_i", [P, E], I32)
        caps = sb("caps", [P, E])
        caps_i = sb("caps_i", [P, E], I32)
        skip = sb("skip", [P, E])
        start = sb("start", [P, E])
        first_i = sb("first_i", [P, ETILES], I32)
        first = sb("first", [P, ETILES])
        past = sb("past", [P, E, ETILES])
        which = sb("which", [P, ETILES])
        pos = sb("pos_t", [P, TILES])
        beyond = sb("beyond", [P, E, TILES])
        step_sem = sem("step_t")
        iota_done = sem("iota_done")
        zeroed = sem("zeroed")
        counted = sem("counted")
        end_ready = sem("end_ready")
        tails = sem("tails")
        block = ctx.enter_context(nc.Block())

        @block.gpsimd
        def _(pool):
            nc.gpsimd.iota(first_i[:], pattern=[[P, ETILES]], base=0, channel_multiplier=0).then_inc(iota_done, 1)
            nc.gpsimd.memset(zeros[:], 0.0).then_inc(zeroed, 1)

        @block.tensor
        def _(pe):
            nc.tensor.matmul(c.bank[0][:, 0:E], c.ones[:], c.seen[:, NT], start=True, stop=True).then_inc(counted, 1)

        @block.sync
        def _(sp):
            sp.wait_ge(zeroed, 1)
            sp.wait_ge(end_ready, 1)
            for e in range(E):
                r = sp.value_load(end_i[0:1, e:e + 1], min_val=0, max_val=E * REGION - TAIL)
                sp.dma_start(c.xg_dram[bass.ds(r, TAIL)].rearrange("(t p) d -> p t d", p=P), zeros[:]).then_inc(tails, 16)
            sp.wait_ge(tails, 16 * E)

        @block.vector
        def _(dve):
            v = nc.vector
            step = Steps(dve, step_sem, 0)
            dve.wait_ge(counted, 1)
            step.then(v.tensor_copy(count[:], c.bank[0][:, 0:E]))
            step.then(v.tensor_tensor(end_row[:], count[:], c.e_row[:], ALU.add))
            v.tensor_copy(end_i[:], end_row[:]).then_inc(end_ready, 1)
            step.then(v.tensor_scalar(caps[:], count[:], float(P - 1), None, ALU.add))
            step.then(v.tensor_copy(caps_i[:], caps[:]))
            step.then(v.tensor_scalar(caps_i[:], caps_i[:], -P, None, ALU.bitwise_and))
            step.then(v.tensor_copy(caps[:], caps_i[:]))
            step.then(v.tensor_scalar(skip[:], caps[:], -1.0, float(REGION), ALU.mult, ALU.add))
            step.then(v.memset(start[:], 0.0))
            for e in range(1, E):
                step.then(v.tensor_tensor(start[:, e:e + 1], start[:, e - 1:e], caps[:, e - 1:e], ALU.add))
            dve.wait_ge(iota_done, 1)
            step.then(v.tensor_copy(first[:], first_i[:]))
            for e in range(1, E):
                ins = v.tensor_scalar(past[:, e], first[:], start[:, e:e + 1], None, ALU.is_ge)
            step.then(ins)
            step.then(v.tensor_reduce(which[:], past[:, 1:E].rearrange("p e t -> p t e"), axis=AX.X, op=ALU.add))
            step.then(v.tensor_copy(c.which_i[:], which[:]))
            for e in range(1, E):
                step.then(v.tensor_scalar(past[:, e], past[:, e], skip[:, e - 1:e], None, ALU.mult))
                step.then(v.tensor_tensor(first[:], first[:], past[:, e], ALU.add))
            step.then(v.tensor_copy(c.row_i[:], first[:]))
            step.then(v.tensor_copy(pos[:], c.pos_i[:]))
            for e in range(1, E):
                ins = v.tensor_scalar(beyond[:, e], pos[:], float(e * REGION), skip[:, e - 1:e], ALU.is_ge, ALU.mult)
            step.then(ins)
            for e in range(1, E):
                step.then(v.tensor_tensor(pos[:], pos[:], beyond[:, e], ALU.subtract))
            step.then(v.tensor_copy(c.pos_y[:], pos[:]))


def experts(core):
    nc, c, d = core.nc, core, core.i
    with ExitStack() as ctx:
        sb = lambda name, shape, dt=FP32: core.sb(name, shape, dt, ctx)
        sem = lambda name: core.sem(name, ctx)
        NH, KF = FF // 512, FF // P
        w1 = sb("w1", [P, E, KD, FF])
        w2 = sb("w2", [P, E, KF, D])
        b1 = sb("b1e", [P, E, FF])
        b2 = sb("b2e", [P, E, D])
        g2, be2 = sb("g2", [P, D]), sb("be2", [P, D])
        xg = sb("xg", [P, 4, D])
        xgT = sb("xgT", [P, 2, KD, P])
        h = sb("h", [P, FF])
        hT = sb("hT", [P, KF, P])
        res = sb("res_e", [P, D])
        sum_ = sb("sum_e", [P, D])
        stats, mv = sb("stats_e", [P, 6]), sb("mv_e", [P, 2])
        ve, rstd = sb("ve_e", [P, 1]), sb("rstd_e", [P, 1])
        norm = sb("norm_e", [P, 2, D])
        y = sb("y_e", [P, 2, D])
        w_in = sem("w_in_e")
        xg_in = [sem(f"xg_in{n}") for n in range(4)]
        x_t, x_tk = sem("x_t"), sem("x_tk")
        h_mm, h_sb = sem("h_mm"), sem("h_sb")
        h_t, h_tk = sem("h_t"), sem("h_tk")
        y_mm, y_tk = sem("y_mm"), sem("y_tk")
        dve_step = sem("step_e")
        ve_r, rstd_r, norm_r, y_r = sem("ve_r"), sem("rstd_r"), sem("norm_r"), sem("y_r")
        y_out = [sem("y_out0"), sem("y_out1")]
        block = ctx.enter_context(nc.Block())
        yg_t = c.yg_dram.rearrange("(i p) d -> i p d", p=P)
        UN = 4

        def loop(eng, body):
            for i in range(UN):
                body(i, i, 0)
            with eng.Fori(1, (ETILES - 3) // UN) as j:
                for n in range(UN):
                    body(UN * j + n, n, j)
            for i in range((ETILES - 3) // UN * UN, ETILES):
                body(i, i % UN, i // UN)

        @block.sync
        def _(sp):
            def first_row(i):
                return sp.value_load(c.row_i[0:1, bass.ds(i, 1)], min_val=0, max_val=E * REGION - P)

            def load(r, n):
                sp.dma_start(xg[:, n], c.xg_dram[bass.ds(r, P)]).then_inc(xg_in[n], 16)

            for i in range(3):
                load(first_row(i), i)
            for e in range(E):
                sp.dma_start(w1[:, e], d["L0_ffn_W1"][e].rearrange("(k p) n -> p k n", p=P)).then_inc(w_in, 16)
                sp.dma_start(w2[:, e], d["L0_ffn_W2"][e].rearrange("(k p) n -> p k n", p=P)).then_inc(w_in, 16)
                sp.dma_start(b1[:, e], row(d["L0_ffn_b1"][e])).then_inc(w_in, 16)
                sp.dma_start(b2[:, e], row(d["L0_ffn_b2"][e])).then_inc(w_in, 16)
            sp.dma_start(g2[:], row(d["L0_ffn_ln2_g"])).then_inc(w_in, 16)
            sp.dma_start(be2[:], row(d["L0_ffn_ln2_b"])).then_inc(w_in, 16)

            def body(i, n, j):
                more = not isinstance(i, int) or i + 3 < ETILES
                if more:
                    r_in = first_row(i + 3)
                    wait(sp, dve_step, 4 * i - 3)
                    load(r_in, (n + 3) % UN)
                sp.wait_ge(y_r, 2 * i + 2)
                sp.dma_start(yg_t[i], y[:, n % 2]).then_inc(y_out[n % 2], 16)

            loop(sp, body)
            sp.wait_ge(y_out[0], 16 * ((ETILES + 1) // 2))
            sp.wait_ge(y_out[1], 16 * (ETILES // 2))

        @block.tensor
        def _(pe):
            def x_transposed(i, n, j):
                pe.wait_ge(xg_in[n], 16 * (j + 1))
                wait(pe, x_tk, i)
                for k in range(KD):
                    ins = nc.tensor.transpose(c.bank[0][:, bass.ts(k, P)], xg[:, n, bass.ts(k, P)], c.ident[:])
                ins.then_inc(x_t, 1)

            def up(i, n):
                e = pe.value_load(c.which_i[0:1, bass.ds(i, 1)], min_val=0, max_val=E - 1)
                pe.wait_ge(x_tk, i + 1)
                wait(pe, h_sb, 2 * i)
                for m in range(NH):
                    for k in range(KD):
                        ins = nc.tensor.matmul(c.bank[1 + m], xgT[:, n % 2, k], w1[:, bass.ds(e, 1), k, bass.ts(m, 512)],
                                               start=k == 0, stop=k == KD - 1)
                    ins.then_inc(h_mm, 1)

            def h_transposed(i):
                for m in range(2):
                    pe.wait_ge(h_sb, 2 * i + 1 + m)
                    wait(pe, h_tk, 2 * i - 1 + m)
                    for k in range(4):
                        ins = nc.tensor.transpose(c.bank[3 + m][:, bass.ts(k, P)], h[:, bass.ts(4 * m + k, P)], c.ident[:])
                    ins.then_inc(h_t, 1)

            def down(i):
                e = pe.value_load(c.which_i[0:1, bass.ds(i, 1)], min_val=0, max_val=E - 1)
                pe.wait_ge(h_tk, 2 * i + 2)
                wait(pe, y_tk, i)
                for k in range(KF):
                    ins = nc.tensor.matmul(c.bank[5][:, 0:D], hT[:, k], w2[:, bass.ds(e, 1), k], start=k == 0, stop=k == KF - 1)
                ins.then_inc(y_mm, 1)

            pe.wait_ge(w_in, 16 * 18)
            x_transposed(0, 0, 0)
            up(0, 0)
            x_transposed(1, 1, 0)

            def body(i, n, j):
                h_transposed(i)
                if not isinstance(i, int) or i + 1 < ETILES:
                    up(i + 1, n + 1)
                if not isinstance(i, int) or i + 2 < ETILES:
                    x_transposed(i + 2, (n + 2) % UN, j + (n + 2) // UN)
                down(i)

            loop(pe, body)

        @block.scalar
        def _(act):
            act.wait_ge(w_in, 16 * 18)

            def x_copy(i, n):
                act.wait_ge(x_t, i + 1)
                wait(act, h_mm, 2 * i - 2)
                nc.scalar.copy(xgT[:, n % 2], c.bank[0][:, 0:KD * P].rearrange("p (k q) -> p k q", k=KD)).then_inc(x_tk, 1)

            x_copy(0, 0)

            def body(i, n, j):
                if not isinstance(i, int) or i + 1 < ETILES:
                    x_copy(i + 1, n + 1)
                for m in range(2):
                    act.wait_ge(h_t, 2 * i + 1 + m)
                    wait(act, y_mm, i)
                    nc.scalar.activation(hT[:, 4 * m:4 * m + 4], c.bank[3 + m].rearrange("p (k q) -> p k q", k=4),
                                         ACT.Relu).then_inc(h_tk, 1)

            loop(act, body)

        @block.vector
        def _(dve):
            dve.wait_ge(w_in, 16 * 18)

            def bias(i):
                e = dve.value_load(c.which_i[0:1, bass.ds(i, 1)], min_val=0, max_val=E - 1)
                for m in range(NH):
                    dve.wait_ge(h_mm, 2 * i + 1 + m)
                    wait(dve, h_t, 2 * i - 1 + m)
                    nc.vector.tensor_tensor(h[:, bass.ts(m, 512)].unsqueeze(1), c.bank[1 + m].unsqueeze(1),
                                            b1[:, bass.ds(e, 1), bass.ts(m, 512)], ALU.add).then_inc(h_sb, 1)

            def tail(i, n):
                e = dve.value_load(c.which_i[0:1, bass.ds(i, 1)], min_val=0, max_val=E - 1)
                step = Steps(dve, dve_step, 4 * i)
                dve.wait_ge(y_mm, i + 1)
                nc.vector.tensor_tensor(sum_[:].unsqueeze(1), c.bank[5][:, 0:D].unsqueeze(1), b2[:, bass.ds(e, 1)],
                                        ALU.add).then_inc(y_tk, 1)
                dve.wait_ge(y_tk, i + 1)
                step.then(nc.vector.tensor_tensor(res[:], sum_[:], xg[:, n], ALU.add))
                step.then(nc.vector.bn_stats(stats[:], res[:]), core)
                step.then(nc.vector.bn_aggr(mv[:], stats[:]))
                nc.vector.tensor_scalar(ve[:], mv[:, 1:2], EPS, None, ALU.add).then_inc(ve_r, 1)
                dve.wait_ge(rstd_r, i + 1)
                wait(dve, y_r, 2 * i - 2)
                step.then(nc.vector.tensor_scalar(norm[:, n % 2], res[:], mv[:, 0:1], rstd[:], ALU.subtract, ALU.mult))

            bias(0)

            def body(i, n, j):
                if not isinstance(i, int) or i + 1 < ETILES:
                    bias(i + 1)
                tail(i, n)

            loop(dve, body)

        @block.gpsimd
        def _(pool):
            pool.wait_ge(w_in, 16 * 18)

            def body(i, n, j):
                pool.wait_ge(ve_r, i + 1)
                nc.gpsimd.tensor_tensor(rstd[:], ve[:], c.neg_half[:, 0:1], ALU.pow).then_inc(rstd_r, 1)
                pool.wait_ge(dve_step, 4 * i + 4)
                wait(pool, y_out[n % 2], 16 * (2 * j + n // 2))
                nc.gpsimd.tensor_tensor(y[:, n % 2], norm[:, n % 2], g2[:], ALU.mult).then_inc(y_r, 1)
                pool.wait_ge(y_r, 2 * i + 1)
                nc.gpsimd.tensor_tensor(y[:, n % 2], y[:, n % 2], be2[:], ALU.add).then_inc(y_r, 1)

            loop(pool, body)


def mamba(core):
    nc, c, d = core.nc, core, core.i
    with ExitStack() as ctx:
        sb = lambda name, shape, dt=FP32: core.sb(name, shape, dt, ctx)
        sem = lambda name: core.sem(name, ctx)
        Z0, X0, B0, C0, DT0 = 0, INNER, 2 * INNER, 2 * INNER + STATE, 2 * INNER + 2 * STATE
        win = sb("win", [P, KD, PROJ])
        wc2 = sb("wc2", [P, KD, 2 * STATE])
        wout = sb("wout", [P, JI, D])
        g_ln, be_ln = sb("g_lnm", [P, KD]), sb("be_lnm", [P, KD])
        be_wide = sb("be_wide", [P, KD, P])
        b_row = sb("b_row", [P, INNER + STATE])
        b_in_row = sb("b_in_row", [P, PROJ - INNER])
        dtb = sb("dtb", [P, HEADS])
        dtb_in = sb("dtb_in", [P, HEADS])
        bz, bz_in = sb("bz", [P, JI]), sb("bz_in", [P, JI])
        bB, bB_in = sb("bB", [STATE, 1]), sb("bB_in", [STATE, 1])
        bC, bC_in = sb("bC", [P, 1]), sb("bC_in", [P, 1])
        b_out = sb("b_out_row", [P, D])
        d_row = sb("d_row", [P, HEADS])
        a_row = sb("a_row", [P, HEADS])
        sp_a, sp_b, sp_c, sp_d, sp_e = (sb(f"sp{n}", [P, TILES, HEADS]) for n in range(5))
        a_all = sb("a_all", [P, TILES, HEADS])
        nxT = sb("nxT_m", [P, NT, KD, P])
        xr = sb("xr", [P, NT, 2, D])
        idx = sb("idx_m", [P, NT], U32)
        y_exp = sb("y_exp", [P, 2, D])
        resid = sb("resid", [P, 2, D])
        aU = sb("aU", [P, 2, HEADS, P])
        xs = sb("xs", [P, INNER])
        Bs = sb("Bs", [P, 2, STATE])
        BT = sb("BT", [STATE, P])
        CT = sb("CT", [P, 2, P])
        z = sb("z", [P, JI, P])
        th = sb("th", [P, JI, P])
        gate = sb("gate", [P, 2, JI, P])
        L = sb("L", [P, 2, HEADS, P])
        E2 = sb("E2", [P, 2, JI, P])
        Gm = sb("Gm", [P, P])
        M = sb("M", [P, 2, HEADS, P])
        CE = sb("CE", [P, 2, JI, P])
        dtx = sb("dtx", [P, 2, HEADS, PW])
        wdtx = sb("wdtx", [P, 2, HEADS, PW])
        xsD = sb("xsD", [P, 2, HEADS, PW])
        Hs = sb("Hs", [P, JI, PW])
        HB = sb("HB", [P, JI, P])
        yg = sb("yg", [P, JI, P])
        r = sb("r_m", [P, 2, D])

        w_in, set_step, set_act, set_done = sem("w_in_m"), sem("set_step"), sem("set_act"), sem("set_done")
        bias_mm = sem("bias_mm")
        nx_in = [sem(f"nx_in{n}") for n in range(NT)]
        xr_in = [sem(f"xr_in{n}") for n in range(NT)]
        aU_r, resid_r, resid_s, wdtx_r, xsD_r = (sem(n) for n in ("aU_r", "resid_r", "resid_s", "wdtx_r", "xsD_r"))
        xs_mm, bc_mm, z_mm, cum_mm, e_mm, g_mm, y_mm, st_mm, out_mm = (
            sem(n) for n in ("xs_mm", "bc_mm", "z_mm", "cum_mm", "e_mm", "g_mm", "y_mm_m", "st_mm", "out_mm"))
        xs_r, bc_r, dtx_r, gate_r, Gm_r, M_r, CE_r, yg_r, h_step, h_r, r_r = (
            sem(n) for n in ("xs_r", "bc_r", "dtx_r", "gate_r", "Gm_r", "M_r", "CE_r", "yg_r", "h_step", "h_r", "r_r"))
        z_r, th_r, L_r, E_r, HB_r = (sem(n) for n in ("z_r", "th_r", "L_r", "E_r", "HB_r"))
        r_out = [sem("r_out0"), sem("r_out1")]
        idx_done = sem("idx_done_m")
        gathered = [sem("gathered0"), sem("gathered1")]
        block = ctx.enter_context(nc.Block())
        W_LOADS = 17
        x_t = d["L0_attn_input_tensor"].rearrange("b (t p) d -> (b t) p d", p=P)
        xn_t = c.xn_dram.rearrange("(i p) d -> i p d", p=P)
        r_t = c.out.rearrange("b (t p) d -> (b t) p d", p=P)

        def chunks(eng, body):
            for n in range(NT):
                body(n, 0, n)
            with eng.Fori(1, B - 1) as b:
                for n in range(NT):
                    body(NT * b + n, b, n)
            for n in range(NT):
                body(NT * (B - 1) + n, B - 1, n)

        @block.sync
        def _(sp):
            ld = lambda dst, src: sp.dma_start(dst, src).then_inc(w_in, 16)
            ld(win[:], d["L0_attn_W_in"].rearrange("(k p) n -> p k n", p=P))
            b_in = d["L0_attn_b_in"]
            with nc.allow_non_contiguous_dma(reason="small vectors"):
                ld(g_ln[:], d["L0_attn_ln_gamma"].rearrange("(k p) -> p k", p=P))
                ld(be_ln[:], d["L0_attn_ln_beta"].rearrange("(k p) -> p k", p=P))
                ld(bz_in[:], b_in[Z0:Z0 + INNER].rearrange("(k p) -> p k", p=P))
                ld(bB_in[:], b_in[B0:B0 + STATE].rearrange("(p o) -> p o", o=1))
                for half in range(2):
                    ld(bC_in[STATE * half:STATE * half + STATE], b_in[C0:C0 + STATE].rearrange("(p o) -> p o", o=1))
            for k in range(2):
                ld(wc2[:, :, bass.ts(k, STATE)], d["L0_attn_W_in"][:, C0:C0 + STATE].rearrange("(k p) n -> p k n", p=P))
            ld(b_in_row[:], row(b_in[INNER:PROJ]))
            ld(dtb_in[:], row(d["L0_attn_dt_bias"]))
            ld(a_row[:], row(d["L0_attn_A_log"]))
            ld(d_row[:], row(d["L0_attn_D_skip"]))
            ld(b_out[:], row(d["L0_attn_b_out"]))
            ld(wout[:], d["L0_attn_W_out"].rearrange("(j p) n -> p j n", p=P))
            sp.dma_start(dtb[:], row(b_in[DT0:PROJ])).then_inc(w_in, 16)
            assert W_LOADS == 17

            def load(i, n):
                sp.dma_start(nxT[:, n], c.nxT_dram[:, :, bass.ts(i, P)].rearrange("k p t -> p k t")).then_inc(nx_in[n], 16)
                sp.dma_start(xr[:, n, 0], x_t[i]).then_inc(xr_in[n], 16)
                sp.dma_start(xr[:, n, 1], xn_t[i]).then_inc(xr_in[n], 16)

            for n in range(NT):
                load(n, n)

            def body(i, b, n):
                sp.wait_ge(r_r, i + 1)
                sp.dma_start(r_t[i], r[:, n % 2]).then_inc(r_out[n % 2], 16)
                if not isinstance(i, int) or i + NT < TILES:
                    sp.wait_ge(z_mm, i + 1)
                    sp.wait_ge(resid_s, 2 * i + 1)
                    load(i + NT, n)

            chunks(sp, body)
            for p in range(2):
                sp.wait_ge(r_out[p], 16 * TILES // 2)

        @block.tensor
        def _(pe):
            pe.wait_ge(w_in, 16 * (W_LOADS - 1))
            pe.wait_ge(set_step, 1)
            mm = nc.tensor.matmul
            for k in range(KD):
                mm(c.bank[0], be_wide[:, k], win[:, k, X0:X0 + INNER], start=k == 0, stop=k == 1)
            for k in range(KD):
                mm(c.bank[1][:, 0:STATE], be_wide[:, k], win[:, k, B0:B0 + STATE], start=k == 0, stop=k == 1)
            for k in range(KD):
                mm(c.bank[1][:, 64:64 + HEADS], be_wide[:, k], win[:, k, DT0:PROJ], start=k == 0, stop=k == 1)
            for j in range(JI):
                for k in range(KD):
                    mm(c.bank[2][:, j:j + 1], win[:, k, bass.ts(j, P)], be_ln[:, k:k + 1], start=k == 0, stop=k == 1)
            for k in range(KD):
                mm(c.bank[2][0:STATE, 8:9], win[:, k, B0:B0 + STATE], be_ln[:, k:k + 1], start=k == 0, stop=k == 1)
            for k in range(KD):
                ins = mm(c.bank[2][:, 9:10], wc2[:, k], be_ln[:, k:k + 1], start=k == 0, stop=k == 1)
            ins.then_inc(bias_mm, 1)
            pe.wait_ge(set_done, 1)

            def front(i, b, n):
                p = n % 2
                pe.wait_ge(nx_in[n], 16 * (b + 1))
                wait(pe, xs_r, i)
                for k in range(KD):
                    ins = mm(c.bank[0], nxT[:, n, k], win[:, k, X0:X0 + INNER], start=k == 0, stop=k == 1)
                ins.then_inc(xs_mm, 1)
                wait(pe, bc_r, i)
                wait(pe, Gm_r, i)
                for k in range(KD):
                    mm(c.bank[1][:, 0:STATE], nxT[:, n, k], win[:, k, B0:B0 + STATE], start=k == 0, stop=k == 1)
                for k in range(KD):
                    mm(c.bank[1][0:STATE, P:2 * P], win[:, k, B0:B0 + STATE], nxT[:, n, k], start=k == 0, stop=k == 1)
                for k in range(KD):
                    ins = mm(c.bank[1][:, 2 * P:3 * P], wc2[:, k], nxT[:, n, k], start=k == 0, stop=k == 1)
                ins.then_inc(bc_mm, 1)
                wait(pe, z_r, i)
                for j in range(JI):
                    for k in range(KD):
                        ins = mm(c.bank[2][:, bass.ts(j, P)], win[:, k, bass.ts(j, P)], nxT[:, n, k], start=k == 0, stop=k == 1)
                ins.then_inc(z_mm, 1)
                pe.wait_ge(aU_r, i + 1)
                wait(pe, L_r, i)
                for half in range(2):
                    ins = mm(c.bank[4 + half], c.strict[:], aU[:, p, 4 * half:4 * half + 4], start=True, stop=True)
                ins.then_inc(cum_mm, 1)
                wait(pe, E_r, i)
                for odd in range(2):
                    ins = mm(c.bank[6][STATE * odd:STATE * odd + STATE], c.ones[:, 0:STATE], aU[:, p, odd:HEADS:2],
                             start=True, stop=True)
                ins.then_inc(e_mm, 1)

            def cb(i, n):
                pe.wait_ge(bc_r, i + 1)
                mm(c.bank[1][:, 3 * P:4 * P], BT[:], CT[0:STATE, n % 2], start=True, stop=True).then_inc(g_mm, 1)

            def back(i, b, n):
                p = n % 2
                pe.wait_ge(xsD_r, i + 1)
                pe.wait_ge(M_r, i + 1)
                pe.wait_ge(CE_r, i + 1)
                wait(pe, yg_r, i)
                if n > 0:
                    pe.wait_ge(HB_r, 2 * (3 * b + n))
                for j in range(JI):
                    out = c.bank[7][:, bass.ts(j, P)]
                    mm(out, xsD[:, p, 2 * j:2 * j + 2].rearrange("p h e -> p (h e)"), c.ident[:], start=True, stop=False)
                    if n > 0:
                        mm(out, HB[:, j], CE[:, p, j], start=False, stop=False)
                    for odd in range(2):
                        ins = mm(c.bank[7][PW * odd:PW * odd + PW, bass.ts(j, P)], dtx[:, p, 2 * j + odd], M[:, p, 2 * j + odd],
                                 start=False, stop=True)
                ins.then_inc(y_mm, 1)
                if n < NT - 1:
                    pe.wait_ge(wdtx_r, i + 1)
                    wait(pe, r_r, i)
                    for odd in range(2):
                        ins = mm(c.bank[3][STATE * odd:STATE * odd + STATE, 0:JI * PW], Bs[:, p],
                                 wdtx[:, p, odd:HEADS:2], start=True, stop=True)
                    ins.then_inc(st_mm, 1)

            def outs(i, b, n):
                pe.wait_ge(yg_r, i + 1)
                if n < NT - 1:
                    pe.wait_ge(h_r, 3 * b + n + 1)
                else:
                    wait(pe, r_r, i)
                for j in range(JI):
                    ins = mm(c.bank[3][:, D:2 * D], yg[:, j], wout[:, j], start=j == 0, stop=j == JI - 1)
                ins.then_inc(out_mm, 1)

            front(0, 0, 0)
            cb(0, 0)

            def body(i, b, n):
                more = not isinstance(i, int) or i + 1 < TILES
                if more:
                    front(i + 1, b + (n + 1) // NT, (n + 1) % NT)
                back(i, b, n)
                if more:
                    cb(i + 1, n + 1)
                outs(i, b, n)

            chunks(pe, body)

        @block.scalar
        def _(act):
            act.wait_ge(w_in, 16 * (W_LOADS - 1))
            nc.scalar.activation(a_row[:], a_row[:], ACT.Exp).then_inc(set_act, 1)
            act.wait_ge(set_step, 2)
            nc.scalar.activation(sp_b[:], sp_b[:], ACT.Exp).then_inc(set_act, 1)
            act.wait_ge(set_step, 3)
            nc.scalar.activation(sp_d[:], sp_c[:], ACT.Ln).then_inc(set_act, 1)
            act.wait_ge(set_done, 1)

            def front(i, n):
                p = n % 2
                act.wait_ge(z_mm, i + 1)
                wait(act, gate_r, i)
                for j in range(JI):
                    ins = nc.scalar.activation(z[:, j], c.bank[2][:, bass.ts(j, P)], ACT.Identity, bias=bz[:, j:j + 1])
                ins.then_inc(z_r, 1)
                act.wait_ge(z_r, i + 1)
                nc.scalar.activation(th[:], z[:], ACT.Tanh, scale=0.5).then_inc(th_r, 1)
                act.wait_ge(cum_mm, i + 1)
                wait(act, M_r, i - 1)
                wait(act, wdtx_r, i - 1)
                nc.scalar.activation(L[:, p], c.psum[:, 4:6].rearrange("p a (h t) -> p (a h) t", t=P), ACT.Exp).then_inc(L_r, 1)
                act.wait_ge(e_mm, i + 1)
                wait(act, CE_r, i - 1)
                wait(act, h_r, h_before)
                nc.scalar.activation(E2[:, p], c.bank[6].rearrange("p (j t) -> p j t", t=P), ACT.Exp).then_inc(E_r, 1)

            h_before = 0
            front(0, 0)

            def body(i, b, n):
                nonlocal h_before
                if not isinstance(i, int) or i + 1 < TILES:
                    h_before = 3 * b + n if n < NT - 1 else 3 * b + NT - 1
                    front(i + 1, (n + 1) % NT)
                if n < NT - 1:
                    act.wait_ge(h_r, 3 * b + n + 1)
                    act.wait_ge(y_mm, i + 1)
                    for odd in range(2):
                        rows = slice(STATE * odd, STATE * odd + STATE)
                        nc.scalar.copy(HB[rows, :, bass.ts(odd, PW)], Hs[rows]).then_inc(HB_r, 1)

            chunks(act, body)

        @block.vector
        def _(dve):
            dve.wait_ge(w_in, 16 * (W_LOADS - 1))
            v = nc.vector
            v.memset(HB[:], 0.0)
            v.tensor_copy(be_wide[:], be_ln[:].unsqueeze(2).to_broadcast([P, KD, P])).then_inc(set_step, 1)
            dve.wait_ge(bias_mm, 1)
            v.tensor_tensor(b_row[:, 0:INNER], c.bank[0], b_in_row[:, 0:INNER], ALU.add)
            v.tensor_tensor(b_row[:, INNER:], c.bank[1][:, 0:STATE], b_in_row[:, INNER:INNER + STATE], ALU.add)
            v.tensor_tensor(dtb[:], c.bank[1][:, 64:64 + HEADS], b_in_row[:, PROJ - INNER - HEADS:], ALU.add)
            v.tensor_tensor(bz[:], c.bank[2][:, 0:JI], bz_in[:], ALU.add)
            v.tensor_tensor(bB[:], c.bank[2][0:STATE, 8:9], bB_in[:], ALU.add)
            v.tensor_tensor(bC[:], c.bank[2][:, 9:10], bC_in[:], ALU.add)
            for k in range(KD):
                v.tensor_scalar(win[:, k], win[:, k], g_ln[:, k:k + 1], None, ALU.mult)
                v.tensor_scalar(wc2[:, k], wc2[:, k], g_ln[:, k:k + 1], None, ALU.mult)
            step = Steps(dve, h_step, 0)
            step.then(v.tensor_scalar(wout[:], wout[:], 0.5, None, ALU.mult))
            step.then(v.tensor_tensor(dtb[:], dtb[:], dtb_in[:], ALU.add))
            step.then(v.tensor_tensor(sp_a[:], c.dt_all[:], dtb[:].unsqueeze(1).to_broadcast([P, TILES, HEADS]), ALU.add))
            step.then(v.tensor_scalar(sp_b[:], sp_a[:], -1.0, None, ALU.mult))
            v.tensor_tensor(sp_b[:], sp_b[:], sp_a[:], ALU.min).then_inc(set_step, 1)
            dve.wait_ge(set_act, 2)
            v.tensor_scalar(sp_c[:], sp_b[:], 1.0, None, ALU.add).then_inc(set_step, 1)
            dve.wait_ge(set_act, 3)
            step.then(v.tensor_scalar(sp_c[:], sp_c[:], -1.0, None, ALU.add))
            step.then(v.tensor_scalar(sp_e[:], sp_c[:], 0.0, None, ALU.is_equal))
            step.then(v.tensor_tensor(sp_c[:], sp_c[:], sp_e[:], ALU.add))
            step.then(v.reciprocal(sp_c[:], sp_c[:]))
            step.then(v.tensor_tensor(sp_d[:], sp_d[:], sp_e[:], ALU.add))
            step.then(v.tensor_tensor(sp_d[:], sp_d[:], sp_c[:], ALU.mult))
            step.then(v.tensor_tensor(sp_d[:], sp_d[:], sp_b[:], ALU.mult))
            step.then(v.tensor_scalar(sp_a[:], sp_a[:], 0.0, None, ALU.max))
            step.then(v.tensor_tensor(c.dt_all[:], sp_a[:], sp_d[:], ALU.add))
            step.then(v.tensor_scalar(a_row[:], a_row[:], -1.0, None, ALU.mult))
            v.tensor_tensor(a_all[:], c.dt_all[:], a_row[:].unsqueeze(1).to_broadcast([P, TILES, HEADS]),
                            ALU.mult).then_inc(set_done, 1)
            H0 = step.at

            def front_a(i, n):
                p = n % 2
                dve.wait_ge(xs_mm, i + 1)
                wait(dve, xsD_r, i)
                v.tensor_tensor(xs[:], c.bank[0], b_row[:, 0:INNER], ALU.add).then_inc(xs_r, 1)
                dve.wait_ge(bc_mm, i + 1)
                wait(dve, st_mm, st_before)
                wait(dve, g_mm, i)
                v.tensor_tensor(Bs[:, p], c.bank[1][:, 0:STATE], b_row[:, INNER:], ALU.add)
                v.tensor_scalar(BT[:], c.bank[1][0:STATE, P:2 * P], bB[:], None, ALU.add)
                v.tensor_scalar(CT[:, p], c.bank[1][:, 2 * P:3 * P], bC[:], None, ALU.add).then_inc(bc_r, 1)
                dve.wait_ge(xs_r, i + 1)
                wait(dve, y_mm, i - 1)
                v.tensor_tensor(dtx[:, p], xs[:].rearrange("p (h e) -> p h e", h=HEADS),
                                c.dt_all[:, bass.ds(i, 1)].rearrange("p o h -> p (o h)").unsqueeze(2).to_broadcast([P, HEADS, PW]),
                                ALU.mult).then_inc(dtx_r, 1)

            def front_b(i, n):
                p = n % 2
                dve.wait_ge(g_mm, i + 1)
                v.tensor_tensor(Gm[:], c.bank[1][:, 3 * P:4 * P], c.upper[:], ALU.mult).then_inc(Gm_r, 1)
                dve.wait_ge(Gm_r, i + 1)
                dve.wait_ge(L_r, i + 1)
                v.tensor_tensor(M[:, p], L[:, p], Gm[:].unsqueeze(1).to_broadcast([P, HEADS, P]), ALU.mult).then_inc(M_r, 1)
                dve.wait_ge(E_r, i + 1)
                v.tensor_tensor(CE[:, p], E2[:, p], CT[:, p].unsqueeze(1).to_broadcast([P, JI, P]), ALU.mult).then_inc(CE_r, 1)
                dve.wait_ge(th_r, i + 1)
                v.scalar_tensor_tensor(out=gate[:, p], in0=th[:], scalar=1.0, in1=z[:], op0=ALU.add,
                                       op1=ALU.mult).then_inc(gate_r, 1)

            st_before = 0
            front_a(0, 0)
            front_b(0, 0)

            def body(i, b, n):
                nonlocal st_before
                more = not isinstance(i, int) or i + 1 < TILES
                if more:
                    st_before = 3 * b + n
                    front_a(i + 1, (n + 1) % NT)
                dve.wait_ge(y_mm, i + 1)
                dve.wait_ge(gate_r, i + 1)
                wait(dve, out_mm, i)
                v.tensor_tensor(yg[:], c.bank[7].rearrange("p (j t) -> p j t", t=P), gate[:, n % 2], ALU.mult).then_inc(yg_r, 1)
                if n < NT - 1:
                    own = c.bank[3][:, 0:JI * PW].rearrange("p (j e) -> p j e", j=JI)
                    wait(dve, HB_r, 2 * (3 * b + n))
                    dve.wait_ge(st_mm, 3 * b + n + 1)
                    if n == 0:
                        v.tensor_copy(Hs[:], own).then_inc(h_r, 1)
                    else:
                        v.tensor_tensor(Hs[:], Hs[:], E2[:, n % 2, :, P - 1:P].to_broadcast([P, JI, PW]),
                                        ALU.mult).then_inc(h_step, 1)
                        dve.wait_ge(h_step, H0 + 2 * b + n)
                        v.tensor_tensor(Hs[:], Hs[:], own, ALU.add).then_inc(h_r, 1)
                if more:
                    front_b(i + 1, (n + 1) % NT)
                dve.wait_ge(out_mm, i + 1)
                dve.wait_ge(resid_r, i + 1)
                wait(dve, r_out[n % 2], 16 * (2 * b + n // 2))
                v.tensor_tensor(r[:, n % 2], c.bank[3][:, D:2 * D], resid[:, n % 2], ALU.add).then_inc(r_r, 1)

            chunks(dve, body)

        @block.gpsimd
        def _(pool):
            pool.wait_ge(set_done, 1)
            g = nc.gpsimd

            def front(i, b, n):
                p = n % 2
                wait(pool, resid_r, i - 1)
                settle(core, g)
                g.tensor_copy(idx[:, n:n + 1], c.pos_y[:, bass.ds(i, 1)]).then_inc(idx_done, 1)
                pool.wait_ge(idx_done, i + 1)
                settle(core, g)
                pool.indirect_dma_start(y_exp[:, p], None, c.yg_dram,
                                        bass.IndirectOffsetOnAxis(ap=idx[:, n:n + 1], axis=0)).then_inc(gathered[p], 16)
                wait(pool, e_mm, i - 1)
                g.tensor_tensor(aU[:, p], c.upper[:].unsqueeze(1).to_broadcast([P, HEADS, P]),
                                a_all[:, bass.ds(i, 1)].rearrange("p o h -> p (o h)").unsqueeze(2).to_broadcast([P, HEADS, P]),
                                ALU.mult).then_inc(aU_r, 1)
                pool.wait_ge(xs_r, i + 1)
                wait(pool, y_mm, i - 1)
                g.tensor_tensor(xsD[:, p], xs[:].rearrange("p (h e) -> p h e", h=HEADS),
                                d_row[:].unsqueeze(2).to_broadcast([P, HEADS, PW]), ALU.mult).then_inc(xsD_r, 1)
                pool.wait_ge(dtx_r, i + 1)
                pool.wait_ge(L_r, i + 1)
                g.tensor_tensor(wdtx[:, p], dtx[:, p], L[:, p, :, P - 1:P].to_broadcast([P, HEADS, PW]), ALU.mult).then_inc(wdtx_r, 1)
                pool.wait_ge(xr_in[n], 32 * (b + 1))
                wait(pool, r_r, i - 1)
                g.tensor_tensor(resid[:, p], xr[:, n, 0], xr[:, n, 1], ALU.add).then_inc(resid_s, 1)
                pool.wait_ge(resid_s, 2 * i + 1)
                g.tensor_tensor(resid[:, p], resid[:, p], b_out[:], ALU.add).then_inc(resid_s, 1)
                pool.wait_ge(gathered[p], 16 * (2 * b + n // 2 + 1))
                pool.wait_ge(resid_s, 2 * i + 2)
                g.tensor_tensor(resid[:, p], resid[:, p], y_exp[:, p], ALU.add).then_inc(resid_r, 1)

            front(0, 0, 0)

            def body(i, b, n):
                if not isinstance(i, int) or i + 1 < TILES:
                    front(i + 1, b + (n + 1) // NT, (n + 1) % NT)

            chunks(pool, body)


def build(nc, ins, out):
    with ExitStack() as ctx:
        core = Core(nc, ctx, ins, out)
        constants(core)
        project(core)
        attend(core)
        tables(core)
        experts(core)
        mamba(core)


_INS = ['L0_attn_input_tensor', 'L0_attn_ln_gamma', 'L0_attn_ln_beta', 'L0_attn_W_in', 'L0_attn_b_in',
        'L0_attn_A_log', 'L0_attn_D_skip', 'L0_attn_dt_bias', 'L0_attn_W_out', 'L0_attn_b_out', 'L0_ffn_Wq',
        'L0_ffn_bq', 'L0_ffn_Wk', 'L0_ffn_bk', 'L0_ffn_Wv', 'L0_ffn_bv', 'L0_ffn_Wo', 'L0_ffn_bo',
        'L0_ffn_router_w', 'L0_ffn_router_b', 'L0_ffn_W1', 'L0_ffn_b1', 'L0_ffn_W2', 'L0_ffn_b2',
        'L0_ffn_ln1_g', 'L0_ffn_ln1_b', 'L0_ffn_ln2_g', 'L0_ffn_ln2_b']


def kernel(**inputs):
    import numpy as np
    import concourse.bacc as bacc
    from concourse.bass_utils import run_bass_kernel_spmd

    nc = bacc.Bacc("TRN2", target_bir_lowering=False, num_devices=1)
    arrays, ins = {}, {}
    for name in _INS:
        a = np.ascontiguousarray(inputs[name])
        arrays["in_" + name] = a
        ins[name] = nc.dram_tensor("in_" + name, a.shape, mybir.dt.from_np(a.dtype), kind="ExternalInput").ap()
    out = nc.dram_tensor("out_0", (B, T, D), FP32, kind="ExternalOutput").ap()
    build(nc, ins, out)
    result = run_bass_kernel_spmd(nc, [arrays], core_ids=[0])
    return result.results[0]["out_0"]
```

```python
import concourse.bass as bass
from concourse import mybir
from contextlib import ExitStack

FP32 = mybir.dt.float32
BF16 = mybir.dt.bfloat16
FP32R = mybir.dt.float32r
I32 = mybir.dt.int32
U32 = mybir.dt.uint32
ALU = mybir.AluOpType
ACT = mybir.ActivationFunctionType
AX = mybir.AxisListType

P = 128
B, T, D = 8, 512, 256
NT = T // P
TILES = B * NT
KD = D // P
H, HD = 16, 16
UH = P // HD
PARTS = 3
PAIRS_Q = (0, 0, 1, 1, 0, 2)
PAIRS_K = (0, 1, 0, 1, 2, 0)
KS = len(PAIRS_Q) * HD
KM = KS + PARTS
SCALE = HD ** -0.5
INNER, STATE, HEADS, PW = 512, 64, 8, 64
PROJ = 2 * INNER + 2 * STATE + HEADS
JI = INNER // P
E, FF = 4, 1024
ETILES = TILES + E - 1
TAIL = E * P
REGION = B * T + TAIL
EPS = 1e-5


def wait(eng, sem, value):
    if not isinstance(value, int) or value > 0:
        eng.wait_ge(sem, value)


def settle(core, eng):
    cell = core.pad[:, core.pads:core.pads + 1]
    core.pads += 1
    if eng is core.nc.vector:
        eng.memset(cell, 0.0)
    else:
        eng.tensor_tensor(cell, core.ones[0:1, 0:1], core.ones[0:1, 0:1], ALU.mult)


class Steps:

    def __init__(self, eng, sem, base):
        self.eng, self.sem, self.at = eng, sem, base

    def then(self, ins, core=None):
        ins.then_inc(self.sem, 1)
        self.at = self.at + 1
        self.eng.wait_ge(self.sem, self.at)
        if core:
            settle(core, core.nc.vector)


class Core:

    def __init__(self, nc, ctx, ins, out):
        self.nc, self.ctx, self.i, self.out = nc, ctx, ins, out
        self.psum = ctx.enter_context(nc.psum_tensor("psum", [P, 8, 512], FP32))
        self.bank = [self.psum[:, n] for n in range(8)]

        def dram(name, shape, dt=FP32):
            return nc.dram_tensor(name, shape, dt).ap()

        self.xn_dram = dram("xn_scratch", [B * T, D])
        self.nxT_dram = dram("nxT_scratch", [KD, P, B * T])
        self.parts_dram = dram("qk_parts", [2, B, 2, PARTS, P, T], BF16)
        self.rows_dram = dram("max_rows", [2, PARTS, UH * NT, P], BF16)
        self.v_dram = dram("v_scratch", [B * T, H * 2 * HD])
        self.xg_dram = dram("x1_grouped", [E * REGION, D])
        self.yg_dram = dram("y_grouped", [ETILES * P, D])
        self.pad, self.pads = self.sb("pad", [1, 128]), 0
        self.ident = self.sb("ident", [P, P])
        self.upper = self.sb("upper", [P, P])
        self.strict = self.sb("strict", [P, P])
        self.ones = self.sb("ones", [P, P])
        self.neg_half = self.sb("neg_half", [P, 8])
        self.dt_all = self.sb("dt_all", [P, TILES, HEADS])
        self.e_i = self.sb("e_i", [P, E], I32)
        self.e_num = self.sb("e_num", [P, E])
        self.e_row = self.sb("e_row", [P, E])
        self.seen = self.sb("seen", [P, NT + 1, E])
        self.pos_i = self.sb("pos_i", [P, TILES], U32)
        self.pos_y = self.sb("pos_y", [P, TILES], U32)
        self.which_i = self.sb("which_i", [P, ETILES], I32)
        self.row_i = self.sb("row_i", [P, ETILES], I32)

    def sb(self, name, shape, dt=FP32, ctx=None):
        return (ctx or self.ctx).enter_context(self.nc.sbuf_tensor(name, shape, dt))

    def sem(self, name, ctx=None):
        return (ctx or self.ctx).enter_context(self.nc.semaphore(name))


def memory(core, ctx, prefix, sizes, sems):
    kept = {n: core.sb(prefix + n, shape, *dt, ctx=ctx) for n, (shape, *dt) in sizes.items()}
    for n, many in sems.items():
        own = [core.sem(f"{prefix}{n}{k}", ctx) for k in range(many)]
        kept[n] = own if many > 1 else own[0]
    return kept


MAMBA_KEEPS = dict(
    win=([P, KD, PROJ],), wc2=([P, KD, 2 * STATE],), wout=([P, JI, D],),
    b_row=([P, INNER + STATE],), bz=([P, JI],), bB=([STATE, 1],), bC=([P, 1],),
    d_row=([P, HEADS],), a_hi=([P, TILES, HEADS],), a_lo=([P, TILES, HEADS],))
ATTEND_KEEPS = dict(qs=([P, 4, UH, T], BF16), ks=([P, 4, UH, T], BF16), v=([P, 2, NT, H * 2 * HD],))
EXPERT_WEIGHTS = dict(w1=([P, E, KD, FF],))
EXPERT_KEEPS = dict(w2=([P, E, FF // P, D],), b1=([P, E, FF],), b2=([P, E, D],), g2=([P, D],), be2=([P, D],), xg=([P, 4, D],))


def row(vector):
    return vector.unsqueeze(0).to_broadcast([P, vector.shape[0]])


def constants(core):
    nc, c = core.nc, core
    with ExitStack() as ctx:
        filled = core.sem("filled", ctx)
        made = core.sem("made", ctx)
        numbered = core.sem("numbered", ctx)
        block = ctx.enter_context(nc.Block())

        @block.vector
        def _(dve):
            nc.vector.memset(c.seen[:], 0.0)
            dve.wait_ge(numbered, 1)
            nc.vector.tensor_copy(c.e_num[:], c.e_i[:]).then_inc(made, 1)
            dve.wait_ge(made, 1)
            nc.vector.tensor_scalar(c.e_row[:], c.e_num[:], float(REGION), None, ALU.mult)

        @block.gpsimd
        def _(pool):
            nc.gpsimd.iota(c.e_i[:], pattern=[[1, E]], base=0, channel_multiplier=0).then_inc(numbered, 1)
            nc.gpsimd.memset(c.ident[:], 0.0)
            nc.gpsimd.memset(c.upper[:], 1.0)
            nc.gpsimd.memset(c.strict[:], 1.0)
            nc.gpsimd.memset(c.ones[:], 1.0)
            nc.gpsimd.memset(c.neg_half[:], -0.5).then_inc(filled, 1)
            pool.wait_ge(filled, 1)
            nc.gpsimd.affine_select(out=c.ident[:], in_=c.ident[:], compare_op=ALU.not_equal, fill=1.0,
                                    base=0, pattern=[[-1, P]], channel_multiplier=1)
            nc.gpsimd.affine_select(out=c.upper[:], in_=c.upper[:], compare_op=ALU.is_ge, fill=0.0,
                                    base=0, pattern=[[1, P]], channel_multiplier=-1)
            nc.gpsimd.affine_select(out=c.strict[:], in_=c.strict[:], compare_op=ALU.is_ge, fill=0.0,
                                    base=-1, pattern=[[-1, P]], channel_multiplier=1)


def project(core):
    nc, c, d = core.nc, core, core.i
    with ExitStack() as ctx:
        sb = lambda name, shape, dt=FP32: core.sb(name, shape, dt, ctx)
        sem = lambda name: core.sem(name, ctx)
        x = sb("x", [P, 2, NT, D])
        xn = sb("xn", [P, 2, NT, D])
        nx = sb("nx", [P, 2, NT, D])
        xnT = sb("xnT", [P, KD, T])
        nxT = sb("nxT", [P, 2, KD, T])
        wq, wk, wv = (sb(n, [P, KD, D]) for n in ("wq", "wk", "wv"))
        wdt = sb("wdt", [P, KD, HEADS])
        bq, bk, g_ln = (sb(n, [P, KD]) for n in ("bq", "bk", "g_ln"))
        bv = sb("bv", [P, D])
        full = sb("qk_full", [P, 4, T])
        rest = sb("qk_rest", [P, 4, T])
        parts = sb("qk_parts_sb", [P, 4, PARTS, T], BF16)
        v = sb("v_padded", [P, NT, H, 2 * HD])
        stats = sb("stats", [P, 2, NT, 6])
        mv = sb("mv", [P, 2, NT, 2])
        ve = sb("ve", [P, 2, NT])
        rstd = sb("rstd", [P, 2, NT])
        minus_mean = sb("minus_mean_p", [P, NT])
        shift = sb("shift_p", [P, NT])

        w_in = sem("w_in")
        x_in = [sem("x_in0"), sem("x_in1")]
        ln_var = sem("ln_var")
        ln_rstd = sem("ln_rstd")
        rstd_made = sem("rstd_made_p")
        xn_ready = sem("xn_ready")
        nx_ready = sem("nx_ready")
        xn_out = [sem("xn_out0"), sem("xn_out1")]
        t_ready = sem("t_ready")
        t_taken = sem("t_taken")
        tn_taken = sem("tn_taken")
        nxT_out = [sem("nxT_out0"), sem("nxT_out1")]
        qk_ready = sem("qk_ready")
        full_ready = sem("full_ready")
        rest_ready = sem("rest_ready")
        mid_ready = sem("mid_ready")
        low_ready = sem("low_ready")
        parts_out = [sem(f"parts_out{j}") for j in range(4)]
        v_ready = sem("v_ready")
        v_taken = sem("v_taken")
        v_out = sem("v_out")
        dt_ready = sem("dt_ready")
        dt_taken = sem("dt_taken")
        dve_step = sem("dve_step")
        block = ctx.enter_context(nc.Block())
        x_tiles = d["L0_attn_input_tensor"].rearrange("b (t p) d -> b p t d", p=P)
        xn_tiles = c.xn_dram.rearrange("(b t p) d -> b p t d", t=NT, p=P)
        v_tiles = c.v_dram.rearrange("(b t p) e -> b p t e", t=NT, p=P)
        dv = d["L0_attn_W_in"]
        WEIGHTS = 9 * 16

        @block.sync
        def _(sp):
            sp.dma_start(x[:, 0], x_tiles[0]).then_inc(x_in[0], 16)
            sp.dma_start(x[:, 1], x_tiles[1]).then_inc(x_in[1], 16)
            for dst, src in ((wq, "Wq"), (wk, "Wk"), (wv, "Wv")):
                sp.dma_start(dst[:], d["L0_ffn_" + src].rearrange("(k p) n -> p k n", p=P)).then_inc(w_in, 16)
            with nc.allow_non_contiguous_dma(reason="small vectors"):
                sp.dma_start(wdt[:], dv[:, PROJ - HEADS:PROJ].rearrange("(k p) n -> p k n", p=P)).then_inc(w_in, 16)
                sp.dma_start(bq[:], d["L0_ffn_bq"].rearrange("(k p) -> p k", p=P)).then_inc(w_in, 16)
                sp.dma_start(bk[:], d["L0_ffn_bk"].rearrange("(k p) -> p k", p=P)).then_inc(w_in, 16)
                sp.dma_start(g_ln[:], d["L0_attn_ln_gamma"].rearrange("(k p) -> p k", p=P)).then_inc(w_in, 16)
            sp.dma_start(bv[:], row(d["L0_ffn_bv"])).then_inc(w_in, 16)

            def batch(b, i, p):
                sp.wait_ge(xn_ready, b + 1)
                sp.dma_start(xn_tiles[b], xn[:, p]).then_inc(xn_out[p], 16)
                if not isinstance(b, int) or b + 2 < B:
                    sp.dma_start(x[:, p], x_tiles[b + 2]).then_inc(x_in[p], 16)
                sp.wait_ge(tn_taken, 2 * b + 2)
                sp.dma_start(c.nxT_dram[:, :, bass.ts(b, T)].rearrange("k p t -> p k t"),
                             nxT[:, p]).then_inc(nxT_out[p], 16)
                for j in range(4):
                    sp.wait_ge(low_ready, 4 * b + j + 1)
                    sp.dma_start(c.parts_dram[j % 2, b, j // 2].rearrange("a p t -> p a t"),
                                 parts[:, j]).then_inc(parts_out[j], 16)
                sp.wait_ge(v_taken, 2 * b + 2)
                sp.dma_start(v_tiles[b], v[:].rearrange("p t h e -> p t (h e)")).then_inc(v_out, 16)

            batch(0, 0, 0)
            with sp.Fori(0, B // 2 - 2) as i:
                batch(2 * i + 1, i, 1)
                batch(2 * i + 2, i + 1, 0)
            batch(B - 3, B // 2 - 2, 1)
            for j in range(4):
                sp.wait_ge(parts_out[j], 16)
            load_stack(core, sp, 0, 0, 0)
            load_stack(core, sp, 0, 1, 0)
            sp.wait_ge(v_out, 16)
            sp.dma_start(c.att["v"][:, 0], v_tiles[0]).then_inc(c.att["v_in"][0], 16)
            for p in range(2):
                batch(B - 2 + p, B // 2 - 1, p)
            for p in range(2):
                sp.wait_ge(xn_out[p], 16 * B // 2)
                sp.wait_ge(nxT_out[p], 16 * B // 2)
            for j in range(4):
                sp.wait_ge(parts_out[j], 16 * B)
            sp.wait_ge(v_out, 16 * B)

        @block.vector
        def _(dve):
            nc.vector.memset(v[:, :, :, HD:2 * HD], 1.0)
            STEPS = 4

            def batch(b, i, p):
                step = Steps(dve, dve_step, STEPS * b)
                dve.wait_ge(x_in[p], 16 * (i + 1))
                for half, src in enumerate((x, xn)):
                    for t in range(NT):
                        ins = nc.vector.bn_stats(stats[:, half, t], src[:, p, t])
                    step.then(ins, core)
                    for t in range(NT):
                        ins = nc.vector.bn_aggr(mv[:, half, t], stats[:, half, t])
                    step.then(ins)
                    if half == 1:
                        wait(dve, nx_ready, b)
                        nc.vector.tensor_scalar(minus_mean[:], mv[:, half, :, 0], -1.0, None, ALU.mult)
                    nc.vector.tensor_scalar(ve[:, half], mv[:, half, :, 1], EPS, None, ALU.add).then_inc(ln_var, 1)
                    if half == 0:
                        dve.wait_ge(ln_rstd, 2 * b + 1)
                        wait(dve, xn_out[p], 16 * i)
                        wait(dve, nx_ready, b)
                        for t in range(NT):
                            ins = nc.vector.tensor_scalar(xn[:, p, t], x[:, p, t], mv[:, half, t, 0:1],
                                                          rstd[:, half, t:t + 1], ALU.subtract, ALU.mult)
                        ins.then_inc(xn_ready, 1)
                        dve.wait_ge(xn_ready, b + 1)

            def rests(b):
                for j in range(4):
                    dve.wait_ge(full_ready, 4 * b + j + 1)
                    wait(dve, low_ready, 4 * b - 3 + j)
                    nc.vector.tensor_tensor(rest[:, j], full[:, j], parts[:, j, 0], ALU.subtract).then_inc(rest_ready, 1)
                    dve.wait_ge(rest_ready, 4 * b + j + 1)
                    wait(dve, parts_out[j], 16 * b)
                    nc.vector.tensor_copy(parts[:, j, 1], rest[:, j]).then_inc(mid_ready, 1)
                for half in range(2):
                    dve.wait_ge(v_ready, 2 * b + half + 1)
                    if half == 0:
                        wait(dve, v_out, 16 * b)
                    nc.vector.tensor_tensor(
                        v[:, 2 * half:2 * half + 2, :, 0:HD],
                        c.bank[6 + half][:].rearrange("p (t h e) -> p t h e", t=2, h=H),
                        bv[:].rearrange("p (h e) -> p h e", h=H).unsqueeze(1).to_broadcast([P, 2, H, HD]),
                        ALU.add).then_inc(v_taken, 1)

            batch(0, 0, 0)
            dve.wait_ge(w_in, WEIGHTS - 16)
            for k in range(KD):
                ins = nc.vector.tensor_scalar(wdt[:, k], wdt[:, k], g_ln[:, k:k + 1], None, ALU.mult)
            ins.then_inc(w_in, 16)
            batch(1, 0, 1)
            rests(0)
            with dve.Fori(1, B // 2) as i:
                batch(2 * i, i, 0)
                rests(2 * i - 1)
                batch(2 * i + 1, i, 1)
                rests(2 * i)
            rests(B - 1)

        @block.gpsimd
        def _(pool):
            def powers(b):
                for half in range(2):
                    pool.wait_ge(ln_var, 2 * b + half + 1)
                    if half == 0:
                        nc.gpsimd.tensor_tensor(rstd[:, 0], ve[:, 0], c.neg_half[:, 0:NT], ALU.pow).then_inc(ln_rstd, 1)
                    else:
                        wait(pool, nx_ready, b)
                        nc.gpsimd.tensor_tensor(rstd[:, 1], ve[:, 1], c.neg_half[:, 0:NT], ALU.pow).then_inc(rstd_made, 1)
                        pool.wait_ge(rstd_made, b + 1)
                        nc.gpsimd.tensor_tensor(shift[:], minus_mean[:], rstd[:, 1], ALU.mult).then_inc(ln_rstd, 1)

            def lows(b):
                for j in range(4):
                    pool.wait_ge(mid_ready, 4 * b + j + 1)
                    nc.gpsimd.tensor_tensor(parts[:, j, 2], rest[:, j], parts[:, j, 1], ALU.subtract).then_inc(low_ready, 1)

            powers(0)
            with pool.Fori(0, B - 1) as b:
                powers(b + 1)
                lows(b)
            lows(B - 1)

        @block.tensor
        def _(pe):
            pe.wait_ge(w_in, WEIGHTS)

            def batch(b, p):
                for n, src in enumerate((xn, nx)):
                    pe.wait_ge((xn_ready, nx_ready)[n], b + 1)
                    for k in range(KD):
                        if n == 0:
                            wait(pe, dt_taken, b)
                        else:
                            pe.wait_ge(t_taken, 2 * b + 1 + k)
                        for t in range(NT):
                            ins = nc.tensor.transpose(c.bank[k][:, bass.ts(t, P)], src[:, p, t, bass.ts(k, P)], c.ident[:])
                        ins.then_inc(t_ready, 1)
                pe.wait_ge(t_taken, 2 * b + 2)
                for j in range(4):
                    w = (wq, wk)[j % 2]
                    wait(pe, full_ready, 4 * b - 3 + j)
                    for k in range(KD):
                        ins = nc.tensor.matmul(c.bank[2 + j][:], w[:, k, bass.ts(j // 2, P)], xnT[:, k],
                                               start=k == 0, stop=k == KD - 1)
                    ins.then_inc(qk_ready, 1)
                for half in range(2):
                    wait(pe, v_taken, 2 * b - 1 + half)
                    for t in (2 * half, 2 * half + 1):
                        for k in range(KD):
                            ins = nc.tensor.matmul(c.bank[6 + half][:, bass.ts(t % 2, D)], xnT[:, k, bass.ts(t, P)],
                                                   wv[:, k], start=k == 0, stop=k == KD - 1)
                    ins.then_inc(v_ready, 1)
                pe.wait_ge(tn_taken, 2 * b + 2)
                for t in range(NT):
                    for k in range(KD):
                        ins = nc.tensor.matmul(c.bank[0][:, bass.ts(t, HEADS)], nxT[:, p, k, bass.ts(t, P)],
                                               wdt[:, k], start=k == 0, stop=k == KD - 1)
                ins.then_inc(dt_ready, 1)

            batch(0, 0)
            with pe.Fori(0, B // 2 - 1) as i:
                batch(2 * i + 1, 1)
                batch(2 * i + 2, 0)
            batch(B - 1, 1)

        @block.scalar
        def _(act):
            def second_norm(b, p):
                act.wait_ge(ln_rstd, 2 * b + 2)
                wait(act, t_ready, 4 * b - 4)
                for t in range(NT):
                    ins = nc.scalar.activation(nx[:, p, t], xn[:, p, t], ACT.Identity, scale=rstd[:, 1, t:t + 1], bias=shift[:, t:t + 1])
                ins.then_inc(nx_ready, 1)

            second_norm(0, 0)
            act.wait_ge(w_in, WEIGHTS)

            def batch(b, i, p):
                for n in range(2):
                    for k in range(KD):
                        act.wait_ge(t_ready, 4 * b + 2 * n + k + 1)
                        if n == 0:
                            if k == 0:
                                wait(act, v_ready, 2 * b)
                            nc.scalar.copy(xnT[:, k], c.bank[k][:]).then_inc(t_taken, 1)
                        else:
                            if k == 0:
                                wait(act, nxT_out[p], 16 * i)
                                wait(act, dt_ready, b - 1)
                            nc.scalar.copy(nxT[:, p, k], c.bank[k][:]).then_inc(tn_taken, 1)
                for j in range(4):
                    act.wait_ge(qk_ready, 4 * b + j + 1)
                    wait(act, rest_ready, 4 * b - 3 + j)
                    wait(act, parts_out[j], 16 * b)
                    bias = (bq, bk)[j % 2][:, j // 2:j // 2 + 1]
                    nc.scalar.activation(full[:, j], c.bank[2 + j][:], ACT.Identity, bias=bias)
                    nc.scalar.activation(parts[:, j, 0], c.bank[2 + j][:], ACT.Identity, bias=bias).then_inc(full_ready, 1)
                    if j == 1 and (not isinstance(b, int) or b + 1 < B):
                        second_norm(b + 1, 1 - p)
                act.wait_ge(dt_ready, b + 1)
                nc.scalar.copy(c.dt_all[:, bass.ts(b, NT)], c.bank[0][:, 0:NT * HEADS].rearrange("p (t h) -> p t h", t=NT)).then_inc(dt_taken, 1)

            batch(0, 0, 0)
            with act.Fori(0, B // 2 - 1) as i:
                batch(2 * i + 1, i, 1)
                batch(2 * i + 2, i + 1, 0)
            batch(B - 1, B // 2 - 1, 1)


JOBS = {1: ["OT3-"], 2: ["aT0-"], 3: ["neg1"], 4: ["aT1-"], 5: ["OT0"], 6: ["Wo0-"], 7: ["Wo1-"], 9: ["OT1"],
        11: ["neg0+"], 13: ["OT2"], 15: ["cnt-"]}
AHEAD = 5
JOBS_B = sum(len(j) for j in JOBS.values())
STEPS_B = 16


class Jobs:

    def __init__(self, b, first=False, last=False, tail=False):
        kept = [(s, j) for s, js in JOBS.items() for j in js
                if not (first and j[-1] == "-") and not (last and j[-1] == "+") and not (tail and j[-1] != "-")]
        start = 1 if first else JOBS_B * (b - 1) + 6
        if tail:
            start = JOBS_B * (B - 1) + 5
        self.of = {s: [(j, start + n) for n, (s2, j) in enumerate(kept) if s2 == s] for s in range(STEPS_B)}
        self.number = {j: start + n for n, (_, j) in enumerate(kept)}


def masked_w1(core, dt):
    return core.att["qs"][:].rearrange("p a b t -> p (a b t)").bitcast(dt).rearrange("p (e k n) -> p e k n", e=E, k=KD)


def w1_leading(core):
    return core.att["ks"][:].rearrange("p a b t -> p (a b t)").bitcast(FP32R).rearrange("p (e k n) -> p e k n", e=E, k=KD)


def load_stack(core, sp, b, hf, p):
    for dst, pairs, n in ((core.att["qs"], PAIRS_Q, 0), (core.att["ks"], PAIRS_K, 1)):
        for r, part in enumerate(pairs):
            sp.dma_start(dst[HD * r:HD * r + HD, 2 * p + hf],
                         core.parts_dram[n, b, hf, part].rearrange("(h e) t -> e h t", e=HD)
                         ).then_inc(core.att["stack_in"][2 * p + hf], 16)


def attend(core):
    nc, c, d = core.nc, core, core.i
    with ExitStack() as ctx:
        sb = lambda name, shape, dt=FP32: core.sb(name, shape, dt, ctx)
        sem = lambda name: core.sem(name, ctx)
        qs, ks, v = c.att["qs"], c.att["ks"], c.att["v"]
        probs = sb("probs", [P, 2, 4, T])
        nmax = sb("nmax", [P, 2, UH * NT])
        nrow = sb("nrow", [UH * NT, P])
        nrest = sb("nrest", [UH * NT, P])
        nparts = sb("nparts", [UH * NT, PARTS, P], BF16)
        oT = sb("oT", [P, 2, T])
        rsum = sb("rsum", [P, NT, 4])
        attn = sb("attn", [P, NT, D])
        aT = sb("aT", [P, KD, T])
        wo = sb("wo", [P, KD, D])
        bo, g1, b1, rw = (sb(n, [P, D]) for n in ("bo", "g1", "b1", "rw"))
        rb = sb("rb", [P, 1])
        xnb = sb("xnb", [P, NT, D])
        res = sb("res", [P, NT, D])
        norm = sb("norm", [P, NT, D])
        x1 = sb("x1", [P, NT, D])
        stats = sb("stats1", [P, NT, 6])
        mv = sb("mv1", [P, NT, 2])
        ve = sb("ve1", [P, NT])
        rstd = sb("rstd1", [P, NT])
        minus_mean = sb("minus_mean", [P, NT])
        shift = sb("shift", [P, NT])
        kt = sb("kt", [P, NT])
        keys, fl, above, pos = (sb(n, [P, NT]) for n in ("keys", "fl", "above", "pos"))
        whole = sb("whole", [P, NT], I32)
        hot = sb("hot", [P, NT, E])
        at = sb("at", [P, NT, E])
        idx = sb("idx", [P, NT], U32)

        w_in = sem("w_in1")
        set_up = sem("set_up")
        stack_in, v_in = c.att["stack_in"], c.att["v_in"]
        xn_in = sem("xn_in")
        rows_in = [sem(f"rows_in{n}") for n in range(2)]
        s1_ready = sem("s1_ready")
        max_done = sem("max_done")
        s2_ready = sem("s2_ready")
        exp_done = sem("exp_done")
        pv_done = sem("pv_done")
        oT_ready = sem("oT_ready")
        job_ready = sem("job_ready")
        job_taken = sem("job_taken")
        nrow_ready = sem("nrow_ready")
        pool_step = sem("pool_step1")
        rows_made = sem("rows_made")
        rows_out = sem("rows_out")
        xnb_ready = sem("xnb_ready")
        res_done = sem("res_done")
        ve_ready = sem("ve_ready")
        rstd_made = sem("rstd_made")
        rstd_ready = sem("rstd_ready")
        norm_ready = sem("norm_ready")
        x1_ready = sem("x1_ready")
        hot_ready = sem("hot_ready")
        pos_ready = sem("pos_ready")
        idx_done = sem("idx_done")
        scattered = sem("scattered")
        recip_done = sem("recip_done")
        dve_step = sem("dve_step1")
        block = ctx.enter_context(nc.Block())
        xn_tiles = c.xn_dram.rearrange("(b t p) d -> b p t d", t=NT, p=P)
        v_tiles = c.v_dram.rearrange("(b t p) e -> b p t e", t=NT, p=P)
        LOADS = 2 * len(PAIRS_Q) * 16

        @block.sync
        def _(sp):
            load_xn = lambda b: sp.dma_start(xnb[:], xn_tiles[b]).then_inc(xn_in, 16)
            sp.dma_start(wo[:], d["L0_ffn_Wo"].rearrange("(k p) n -> p k n", p=P)).then_inc(w_in, 16)
            for dst, name in ((bo, "bo"), (g1, "ln1_g"), (b1, "ln1_b")):
                sp.dma_start(dst[:], row(d["L0_ffn_" + name])).then_inc(w_in, 16)
            sp.dma_start(rw[:], row(d["L0_ffn_router_w"].rearrange("d o -> (d o)"))).then_inc(w_in, 16)
            with nc.allow_non_contiguous_dma(reason="one number"):
                sp.dma_start(rb[:], row(d["L0_ffn_router_b"])).then_inc(w_in, 16)
            load_xn(0)

            def body(b, p):
                wait(sp, s2_ready, 32 * b - 16)
                load_stack(core, sp, b + 1, 0, 1 - p)
                wait(sp, s2_ready, 32 * b)
                load_stack(core, sp, b + 1, 1, 1 - p)
                wait(sp, oT_ready, 4 * b)
                sp.dma_start(v[:, 1 - p], v_tiles[b + 1]).then_inc(v_in[1 - p], 16)

            def body_xn(b):
                sp.wait_ge(res_done, 2 * b + 2)
                load_xn(b + 1)

            body(0, 0)
            for dst, name in ((c.mam["win"], "W_in"), (c.mam["wout"], "W_out")):
                sp.dma_start(dst[:], d["L0_attn_" + name].rearrange("(k p) n -> p k n", p=P)).then_inc(c.mam["w_in"], 16)
            C0 = 2 * INNER + STATE
            for k in range(2):
                sp.dma_start(c.mam["wc2"][:, :, bass.ts(k, STATE)],
                             d["L0_attn_W_in"][:, C0:C0 + STATE].rearrange("(k p) n -> p k n", p=P)).then_inc(c.mam["w_in"], 16)
            for e in range(E):
                sp.dma_start(c.exp_w["w1"][:, e], d["L0_ffn_W1"][e].rearrange("(k p) n -> p k n", p=P)).then_inc(c.exp_w["w_in"], 16)
            with sp.Fori(0, (B - 2) // 2) as i:
                body(2 * i + 1, 1)
                body_xn(2 * i)
                body(2 * i + 2, 0)
                body_xn(2 * i + 1)
            body_xn(B - 2)

        @block.tensor
        def _(pe):
            def s1(b, hf, p, q, head, tiles=range(NT)):
                n = (2 * b + hf) * UH * NT + head * NT
                if head == 0 and 0 in tiles:
                    pe.wait_ge(stack_in[2 * p + hf], LOADS * (q + 1))
                for t in tiles:
                    wait(pe, max_done, n + t - 1)
                    nc.tensor.matmul(c.bank[t % 2], qs[0:KS, 2 * p + hf, head, bass.ts(t, P)],
                                     ks[0:KS, 2 * p + hf, head], start=True, stop=True).then_inc(s1_ready, 1)

            def s2(b, p, s, pair):
                hf, g, k = s // 8, s // 4 % 2, s % 4
                if s % 8 == 0 and pair == 0:
                    pe.wait_ge(rows_in[hf], 16 * (b + 1))
                    pe.wait_ge(set_up, 1)
                wait(pe, exp_done, 2 * (16 * b + s) + pair - 1)
                for j in (2 * pair, 2 * pair + 1):
                    ins = nc.tensor.matmul(c.bank[2 + j], ks[0:KM, 2 * p + hf, 4 * g + j, bass.ts(k, P)],
                                           qs[0:KM, 2 * p + hf, 4 * g + j], start=True, stop=True)
                ins.then_inc(s2_ready, 1)

            def pv(b, p, q, s):
                k = s % 4
                pe.wait_ge(exp_done, 2 * (16 * b + s) + 2)
                if s == 0:
                    pe.wait_ge(v_in[p], 16 * (q + 1))
                if k == 0:
                    wait(pe, oT_ready, 4 * b + s // 4)
                for j in range(4):
                    ins = nc.tensor.matmul(c.bank[6][32 * j:32 * j + 32], v[:, p, k, bass.ts(s // 4 * 4 + j, 32)],
                                           probs[:, s % 2, j], start=k == 0, stop=k == 3)
                ins.then_inc(pv_done, 1)

            def job(name, n, b):
                wait(pe, job_taken, n)
                if name[:2] == "OT":
                    g = 4 * b + int(name[2]) - (4 if name[-1] == "-" else 0)
                    pe.wait_ge(oT_ready, g + 1)
                    for t in range(NT):
                        ins = nc.tensor.transpose(c.bank[7][:, bass.ts(t, P)], oT[:, int(name[2]) % 2, bass.ts(t, P)], c.ident[:])
                elif name[:2] == "aT":
                    k = int(name[2])
                    for t in range(NT):
                        ins = nc.tensor.transpose(c.bank[7][:, bass.ts(t, P)], attn[:, t, bass.ts(k, P)], c.ident[:])
                elif name[:2] == "Wo":
                    half = int(name[2])
                    for t in (2 * half, 2 * half + 1):
                        for k in range(KD):
                            ins = nc.tensor.matmul(c.bank[7][:, bass.ts(t % 2, D)], aT[:, k, bass.ts(t, P)], wo[:, k],
                                                   start=k == 0, stop=k == KD - 1)
                elif name == "cnt-":
                    pe.wait_ge(hot_ready, b)
                    rows = c.bank[7][:, 0:NT * E]
                    nc.tensor.matmul(rows, c.upper[:], hot[:].rearrange("p t e -> p (t e)"), start=True, stop=False)
                    ins = nc.tensor.matmul(rows, c.ones[:], c.seen[:, 0:NT].rearrange("p t e -> p (t e)"), start=False, stop=True)
                else:
                    hf = int(name[3])
                    u = 2 * b + 1 if hf else 2 * b + 2
                    pe.wait_ge(max_done, UH * NT * (u + 1))
                    ins = nc.tensor.transpose(c.bank[7][0:UH * NT, 0:P], nmax[:, hf], c.ident[:])
                ins.then_inc(job_ready, 1)

            for head in range(UH):
                s1(0, 0, 0, 0, head)
            job("neg0+", 0, -1)
            for head in range(AHEAD):
                s1(0, 1, 0, 0, head)

            def body(b, p, q, first=False, last=False):
                jobs = Jobs(b, first, last)
                for s in range(STEPS_B):
                    w = AHEAD + s - UH
                    if w < 0:
                        ahead = lambda t: s1(b, 1, p, q, AHEAD + s, (t,))
                    elif not last:
                        ahead = lambda t: s1(b + 1, w // UH, 1 - p, q + p, w % UH, (t,))
                    else:
                        ahead = lambda t: None
                    ahead(0)
                    s2(b, p, s, 0)
                    ahead(1)
                    s2(b, p, s, 1)
                    ahead(2)
                    if s == 0 and not first:
                        pv(b - 1, 1 - p, q - (1 - p), STEPS_B - 1)
                    elif s > 0:
                        pv(b, p, q, s - 1)
                    ahead(3)
                    for name, n in jobs.of[s]:
                        job(name, n, b)

            pe.wait_ge(w_in, 6 * 16)
            body(0, 0, 0, first=True)
            with pe.Fori(0, (B - 2) // 2) as i:
                body(2 * i + 1, 1, i)
                body(2 * i + 2, 0, i + 1)
            body(B - 1, 1, B // 2 - 1, last=True)
            pv(B - 1, 1, B // 2 - 1, STEPS_B - 1)
            jobs = Jobs(B, tail=True)
            for s in range(STEPS_B):
                for name, n in jobs.of[s]:
                    job(name, n, B)

        @block.scalar
        def _(act):
            def job(name, n, b):
                if name[:2] in ("OT", "cn"):
                    return
                act.wait_ge(job_ready, n + 1)
                if name[:2] == "aT":
                    nc.scalar.copy(aT[:, int(name[2])], c.bank[7][:]).then_inc(job_taken, 1)
                elif name[:2] == "Wo":
                    half = int(name[2])
                    nc.scalar.copy(res[:, 2 * half:2 * half + 2], c.bank[7].rearrange("p (t e) -> p t e", t=2)).then_inc(job_taken, 1)
                else:
                    u = 2 * b + 1 if name[3] == "1" else 2 * b + 2
                    wait(act, rows_made, u)
                    nc.scalar.copy(nrow[:], c.bank[7][0:UH * NT, 0:P]).then_inc(job_taken, 1)

            def normalize(b):
                act.wait_ge(rstd_ready, b + 1)
                wait(act, x1_ready, 2 * b)
                for t in range(NT):
                    ins = nc.scalar.activation(norm[:, t], res[:, t], ACT.Identity, scale=rstd[:, t:t + 1], bias=shift[:, t:t + 1])
                ins.then_inc(norm_ready, 1)

            def out_copy(g, half):
                act.wait_ge(pv_done, 4 * (g + 1))
                wait(act, recip_done, g - 1)
                nc.scalar.copy(oT[:, half], c.bank[6][:]).then_inc(oT_ready, 1)

            job("neg0+", 0, -1)

            def body(b, first=False, last=False):
                jobs = Jobs(b, first, last)
                for s in range(STEPS_B):
                    wait(act, pv_done, 16 * b + s - 1)
                    for pair in range(2):
                        act.wait_ge(s2_ready, 2 * (16 * b + s) + pair + 1)
                        nc.scalar.activation(probs[:, s % 2, 2 * pair:2 * pair + 2], c.psum[:, 2 + 2 * pair:4 + 2 * pair],
                                             ACT.Exp, scale=SCALE).then_inc(exp_done, 1)
                    if s % 4 == 0 and not (first and s == 0):
                        out_copy(4 * b + s // 4 - 1, (s // 4 - 1) % 2)
                    for name, n in jobs.of[s]:
                        job(name, n, b)
                    if s == 10 and not first:
                        normalize(b - 1)

            body(0, first=True)
            with act.Fori(0, (B - 2) // 2) as i:
                body(2 * i + 1)
                body(2 * i + 2)
            body(B - 1, last=True)
            out_copy(4 * B - 1, 1)
            jobs = Jobs(B, tail=True)
            for s in range(STEPS_B):
                for name, n in jobs.of[s]:
                    job(name, n, B)
            normalize(B - 1)

        @block.vector
        def _(dve):

            def maxima(b, hf, head, tiles=range(NT)):
                n = (2 * b + hf) * UH * NT + head * NT
                for t in tiles:
                    dve.wait_ge(s1_ready, n + t + 1)
                    nc.vector.tensor_reduce(nmax[:, hf, head * NT + t:head * NT + t + 1], c.bank[t % 2], axis=AX.X,
                                            op=ALU.max, negate=True).then_inc(max_done, 1)

            def group(name, n, b):
                g = int(name[2])
                dve.wait_ge(job_ready, n + 1)
                o = c.bank[7].rearrange("p (t j e) -> p t j e", t=NT, j=4)
                nc.vector.reciprocal(rsum[:], o[:, :, :, HD]).then_inc(recip_done, 1)
                dve.wait_ge(recip_done, 4 * b + g + 1 - (4 if name[-1] == "-" else 0))
                nc.vector.tensor_tensor(
                    attn[:, :, bass.ts(g, 4 * HD)].rearrange("p t (j e) -> p t j e", j=4),
                    o[:, :, :, 0:HD], rsum[:].unsqueeze(3).to_broadcast([P, NT, 4, HD]), ALU.mult).then_inc(job_taken, 1)

            def job(name, n, b, p):
                if name[:2] == "OT":
                    group(name, n, b)
                elif name == "cnt-":
                    step = Steps(dve, dve_step, CHAIN * b - 4)
                    dve.wait_ge(job_ready, n + 1)
                    nc.vector.tensor_tensor(at[:], c.bank[7][:, 0:NT * E].rearrange("p (t e) -> p t e", t=NT),
                                            c.e_row[:].unsqueeze(1).to_broadcast([P, NT, E]), ALU.add).then_inc(job_taken, 1)
                    dve.wait_ge(job_taken, n + 1)
                    step.then(nc.vector.tensor_tensor(at[:], at[:], hot[:], ALU.mult))
                    step.then(nc.vector.tensor_reduce(pos[:], at[:], axis=AX.X, op=ALU.add))
                    step.then(nc.vector.tensor_scalar(pos[:], pos[:], -1.0, None, ALU.add))
                    nc.vector.tensor_copy(c.pos_i[:, bass.ds(NT * b - NT, NT)], pos[:]).then_inc(pos_ready, 1)
                    step.then(nc.vector.tensor_copy(c.seen[:, 0], c.seen[:, NT]))

            def finish(b, s, half):
                v = nc.vector
                if (s, half) == (9, 0):
                    dve.wait_ge(res_done, 2 * b + 2)
                    for t in range(NT):
                        ins = v.bn_stats(stats[:, t], res[:, t])
                    Steps(dve, dve_step, CHAIN * b).then(ins, core)
                if (s, half) == (9, 1):
                    for t in range(NT):
                        ins = v.bn_aggr(mv[:, t], stats[:, t])
                    Steps(dve, dve_step, CHAIN * b + 1).then(ins)
                    v.tensor_scalar(minus_mean[:], mv[:, :, 0], -1.0, None, ALU.mult)
                    v.tensor_scalar(ve[:], mv[:, :, 1], EPS, None, ALU.add).then_inc(ve_ready, 1)
                if (s, half) == (13, 0):
                    dve.wait_ge(x1_ready, 2 * b + 2)
                    for t in range(NT):
                        ins = v.tensor_tensor_reduce(out=norm[:, t], in0=x1[:, t], in1=rw[:], scale=1.0, scalar=0.0,
                                                     op0=ALU.mult, op1=ALU.add, accum_out=kt[:, t:t + 1])
                    ins.then_inc(dve_step, 1)
                if (s, half) == (13, 1):
                    dve.wait_ge(dve_step, CHAIN * b + 3)
                    step = Steps(dve, dve_step, CHAIN * b + 3)
                    step.then(v.tensor_scalar(keys[:], kt[:], rb[:], None, ALU.add))
                    step.then(v.tensor_copy(whole[:], keys[:]))
                    v.tensor_copy(fl[:], whole[:]).then_inc(dve_step, 1)
                if (s, half) == (14, 0):
                    dve.wait_ge(dve_step, CHAIN * b + 6)
                    step = Steps(dve, dve_step, CHAIN * b + 6)
                    step.then(v.tensor_tensor(above[:], fl[:], keys[:], ALU.is_gt))
                    step.then(v.tensor_tensor(fl[:], fl[:], above[:], ALU.subtract))
                    step.then(v.tensor_copy(whole[:], fl[:]))
                    v.tensor_scalar(whole[:], whole[:], E - 1, None, ALU.bitwise_and).then_inc(dve_step, 1)
                if (s, half) == (14, 1):
                    dve.wait_ge(dve_step, CHAIN * b + 10)
                    step = Steps(dve, dve_step, CHAIN * b + 10)
                    step.then(v.tensor_copy(fl[:], whole[:]))
                    step.then(v.tensor_tensor(hot[:], fl[:].unsqueeze(2).to_broadcast([P, NT, E]),
                                              c.e_num[:].unsqueeze(1).to_broadcast([P, NT, E]), ALU.is_equal))
                    step.then(v.tensor_tensor(c.seen[:, 1], c.seen[:, 0], hot[:, 0], ALU.add))
                    v.tensor_tensor(c.seen[:, 2], c.seen[:, 1], hot[:, 1], ALU.add).then_inc(dve_step, 1)
                if (s, half) == (15, 0):
                    dve.wait_ge(dve_step, CHAIN * b + 14)
                    step = Steps(dve, dve_step, CHAIN * b + 14)
                    step.then(v.tensor_tensor(c.seen[:, 3], c.seen[:, 2], hot[:, 2], ALU.add))
                    v.tensor_tensor(c.seen[:, 4], c.seen[:, 3], hot[:, 3], ALU.add).then_inc(hot_ready, 1)

            CHAIN = 2 + 10 + NT - 1 + 4
            for head in range(UH):
                maxima(0, 0, head)
            for head in range(AHEAD):
                maxima(0, 1, head)

            def body(b, p, first=False, last=False):
                jobs = Jobs(b, first, last)
                for s in range(STEPS_B):
                    w = AHEAD + s - UH
                    for half in range(2):
                        tiles = (2 * half, 2 * half + 1)
                        if w < 0:
                            maxima(b, 1, AHEAD + s, tiles)
                        elif not last:
                            maxima(b + 1, w // UH, w % UH, tiles)
                        for name, n in jobs.of[s - 1] if half == 0 and s > 0 else ():
                            job(name, n, b, p)
                        if not first:
                            finish(b - 1, s, half)
                for name, n in jobs.of[STEPS_B - 1]:
                    job(name, n, b, p)

            body(0, 0, first=True)
            with dve.Fori(0, (B - 2) // 2) as i:
                body(2 * i + 1, 1)
                body(2 * i + 2, 0)
            body(B - 1, 1, last=True)
            jobs = Jobs(B, tail=True)
            for s in range(STEPS_B):
                for name, n in jobs.of[s]:
                    if name != "cnt-":
                        job(name, n, B, 0)
                for half in range(2):
                    finish(B - 1, s, half)
                if s in (2, 3, 9, 10):
                    if s == 2:
                        dve.wait_ge(s2_ready, 32 * B)
                        dve.wait_ge(c.exp_w["w_in"], 16 * E)
                    e = (2, 3, 9, 10).index(s)
                    nc.vector.tensor_scalar(masked_w1(core, I32)[:, e], c.exp_w["w1"][:, e].bitcast(I32), -(1 << 12), None,
                                            ALU.bitwise_and).then_inc(c.exp_w["leading"], 1)
            job("cnt-", jobs.number["cnt-"], B, 0)

        @block.gpsimd
        def _(pool):
            nc.gpsimd.memset(ks[KS:KM], 1.0).then_inc(set_up, 1)
            pool.wait_ge(w_in, 6 * 16)

            def rows(u, b, hf, p):
                step = Steps(pool, pool_step, 3 * u)
                ord_ = 0 if isinstance(b, int) and b == 0 and hf == 0 else JOBS_B * (b - 1) + 6 + (2 if hf else 8 - JOBS_B)
                if isinstance(b, int) and b == 0 and hf == 1:
                    ord_ = 1
                if isinstance(b, int) and b == 1 and hf == 0:
                    ord_ = 4
                pool.wait_ge(job_taken, ord_ + 1)
                wait(pool, rows_in[hf], 16 * b)
                step.then(nc.gpsimd.tensor_tensor(nparts[:, 0], nrow[:], c.ones[0:UH * NT], ALU.mult))
                step.then(nc.gpsimd.tensor_tensor(nrest[:], nrow[:], nparts[:, 0], ALU.subtract))
                step.then(nc.gpsimd.tensor_tensor(nparts[:, 1], nrest[:], c.ones[0:UH * NT], ALU.mult))
                nc.gpsimd.tensor_tensor(nparts[:, 2], nrest[:], nparts[:, 1], ALU.subtract).then_inc(rows_made, 1)
                pool.wait_ge(rows_made, u + 1)
                settle(core, nc.gpsimd)
                pool.dma_start(c.rows_dram[hf].rearrange("a r q -> r a q"), nparts[:]).then_inc(rows_out, 16)
                pool.wait_ge(rows_out, 16 * (u + 1))
                settle(core, nc.gpsimd)
                pool.dma_start(qs[KS:KM, 2 * p + hf].rearrange("a h t -> a (h t)"),
                               c.rows_dram[hf].rearrange("a r q -> a (r q)")).then_inc(rows_in[hf], 16)

            def add_bias(b):
                pool.wait_ge(xn_in, 16 * (b + 1))
                nc.gpsimd.tensor_tensor(xnb[:], xnb[:], bo[:].unsqueeze(1).to_broadcast([P, NT, D]),
                                        ALU.add).then_inc(xnb_ready, 1)

            def finish(b, jobs):
                pool.wait_ge(xnb_ready, b + 1)
                for half in range(2):
                    pool.wait_ge(job_taken, jobs.number[f"Wo{half}-"] + 1)
                    rows_of = slice(2 * half, 2 * half + 2)
                    nc.gpsimd.tensor_tensor(res[:, rows_of], res[:, rows_of], xnb[:, rows_of], ALU.add).then_inc(res_done, 1)
                pool.wait_ge(ve_ready, b + 1)
                wait(pool, norm_ready, b)
                nc.gpsimd.tensor_tensor(rstd[:], ve[:], c.neg_half[:, 0:NT], ALU.pow).then_inc(rstd_made, 1)
                pool.wait_ge(rstd_made, b + 1)
                nc.gpsimd.tensor_tensor(shift[:], minus_mean[:], rstd[:], ALU.mult).then_inc(rstd_ready, 1)
                pool.wait_ge(norm_ready, b + 1)
                wait(pool, scattered, 16 * NT * b)
                nc.gpsimd.tensor_tensor(x1[:], norm[:], g1[:].unsqueeze(1).to_broadcast([P, NT, D]), ALU.mult).then_inc(x1_ready, 1)
                pool.wait_ge(x1_ready, 2 * b + 1)
                nc.gpsimd.tensor_tensor(x1[:], x1[:], b1[:].unsqueeze(1).to_broadcast([P, NT, D]), ALU.add).then_inc(x1_ready, 1)

            def scatter(b):
                wait(pool, scattered, 16 * NT * b)
                pool.wait_ge(pos_ready, b + 1)
                settle(core, nc.gpsimd)
                nc.gpsimd.tensor_copy(idx[:], c.pos_i[:, bass.ts(b, NT)]).then_inc(idx_done, 1)
                pool.wait_ge(idx_done, b + 1)
                pool.wait_ge(x1_ready, 2 * b + 2)
                settle(core, nc.gpsimd)
                for t in range(NT):
                    pool.indirect_dma_start(c.xg_dram, bass.IndirectOffsetOnAxis(ap=idx[:, t:t + 1], axis=0),
                                            x1[:, t], None).then_inc(scattered, 16)

            rows(0, 0, 0, 0)

            def body(b, p, q, first=False, last=False):
                rows(2 * b + 1, b, 1, p)
                if not first:
                    finish(b - 1, Jobs(b, first, last))
                add_bias(b)
                if not last:
                    rows(2 * b + 2, b + 1, 0, 1 - p)
                if not first:
                    scatter(b - 1)

            body(0, 0, 0, first=True)
            with pool.Fori(0, (B - 2) // 2) as i:
                body(2 * i + 1, 1, i)
                body(2 * i + 2, 0, i + 1)
            body(B - 1, 1, B // 2 - 1, last=True)
            finish(B - 1, Jobs(B, tail=True))
            scatter(B - 1)
            pool.wait_ge(scattered, 16 * NT * B)


def prepare(core):
    nc, c, d = core.nc, core, core.i
    with ExitStack() as ctx:
        sb = lambda name, shape, dt=FP32: core.sb(name, shape, dt, ctx)
        sem = lambda name: core.sem(name, ctx)
        zeros = sb("zeros", [P, D])
        count = sb("count", [P, E])
        end_row = sb("end_row", [P, E])
        end_i = sb("end_i", [P, E], I32)
        caps = sb("caps", [P, E])
        caps_i = sb("caps_i", [P, E], I32)
        skip = sb("skip", [P, E])
        start = sb("start", [P, E])
        first_i = sb("first_i", [P, ETILES], I32)
        first = sb("first", [P, ETILES])
        past = sb("past", [P, E, ETILES])
        which = sb("which", [P, ETILES])
        pos = sb("pos_t", [P, TILES])
        beyond = sb("beyond", [P, E, TILES])
        step_sem = sem("step_t")
        iota_done = sem("iota_done")
        zeroed = sem("zeroed")
        counted = sem("counted")
        end_ready = sem("end_ready")
        tails = sem("tails")
        rows_ready = sem("rows_ready")
        win, wc2, wout, b_row, bz, bB, bC, d_row, a_hi, a_lo = (
            c.mam["win"], c.mam["wc2"], c.mam["wout"], c.mam["b_row"], c.mam["bz"], c.mam["bB"], c.mam["bC"], c.mam["d_row"], c.mam["a_hi"], c.mam["a_lo"])
        Z0, X0, B0, C0, DT0 = 0, INNER, 2 * INNER, 2 * INNER + STATE, 2 * INNER + 2 * STATE
        g_ln, be_ln = sb("g_lnm", [P, KD]), sb("be_lnm", [P, KD])
        be_wide = sb("be_wide", [P, KD, P])
        b_in_row = sb("b_in_row", [P, PROJ - INNER])
        dtb = sb("dtb", [P, HEADS])
        dtb_in = sb("dtb_in", [P, HEADS])
        bz_in, bB_in, bC_in = sb("bz_in", [P, JI]), sb("bB_in", [STATE, 1]), sb("bC_in", [P, 1])
        a_row = sb("a_row", [P, HEADS])
        sp_a, sp_b, sp_c, sp_d, sp_e = (sb(f"sp{n}", [P, TILES, HEADS]) for n in range(5))
        v_in, set_step, set_act = sem("vectors_in"), sem("set_step"), sem("set_act")
        bias_mm, h_step = sem("bias_mm"), sem("set_chain")
        VECTORS = 10
        block = ctx.enter_context(nc.Block())

        @block.gpsimd
        def _(pool):
            nc.gpsimd.iota(first_i[:], pattern=[[P, ETILES]], base=0, channel_multiplier=0).then_inc(iota_done, 1)
            nc.gpsimd.memset(zeros[:], 0.0).then_inc(zeroed, 1)
            w1 = c.exp_w["w1"]
            pool.wait_ge(c.exp_w["leading"], E)
            for e in range(E):
                nc.gpsimd.tensor_tensor(w1[:, e].bitcast(FP32R), w1[:, e], masked_w1(core, FP32)[:, e], ALU.subtract).then_inc(c.exp["w1_rest"], 1)

        @block.tensor
        def _(pe):
            nc.tensor.matmul(c.bank[0][:, 0:E], c.ones[:], c.seen[:, NT], start=True, stop=True).then_inc(counted, 1)
            pe.wait_ge(c.mam["w_in"], 16 * 4)
            pe.wait_ge(v_in, 16 * VECTORS)
            pe.wait_ge(set_step, 1)
            mm = nc.tensor.matmul
            for k in range(KD):
                mm(c.bank[1], be_wide[:, k], win[:, k, X0:X0 + INNER], start=k == 0, stop=k == 1)
            for k in range(KD):
                mm(c.bank[2][:, 0:STATE], be_wide[:, k], win[:, k, B0:B0 + STATE], start=k == 0, stop=k == 1)
            for k in range(KD):
                mm(c.bank[2][:, 64:64 + HEADS], be_wide[:, k], win[:, k, DT0:PROJ], start=k == 0, stop=k == 1)
            for j in range(JI):
                for k in range(KD):
                    mm(c.bank[3][:, j:j + 1], win[:, k, bass.ts(j, P)], be_ln[:, k:k + 1], start=k == 0, stop=k == 1)
            for k in range(KD):
                mm(c.bank[3][0:STATE, 8:9], win[:, k, B0:B0 + STATE], be_ln[:, k:k + 1], start=k == 0, stop=k == 1)
            for k in range(KD):
                ins = mm(c.bank[3][:, 9:10], wc2[:, k], be_ln[:, k:k + 1], start=k == 0, stop=k == 1)
            ins.then_inc(bias_mm, 1)

        @block.scalar
        def _(act):
            for e in range(E):
                act.wait_ge(c.exp_w["leading"], e + 1)
                nc.scalar.copy(w1_leading(core)[:, e], masked_w1(core, FP32)[:, e]).then_inc(c.exp["w1_typed"], 1)
            act.wait_ge(v_in, 16 * VECTORS)
            nc.scalar.activation(a_row[:], a_row[:], ACT.Exp).then_inc(set_act, 1)
            act.wait_ge(set_step, 2)
            nc.scalar.activation(sp_b[:], sp_b[:], ACT.Exp).then_inc(set_act, 1)
            act.wait_ge(set_step, 3)
            nc.scalar.activation(sp_d[:], sp_c[:], ACT.Ln).then_inc(set_act, 1)

        @block.sync
        def _(sp):
            ld = lambda dst, src: sp.dma_start(dst, src).then_inc(v_in, 16)
            b_in = d["L0_attn_b_in"]
            with nc.allow_non_contiguous_dma(reason="small vectors"):
                ld(g_ln[:], d["L0_attn_ln_gamma"].rearrange("(k p) -> p k", p=P))
                ld(be_ln[:], d["L0_attn_ln_beta"].rearrange("(k p) -> p k", p=P))
                ld(bz_in[:], b_in[Z0:Z0 + INNER].rearrange("(k p) -> p k", p=P))
                ld(bB_in[:], b_in[B0:B0 + STATE].rearrange("(p o) -> p o", o=1))
                for half in range(2):
                    ld(bC_in[STATE * half:STATE * half + STATE], b_in[C0:C0 + STATE].rearrange("(p o) -> p o", o=1))
            ld(b_in_row[:], row(b_in[INNER:PROJ]))
            ld(dtb_in[:], row(d["L0_attn_dt_bias"]))
            ld(a_row[:], row(d["L0_attn_A_log"]))
            ld(d_row[:], row(d["L0_attn_D_skip"]))
            sp.wait_ge(zeroed, 1)
            sp.wait_ge(end_ready, 1)
            for e in range(E):
                r = sp.value_load(end_i[0:1, e:e + 1], min_val=0, max_val=E * REGION - TAIL)
                sp.dma_start(c.xg_dram[bass.ds(r, TAIL)].rearrange("(t p) d -> p t d", p=P),
                             zeros[:].unsqueeze(1).to_broadcast([P, TAIL // P, D])).then_inc(tails, 16)
            for e in range(E):
                sp.dma_start(c.exp["b1"][:, e], row(d["L0_ffn_b1"][e])).then_inc(c.exp["b_in"], 16)
                sp.dma_start(c.exp["b2"][:, e], row(d["L0_ffn_b2"][e])).then_inc(c.exp["b_in"], 16)
            sp.dma_start(c.exp["g2"][:], row(d["L0_ffn_ln2_g"])).then_inc(c.exp["b_in"], 16)
            sp.dma_start(c.exp["be2"][:], row(d["L0_ffn_ln2_b"])).then_inc(c.exp["b_in"], 16)
            sp.wait_ge(tails, 16 * E)
            sp.wait_ge(rows_ready, 1)
            for i in range(3):
                load_rows(core, sp, first_row(core, sp, i), i)
            for e in range(E):
                sp.dma_start(c.exp["w2"][:, e], d["L0_ffn_W2"][e].rearrange("(k p) n -> p k n", p=P)).then_inc(c.exp["w2_in"], 16)
            sp.wait_ge(v_in, 16 * VECTORS)

        @block.vector
        def _(dve):
            v = nc.vector
            step = Steps(dve, step_sem, 0)
            dve.wait_ge(counted, 1)
            step.then(v.tensor_copy(count[:], c.bank[0][:, 0:E]))
            step.then(v.tensor_tensor(end_row[:], count[:], c.e_row[:], ALU.add))
            v.tensor_copy(end_i[:], end_row[:]).then_inc(end_ready, 1)
            step.then(v.tensor_scalar(caps[:], count[:], float(P - 1), None, ALU.add))
            step.then(v.tensor_copy(caps_i[:], caps[:]))
            step.then(v.tensor_scalar(caps_i[:], caps_i[:], -P, None, ALU.bitwise_and))
            step.then(v.tensor_copy(caps[:], caps_i[:]))
            step.then(v.tensor_scalar(skip[:], caps[:], -1.0, float(REGION), ALU.mult, ALU.add))
            step.then(v.memset(start[:], 0.0))
            for e in range(1, E):
                step.then(v.tensor_tensor(start[:, e:e + 1], start[:, e - 1:e], caps[:, e - 1:e], ALU.add))
            dve.wait_ge(v_in, 16 * VECTORS)
            v.tensor_copy(be_wide[:], be_ln[:].unsqueeze(2).to_broadcast([P, KD, P])).then_inc(set_step, 1)
            dve.wait_ge(iota_done, 1)
            step.then(v.tensor_copy(first[:], first_i[:]))
            for e in range(1, E):
                ins = v.tensor_scalar(past[:, e], first[:], start[:, e:e + 1], None, ALU.is_ge)
            step.then(ins)
            step.then(v.tensor_reduce(which[:], past[:, 1:E].rearrange("p e t -> p t e"), axis=AX.X, op=ALU.add))
            step.then(v.tensor_copy(c.which_i[:], which[:]))
            for e in range(1, E):
                step.then(v.tensor_scalar(past[:, e], past[:, e], skip[:, e - 1:e], None, ALU.mult))
                step.then(v.tensor_tensor(first[:], first[:], past[:, e], ALU.add))
            v.tensor_copy(c.row_i[:], first[:]).then_inc(rows_ready, 1)
            step.then(v.tensor_copy(pos[:], c.pos_i[:]))
            for e in range(1, E):
                ins = v.tensor_scalar(beyond[:, e], pos[:], float(e * REGION), skip[:, e - 1:e], ALU.is_ge, ALU.mult)
            step.then(ins)
            for e in range(1, E):
                step.then(v.tensor_tensor(pos[:], pos[:], beyond[:, e], ALU.subtract))
            step.then(v.tensor_copy(c.pos_y[:], pos[:]))
            dve.wait_ge(bias_mm, 1)
            v.tensor_tensor(b_row[:, 0:INNER], c.bank[1], b_in_row[:, 0:INNER], ALU.add)
            v.tensor_tensor(b_row[:, INNER:], c.bank[2][:, 0:STATE], b_in_row[:, INNER:INNER + STATE], ALU.add)
            v.tensor_tensor(dtb[:], c.bank[2][:, 64:64 + HEADS], b_in_row[:, PROJ - INNER - HEADS:], ALU.add)
            v.tensor_tensor(bz[:], c.bank[3][:, 0:JI], bz_in[:], ALU.add)
            v.tensor_tensor(bB[:], c.bank[3][0:STATE, 8:9], bB_in[:], ALU.add)
            v.tensor_tensor(bC[:], c.bank[3][:, 9:10], bC_in[:], ALU.add)
            for k in range(KD):
                v.tensor_scalar(win[:, k], win[:, k], g_ln[:, k:k + 1], None, ALU.mult)
                v.tensor_scalar(wc2[:, k], wc2[:, k], g_ln[:, k:k + 1], None, ALU.mult)
            step = Steps(dve, h_step, 0)
            step.then(v.tensor_scalar(wout[:], wout[:], 0.5, None, ALU.mult))
            step.then(v.tensor_tensor(dtb[:], dtb[:], dtb_in[:], ALU.add))
            step.then(v.tensor_tensor(sp_a[:], c.dt_all[:], dtb[:].unsqueeze(1).to_broadcast([P, TILES, HEADS]), ALU.add))
            step.then(v.tensor_scalar(sp_b[:], sp_a[:], -1.0, None, ALU.mult))
            v.tensor_tensor(sp_b[:], sp_b[:], sp_a[:], ALU.min).then_inc(set_step, 1)
            dve.wait_ge(set_act, 2)
            v.tensor_scalar(sp_c[:], sp_b[:], 1.0, None, ALU.add).then_inc(set_step, 1)
            dve.wait_ge(set_act, 3)
            step.then(v.tensor_scalar(sp_c[:], sp_c[:], -1.0, None, ALU.add))
            step.then(v.tensor_scalar(sp_e[:], sp_c[:], 0.0, None, ALU.is_equal))
            step.then(v.tensor_tensor(sp_c[:], sp_c[:], sp_e[:], ALU.add))
            step.then(v.reciprocal(sp_c[:], sp_c[:]))
            step.then(v.tensor_tensor(sp_d[:], sp_d[:], sp_e[:], ALU.add))
            step.then(v.tensor_tensor(sp_d[:], sp_d[:], sp_c[:], ALU.mult))
            step.then(v.tensor_tensor(sp_d[:], sp_d[:], sp_b[:], ALU.mult))
            step.then(v.tensor_scalar(sp_a[:], sp_a[:], 0.0, None, ALU.max))
            step.then(v.tensor_tensor(c.dt_all[:], sp_a[:], sp_d[:], ALU.add))
            step.then(v.tensor_scalar(a_row[:], a_row[:], -1.0, None, ALU.mult))
            step.then(v.tensor_tensor(sp_a[:], c.dt_all[:], a_row[:].unsqueeze(1).to_broadcast([P, TILES, HEADS]), ALU.mult))
            step.then(v.tensor_scalar(a_hi[:].bitcast(I32), sp_a[:].bitcast(I32), -(1 << 12), None, ALU.bitwise_and))
            step.then(v.tensor_tensor(a_lo[:], sp_a[:], a_hi[:], ALU.subtract))


def first_row(core, sp, i):
    return sp.value_load(core.row_i[0:1, bass.ds(i, 1)], min_val=0, max_val=E * REGION - P)


def load_rows(core, sp, r, n):
    sp.dma_start(core.exp["xg"][:, n], core.xg_dram[bass.ds(r, P)]).then_inc(core.exp["xg_in"][n], 16)


def experts(core):
    nc, c, d = core.nc, core, core.i
    with ExitStack() as ctx:
        sb = lambda name, shape, dt=FP32: core.sb(name, shape, dt, ctx)
        sem = lambda name: core.sem(name, ctx)
        NH, KF = FF // 512, FF // P
        w1, w2 = c.exp_w["w1"], c.exp["w2"]
        b1, b2, g2, be2, xg, xg_in = c.exp["b1"], c.exp["b2"], c.exp["g2"], c.exp["be2"], c.exp["xg"], c.exp["xg_in"]
        xgT = sb("xgT", [P, 2, KD, P])
        x_masked = lambda dt: masked_w1(core, dt)[:, 0, :, 0:2 * P].rearrange("p k (n q) -> p n k q", n=2)
        x_parts = c.att["v"][:].rearrange("p a b e -> p (a b e)")[:, 0:2 * 2 * KD * P].bitcast(FP32R).rearrange(
            "p (n a k q) -> p n a k q", n=2, a=2, k=KD)
        h = sb("h", [P, FF])
        hT = sb("hT", [P, KF, P])
        res = sb("res_e", [P, D])
        stats, mv = sb("stats_e", [P, 6]), sb("mv_e", [P, 2])
        ve, rstd = sb("ve_e", [P, 1]), sb("rstd_e", [P, 1])
        norm = sb("norm_e", [P, 2, D])
        y = sb("y_e", [P, 2, D])
        x_t, x_tk = sem("x_t"), sem("x_tk")
        x_leading, x_split, x_parted = sem("x_leading"), sem("x_split"), sem("x_parted")
        h_mm, h_sb = sem("h_mm"), sem("h_sb")
        h_t, h_tk = sem("h_t"), sem("h_tk")
        y_mm, y_tk = sem("y_mm"), sem("y_tk")
        dve_step = sem("step_e")
        ve_r, rstd_r, y_r = sem("ve_r"), sem("rstd_r"), sem("y_r")
        y_out = [sem("y_out0"), sem("y_out1")]
        block = ctx.enter_context(nc.Block())
        yg_t = c.yg_dram.rearrange("(i p) d -> i p d", p=P)
        UN = 4

        def loop(eng, body):
            for i in range(UN):
                body(i, i, 0)
            with eng.Fori(1, (ETILES - 3) // UN) as j:
                for n in range(UN):
                    body(UN * j + n, n, j)
            for i in range((ETILES - 3) // UN * UN, ETILES):
                body(i, i % UN, i // UN)

        @block.sync
        def _(sp):
            def body(i, n, j):
                more = not isinstance(i, int) or i + 3 < ETILES
                if more:
                    r = first_row(core, sp, i + 3)
                    wait(sp, dve_step, 4 * i - 3)
                    load_rows(core, sp, r, (n + 3) % UN)
                sp.wait_ge(y_r, 2 * i + 2)
                sp.dma_start(yg_t[i], y[:, n % 2]).then_inc(y_out[n % 2], 16)

            loop(sp, body)
            sp.wait_ge(y_out[0], 16 * ((ETILES + 1) // 2))
            sp.wait_ge(y_out[1], 16 * (ETILES // 2))

        @block.tensor
        def _(pe):
            def x_transposed(i, n, j):
                pe.wait_ge(xg_in[n], 16 * (j + 1))
                wait(pe, x_tk, i)
                for k in range(KD):
                    ins = nc.tensor.transpose(c.bank[0][:, bass.ts(k, P)], xg[:, n, bass.ts(k, P)], c.ident[:])
                ins.then_inc(x_t, 1)

            def up(i, n):
                e = pe.value_load(c.which_i[0:1, bass.ds(i, 1)], min_val=0, max_val=E - 1)
                pe.wait_ge(x_parted, i + 1)
                wait(pe, h_sb, 2 * i)
                for m in range(NH):
                    cols = bass.ts(m, 512)
                    for k in range(KD):
                        for x_part, w in ((0, w1_hi), (1, w1_hi), (0, w1_lo)):
                            ins = nc.tensor.matmul(c.bank[1 + m], x_parts[:, n % 2, x_part, k], w[:, bass.ds(e, 1), k, cols],
                                                   start=k + x_part == 0 and w is w1_hi, stop=k == KD - 1 and w is w1_lo)
                    ins.then_inc(h_mm, 1)

            def h_transposed(i):
                for m in range(2):
                    pe.wait_ge(h_sb, 2 * i + 1 + m)
                    wait(pe, h_tk, 2 * i - 1 + m)
                    for k in range(4):
                        ins = nc.tensor.transpose(c.bank[3 + m][:, bass.ts(k, P)], h[:, bass.ts(4 * m + k, P)], c.ident[:])
                    ins.then_inc(h_t, 1)

            def down(i):
                e = pe.value_load(c.which_i[0:1, bass.ds(i, 1)], min_val=0, max_val=E - 1)
                pe.wait_ge(h_tk, 2 * i + 2)
                wait(pe, y_tk, i)
                for k in range(KF):
                    ins = nc.tensor.matmul(c.bank[5][:, 0:D], hT[:, k], w2[:, bass.ds(e, 1), k], start=k == 0, stop=k == KF - 1)
                ins.then_inc(y_mm, 1)

            w1_hi, w1_lo = w1_leading(core), w1[:].bitcast(FP32R)
            pe.wait_ge(c.exp["w1_typed"], E)
            pe.wait_ge(c.exp["w1_rest"], E)
            x_transposed(0, 0, 0)
            up(0, 0)
            x_transposed(1, 1, 0)
            pe.wait_ge(c.exp["w2_in"], 16 * E)

            def body(i, n, j):
                h_transposed(i)
                if not isinstance(i, int) or i + 1 < ETILES:
                    up(i + 1, n + 1)
                if not isinstance(i, int) or i + 2 < ETILES:
                    x_transposed(i + 2, (n + 2) % UN, j + (n + 2) // UN)
                down(i)

            loop(pe, body)

        @block.scalar
        def _(act):

            def x_copy(i, n):
                act.wait_ge(x_t, i + 1)
                nc.scalar.copy(xgT[:, n % 2], c.bank[0][:, 0:KD * P].rearrange("p (k q) -> p k q", k=KD)).then_inc(x_tk, 1)
                act.wait_ge(x_split, i + 1)
                nc.scalar.copy(x_parts[:, n % 2, 0], x_masked(FP32)[:, n % 2]).then_inc(x_parted, 1)

            x_copy(0, 0)
            x_copy(1, 1)

            def body(i, n, j):
                for m in range(2):
                    act.wait_ge(h_t, 2 * i + 1 + m)
                    wait(act, y_mm, i)
                    nc.scalar.activation(hT[:, 4 * m:4 * m + 4], c.bank[3 + m].rearrange("p (k q) -> p k q", k=4),
                                         ACT.Relu).then_inc(h_tk, 1)
                if not isinstance(i, int) or i + 2 < ETILES:
                    x_copy(i + 2, n + 2)

            loop(act, body)

        @block.vector
        def _(dve):
            dve.wait_ge(c.exp["b_in"], 16 * (2 * E + 2))

            def bias(i):
                e = dve.value_load(c.which_i[0:1, bass.ds(i, 1)], min_val=0, max_val=E - 1)
                for m in range(NH):
                    dve.wait_ge(h_mm, 2 * i + 1 + m)
                    wait(dve, h_t, 2 * i - 1 + m)
                    nc.vector.tensor_tensor(h[:, bass.ts(m, 512)].unsqueeze(1), c.bank[1 + m].unsqueeze(1),
                                            b1[:, bass.ds(e, 1), bass.ts(m, 512)], ALU.add).then_inc(h_sb, 1)

            def tail(i, n):
                e = dve.value_load(c.which_i[0:1, bass.ds(i, 1)], min_val=0, max_val=E - 1)
                step = Steps(dve, dve_step, 4 * i)
                dve.wait_ge(y_mm, i + 1)
                nc.vector.tensor_tensor(res[:].unsqueeze(1), c.bank[5][:, 0:D].unsqueeze(1), b2[:, bass.ds(e, 1)],
                                        ALU.add).then_inc(y_tk, 1)
                dve.wait_ge(y_tk, i + 1)
                step.then(nc.vector.tensor_tensor(res[:], res[:], xg[:, n], ALU.add))
                step.then(nc.vector.bn_stats(stats[:], res[:]), core)
                step.then(nc.vector.bn_aggr(mv[:], stats[:]))
                nc.vector.tensor_scalar(ve[:], mv[:, 1:2], EPS, None, ALU.add).then_inc(ve_r, 1)
                dve.wait_ge(rstd_r, i + 1)
                wait(dve, y_r, 2 * i - 2)
                step.then(nc.vector.tensor_scalar(norm[:, n % 2], res[:], mv[:, 0:1], rstd[:], ALU.subtract, ALU.mult))

            def split(i, n):
                dve.wait_ge(x_tk, i + 1)
                wait(dve, h_mm, 2 * i - 2)
                nc.vector.tensor_scalar(x_masked(I32)[:, n % 2], xgT[:, n % 2].bitcast(I32), -(1 << 12), None,
                                        ALU.bitwise_and).then_inc(x_leading, 1)
                dve.wait_ge(x_leading, i + 1)
                nc.vector.tensor_tensor(x_parts[:, n % 2, 1], xgT[:, n % 2], x_masked(FP32)[:, n % 2],
                                        ALU.subtract).then_inc(x_split, 1)

            split(0, 0)
            bias(0)
            split(1, 1)

            def body(i, n, j):
                if not isinstance(i, int) or i + 1 < ETILES:
                    bias(i + 1)
                if not isinstance(i, int) or i + 2 < ETILES:
                    split(i + 2, n + 2)
                tail(i, n)

            loop(dve, body)

        @block.gpsimd
        def _(pool):
            pool.wait_ge(c.exp["b_in"], 16 * (2 * E + 2))

            def body(i, n, j):
                pool.wait_ge(ve_r, i + 1)
                nc.gpsimd.tensor_tensor(rstd[:], ve[:], c.neg_half[:, 0:1], ALU.pow).then_inc(rstd_r, 1)
                pool.wait_ge(dve_step, 4 * i + 4)
                wait(pool, y_out[n % 2], 16 * (2 * j + n // 2))
                nc.gpsimd.tensor_tensor(y[:, n % 2], norm[:, n % 2], g2[:], ALU.mult).then_inc(y_r, 1)
                pool.wait_ge(y_r, 2 * i + 1)
                nc.gpsimd.tensor_tensor(y[:, n % 2], y[:, n % 2], be2[:], ALU.add).then_inc(y_r, 1)

            loop(pool, body)


def mamba(core):
    nc, c, d = core.nc, core, core.i
    with ExitStack() as ctx:
        sb = lambda name, shape, dt=FP32: core.sb(name, shape, dt, ctx)
        sem = lambda name: core.sem(name, ctx)
        X0, B0 = INNER, 2 * INNER
        win, wc2, wout, b_row, bz, bB, bC, d_row, a_hi, a_lo = (
            c.mam["win"], c.mam["wc2"], c.mam["wout"], c.mam["b_row"], c.mam["bz"], c.mam["bB"], c.mam["bC"], c.mam["d_row"], c.mam["a_hi"], c.mam["a_lo"])
        nxT = sb("nxT_m", [P, NT, KD, P])
        xr = sb("xr", [P, NT, 2, D])
        idx = sb("idx_m", [P, NT], U32)
        y_exp = sb("y_exp", [P, 2, D])
        resid = sb("resid", [P, 2, D])
        aU = sb("aU", [P, 2, 2, HEADS, P], FP32R)
        strict = sb("strict_r", [P, P], FP32R)
        ones = sb("ones_r", [P, 2, P], FP32R)
        xs = sb("xs", [P, INNER])
        Bs = sb("Bs", [P, 2, STATE])
        BT = sb("BT", [STATE, P])
        CT = sb("CT", [P, 2, P])
        z = sb("z", [P, JI, P])
        th = sb("th", [P, JI, P])
        gate = sb("gate", [P, 2, JI, P])
        L = sb("L", [P, 2, HEADS, P])
        E2 = sb("E2", [P, 2, JI, P])
        Gm = sb("Gm", [P, P])
        M = sb("M", [P, 2, HEADS, P])
        CE = sb("CE", [P, 2, JI, P])
        dtx = sb("dtx", [P, 2, HEADS, PW])
        wdtx = sb("wdtx", [P, 2, HEADS, PW])
        xsD = sb("xsD", [P, 2, HEADS, PW])
        Hs = sb("Hs", [P, JI, PW])
        HB = sb("HB", [P, JI, P])
        yg = sb("yg", [P, JI, P])
        r = sb("r_m", [P, 2, D])

        cleared = sem("cleared")
        b_out, b_out_in = sb("b_out_row", [P, D]), sem("b_out_in")
        nx_in = [sem(f"nx_in{n}") for n in range(NT)]
        xr_in = [sem(f"xr_in{n}") for n in range(NT)]
        aU_lo_r = sem("aU_lo_r")
        aU_r, resid_r, resid_s, wdtx_r, xsD_r = (sem(n) for n in ("aU_r", "resid_r", "resid_s", "wdtx_r", "xsD_r"))
        xs_mm, bc_mm, z_mm, cum_mm, e_mm, g_mm, y_mm, st_mm, out_mm = (
            sem(n) for n in ("xs_mm", "bc_mm", "z_mm", "cum_mm", "e_mm", "g_mm", "y_mm_m", "st_mm", "out_mm"))
        xs_r, bc_r, dtx_r, gate_r, Gm_r, M_r, CE_r, yg_r, h_step, h_r, r_r = (
            sem(n) for n in ("xs_r", "bc_r", "dtx_r", "gate_r", "Gm_r", "M_r", "CE_r", "yg_r", "h_step", "h_r", "r_r"))
        z_r, th_r, L_r, E_r, HB_r = (sem(n) for n in ("z_r", "th_r", "L_r", "E_r", "HB_r"))
        r_out = [sem("r_out0"), sem("r_out1")]
        idx_done = sem("idx_done_m")
        gathered = [sem("gathered0"), sem("gathered1")]
        block = ctx.enter_context(nc.Block())
        x_t = d["L0_attn_input_tensor"].rearrange("b (t p) d -> (b t) p d", p=P)
        xn_t = c.xn_dram.rearrange("(i p) d -> i p d", p=P)
        r_t = c.out.rearrange("b (t p) d -> (b t) p d", p=P)

        def chunks(eng, body):
            for n in range(NT):
                body(n, 0, n)
            with eng.Fori(1, B - 1) as b:
                for n in range(NT):
                    body(NT * b + n, b, n)
            for n in range(NT):
                body(NT * (B - 1) + n, B - 1, n)

        @block.sync
        def _(sp):
            def load(i, n):
                sp.dma_start(nxT[:, n], c.nxT_dram[:, :, bass.ts(i, P)].rearrange("k p t -> p k t")).then_inc(nx_in[n], 16)
                sp.dma_start(xr[:, n, 0], x_t[i]).then_inc(xr_in[n], 16)
                sp.dma_start(xr[:, n, 1], xn_t[i]).then_inc(xr_in[n], 16)

            for n in range(NT):
                load(n, n)
            sp.dma_start(b_out[:], row(d["L0_attn_b_out"])).then_inc(b_out_in, 16)

            def body(i, b, n):
                sp.wait_ge(r_r, i + 1)
                sp.dma_start(r_t[i], r[:, n % 2]).then_inc(r_out[n % 2], 16)
                if not isinstance(i, int) or i + NT < TILES:
                    sp.wait_ge(z_mm, i + 1)
                    sp.wait_ge(resid_s, 2 * i + 1)
                    load(i + NT, n)

            chunks(sp, body)
            for p in range(2):
                sp.wait_ge(r_out[p], 16 * TILES // 2)

        @block.tensor
        def _(pe):
            mm = nc.tensor.matmul

            def front(i, b, n):
                p = n % 2
                pe.wait_ge(nx_in[n], 16 * (b + 1))
                wait(pe, xs_r, i)
                for k in range(KD):
                    ins = mm(c.bank[0], nxT[:, n, k], win[:, k, X0:X0 + INNER], start=k == 0, stop=k == 1)
                ins.then_inc(xs_mm, 1)
                wait(pe, bc_r, i)
                wait(pe, Gm_r, i)
                for k in range(KD):
                    mm(c.bank[1][:, 0:STATE], nxT[:, n, k], win[:, k, B0:B0 + STATE], start=k == 0, stop=k == 1)
                for k in range(KD):
                    mm(c.bank[1][0:STATE, P:2 * P], win[:, k, B0:B0 + STATE], nxT[:, n, k], start=k == 0, stop=k == 1)
                for k in range(KD):
                    ins = mm(c.bank[1][:, 2 * P:3 * P], wc2[:, k], nxT[:, n, k], start=k == 0, stop=k == 1)
                ins.then_inc(bc_mm, 1)

            def front_z(i, n):
                p = n % 2
                wait(pe, z_r, i)
                for j in range(JI):
                    for k in range(KD):
                        ins = mm(c.bank[2][:, bass.ts(j, P)], win[:, k, bass.ts(j, P)], nxT[:, n, k], start=k == 0, stop=k == 1)
                ins.then_inc(z_mm, 1)
                pe.wait_ge(aU_r, i + 1)
                pe.wait_ge(aU_lo_r, i + 1)
                wait(pe, L_r, i)
                for half in range(2):
                    for part in range(2):
                        ins = mm(c.bank[4 + half], strict[:], aU[:, p, part, 4 * half:4 * half + 4],
                                 start=part == 0, stop=part == 1)
                ins.then_inc(cum_mm, 1)
                wait(pe, E_r, i)
                for odd in range(2):
                    for part in range(2):
                        ins = mm(c.bank[6], ones[:, odd], aU[:, p, part, odd:HEADS:2],
                                 start=odd + part == 0, stop=odd + part == 2)
                ins.then_inc(e_mm, 1)

                pe.wait_ge(bc_r, i + 1)
                mm(c.bank[1][:, 3 * P:4 * P], BT[:], CT[0:STATE, n % 2], start=True, stop=True).then_inc(g_mm, 1)

            def back(i, b, n):
                p = n % 2
                pe.wait_ge(xsD_r, i + 1)
                pe.wait_ge(M_r, i + 1)
                pe.wait_ge(CE_r, i + 1)
                wait(pe, yg_r, i)
                if n > 0:
                    pe.wait_ge(HB_r, 2 * (3 * b + n))
                for j in range(JI):
                    out = c.bank[7][:, bass.ts(j, P)]
                    mm(out, xsD[:, p, 2 * j:2 * j + 2].rearrange("p h e -> p (h e)"), c.ident[:], start=True, stop=False)
                    if n > 0:
                        mm(out, HB[:, j], CE[:, p, j], start=False, stop=False)
                    for odd in range(2):
                        ins = mm(c.bank[7][PW * odd:PW * odd + PW, bass.ts(j, P)], dtx[:, p, 2 * j + odd], M[:, p, 2 * j + odd],
                                 start=False, stop=True)
                ins.then_inc(y_mm, 1)
                if n < NT - 1:
                    pe.wait_ge(wdtx_r, i + 1)
                    wait(pe, r_r, i)
                    for odd in range(2):
                        ins = mm(c.bank[3][STATE * odd:STATE * odd + STATE, 0:JI * PW], Bs[:, p],
                                 wdtx[:, p, odd:HEADS:2], start=True, stop=True)
                    ins.then_inc(st_mm, 1)

            def outs(i, b, n):
                pe.wait_ge(yg_r, i + 1)
                if n < NT - 1:
                    pe.wait_ge(h_r, 3 * b + n + 1)
                else:
                    wait(pe, r_r, i)
                for j in range(JI):
                    ins = mm(c.bank[3][:, D:2 * D], yg[:, j], wout[:, j], start=j == 0, stop=j == JI - 1)
                ins.then_inc(out_mm, 1)

            pe.wait_ge(cleared, 1)
            front(0, 0, 0)
            front_z(0, 0)

            def body(i, b, n):
                more = not isinstance(i, int) or i + 1 < TILES
                if more:
                    front(i + 1, b + (n + 1) // NT, (n + 1) % NT)
                back(i, b, n)
                if more:
                    front_z(i + 1, (n + 1) % NT)
                outs(i, b, n)

            chunks(pe, body)

        @block.scalar
        def _(act):
            def front(i, n):
                p = n % 2
                act.wait_ge(z_mm, i + 1)
                wait(act, gate_r, i)
                for j in range(JI):
                    ins = nc.scalar.activation(z[:, j], c.bank[2][:, bass.ts(j, P)], ACT.Identity, bias=bz[:, j:j + 1])
                ins.then_inc(z_r, 1)
                act.wait_ge(z_r, i + 1)
                nc.scalar.activation(th[:], z[:], ACT.Tanh, scale=0.5).then_inc(th_r, 1)
                act.wait_ge(cum_mm, i + 1)
                wait(act, M_r, i - 1)
                wait(act, wdtx_r, i - 1)
                nc.scalar.activation(L[:, p], c.psum[:, 4:6].rearrange("p a (h t) -> p (a h) t", t=P), ACT.Exp).then_inc(L_r, 1)
                act.wait_ge(e_mm, i + 1)
                wait(act, CE_r, i - 1)
                wait(act, h_r, h_before)
                nc.scalar.activation(E2[:, p], c.bank[6].rearrange("p (j t) -> p j t", t=P), ACT.Exp).then_inc(E_r, 1)

            act.wait_ge(cleared, 1)
            h_before = 0
            front(0, 0)

            def body(i, b, n):
                nonlocal h_before
                if n < NT - 1:
                    act.wait_ge(h_r, 3 * b + n + 1)
                    act.wait_ge(y_mm, i + 1)
                    for odd in range(2):
                        rows = slice(STATE * odd, STATE * odd + STATE)
                        nc.scalar.copy(HB[rows, :, bass.ts(odd, PW)], Hs[rows]).then_inc(HB_r, 1)
                if not isinstance(i, int) or i + 1 < TILES:
                    h_before = 3 * b + n if n < NT - 1 else 3 * b + NT - 1
                    front(i + 1, (n + 1) % NT)

            chunks(act, body)

        @block.vector
        def _(dve):
            v = nc.vector
            v.tensor_copy(strict[:], c.strict[:])
            v.memset(HB[:], 0.0).then_inc(h_step, 1)
            dve.wait_ge(h_step, 1)
            for odd in range(2):
                v.tensor_copy(ones[:, odd, bass.ts(odd, STATE)], c.ones[:, 0:STATE])
                ins = v.tensor_copy(ones[:, odd, bass.ts(1 - odd, STATE)], HB[:, 0, 0:STATE])
            ins.then_inc(cleared, 1)
            H0 = 1

            def front_a(i, n):
                p = n % 2
                wait(dve, e_mm, i - 1)
                v.tensor_tensor(aU[:, p, 1], c.upper[:].unsqueeze(1).to_broadcast([P, HEADS, P]),
                                a_lo[:, bass.ds(i, 1)].rearrange("p o h -> p (o h)").unsqueeze(2).to_broadcast([P, HEADS, P]),
                                ALU.mult).then_inc(aU_lo_r, 1)
                dve.wait_ge(xs_mm, i + 1)
                wait(dve, xsD_r, i)
                v.tensor_tensor(xs[:], c.bank[0], b_row[:, 0:INNER], ALU.add).then_inc(xs_r, 1)
                dve.wait_ge(bc_mm, i + 1)
                wait(dve, st_mm, st_before)
                wait(dve, g_mm, i)
                v.tensor_tensor(Bs[:, p], c.bank[1][:, 0:STATE], b_row[:, INNER:], ALU.add)
                v.tensor_scalar(BT[:], c.bank[1][0:STATE, P:2 * P], bB[:], None, ALU.add)
                v.tensor_scalar(CT[:, p], c.bank[1][:, 2 * P:3 * P], bC[:], None, ALU.add).then_inc(bc_r, 1)
                dve.wait_ge(xs_r, i + 1)
                wait(dve, y_mm, i - 1)
                v.tensor_tensor(dtx[:, p], xs[:].rearrange("p (h e) -> p h e", h=HEADS),
                                c.dt_all[:, bass.ds(i, 1)].rearrange("p o h -> p (o h)").unsqueeze(2).to_broadcast([P, HEADS, PW]),
                                ALU.mult).then_inc(dtx_r, 1)

            def front_b(i, n):
                p = n % 2
                dve.wait_ge(g_mm, i + 1)
                v.tensor_tensor(Gm[:], c.bank[1][:, 3 * P:4 * P], c.upper[:], ALU.mult).then_inc(Gm_r, 1)
                dve.wait_ge(Gm_r, i + 1)
                dve.wait_ge(L_r, i + 1)
                v.tensor_tensor(M[:, p], L[:, p], Gm[:].unsqueeze(1).to_broadcast([P, HEADS, P]), ALU.mult).then_inc(M_r, 1)
                dve.wait_ge(E_r, i + 1)
                v.tensor_tensor(CE[:, p], E2[:, p], CT[:, p].unsqueeze(1).to_broadcast([P, JI, P]), ALU.mult).then_inc(CE_r, 1)
                dve.wait_ge(th_r, i + 1)
                v.scalar_tensor_tensor(out=gate[:, p], in0=th[:], scalar=1.0, in1=z[:], op0=ALU.add,
                                       op1=ALU.mult).then_inc(gate_r, 1)

            st_before = 0
            front_a(0, 0)
            front_b(0, 0)

            def body(i, b, n):
                nonlocal st_before
                more = not isinstance(i, int) or i + 1 < TILES
                if more:
                    st_before = 3 * b + n
                    front_a(i + 1, (n + 1) % NT)
                dve.wait_ge(y_mm, i + 1)
                dve.wait_ge(gate_r, i + 1)
                wait(dve, out_mm, i)
                v.tensor_tensor(yg[:], c.bank[7].rearrange("p (j t) -> p j t", t=P), gate[:, n % 2], ALU.mult).then_inc(yg_r, 1)
                if n < NT - 1:
                    own = c.bank[3][:, 0:JI * PW].rearrange("p (j e) -> p j e", j=JI)
                    wait(dve, HB_r, 2 * (3 * b + n))
                    dve.wait_ge(st_mm, 3 * b + n + 1)
                    if n == 0:
                        v.tensor_copy(Hs[:], own).then_inc(h_r, 1)
                    else:
                        v.tensor_tensor(Hs[:], Hs[:], E2[:, n % 2, :, P - 1:P].to_broadcast([P, JI, PW]),
                                        ALU.mult).then_inc(h_step, 1)
                        dve.wait_ge(h_step, H0 + 2 * b + n)
                        v.tensor_tensor(Hs[:], Hs[:], own, ALU.add).then_inc(h_r, 1)
                if more:
                    front_b(i + 1, (n + 1) % NT)
                dve.wait_ge(out_mm, i + 1)
                dve.wait_ge(resid_r, i + 1)
                wait(dve, r_out[n % 2], 16 * (2 * b + n // 2))
                v.tensor_tensor(r[:, n % 2], c.bank[3][:, D:2 * D], resid[:, n % 2], ALU.add).then_inc(r_r, 1)

            chunks(dve, body)

        @block.gpsimd
        def _(pool):
            g = nc.gpsimd

            def front(i, b, n):
                p = n % 2
                wait(pool, resid_r, i - 1)
                settle(core, g)
                g.tensor_copy(idx[:, n:n + 1], c.pos_y[:, bass.ds(i, 1)]).then_inc(idx_done, 1)
                pool.wait_ge(idx_done, i + 1)
                settle(core, g)
                pool.indirect_dma_start(y_exp[:, p], None, c.yg_dram,
                                        bass.IndirectOffsetOnAxis(ap=idx[:, n:n + 1], axis=0)).then_inc(gathered[p], 16)
                wait(pool, e_mm, i - 1)
                g.tensor_tensor(aU[:, p, 0], c.upper[:].unsqueeze(1).to_broadcast([P, HEADS, P]),
                                a_hi[:, bass.ds(i, 1)].rearrange("p o h -> p (o h)").unsqueeze(2).to_broadcast([P, HEADS, P]),
                                ALU.mult).then_inc(aU_r, 1)
                pool.wait_ge(xs_r, i + 1)
                wait(pool, y_mm, i - 1)
                g.tensor_tensor(xsD[:, p], xs[:].rearrange("p (h e) -> p h e", h=HEADS),
                                d_row[:].unsqueeze(2).to_broadcast([P, HEADS, PW]), ALU.mult).then_inc(xsD_r, 1)
                pool.wait_ge(dtx_r, i + 1)
                pool.wait_ge(L_r, i + 1)
                g.tensor_tensor(wdtx[:, p], dtx[:, p], L[:, p, :, P - 1:P].to_broadcast([P, HEADS, PW]), ALU.mult).then_inc(wdtx_r, 1)
                if isinstance(i, int) and i == 0:
                    pool.wait_ge(b_out_in, 16)
                pool.wait_ge(xr_in[n], 32 * (b + 1))
                wait(pool, r_r, i - 1)
                g.tensor_tensor(resid[:, p], xr[:, n, 0], xr[:, n, 1], ALU.add).then_inc(resid_s, 1)
                pool.wait_ge(resid_s, 2 * i + 1)
                g.tensor_tensor(resid[:, p], resid[:, p], b_out[:], ALU.add).then_inc(resid_s, 1)
                pool.wait_ge(gathered[p], 16 * (2 * b + n // 2 + 1))
                pool.wait_ge(resid_s, 2 * i + 2)
                g.tensor_tensor(resid[:, p], resid[:, p], y_exp[:, p], ALU.add).then_inc(resid_r, 1)

            front(0, 0, 0)

            def body(i, b, n):
                if not isinstance(i, int) or i + 1 < TILES:
                    front(i + 1, b + (n + 1) // NT, (n + 1) % NT)

            chunks(pool, body)


def build(nc, ins, out):
    with ExitStack() as ctx:
        core = Core(nc, ctx, ins, out)
        core.mam = memory(core, ctx, "mamba_", MAMBA_KEEPS, dict(w_in=1))
        with ExitStack() as stage:
            core.att = memory(core, stage, "attend_", ATTEND_KEEPS, dict(stack_in=4, v_in=2))
            constants(core)
            project(core)
            core.exp_w = memory(core, stage, "expert_", EXPERT_WEIGHTS, dict(w_in=1, leading=1))
            attend(core)
            core.exp = memory(core, stage, "expert_", EXPERT_KEEPS, dict(b_in=1, w1_typed=1, w1_rest=1, w2_in=1, xg_in=4))
            prepare(core)
            experts(core)
        mamba(core)


_INS = ['L0_attn_input_tensor', 'L0_attn_ln_gamma', 'L0_attn_ln_beta', 'L0_attn_W_in', 'L0_attn_b_in',
        'L0_attn_A_log', 'L0_attn_D_skip', 'L0_attn_dt_bias', 'L0_attn_W_out', 'L0_attn_b_out', 'L0_ffn_Wq',
        'L0_ffn_bq', 'L0_ffn_Wk', 'L0_ffn_bk', 'L0_ffn_Wv', 'L0_ffn_bv', 'L0_ffn_Wo', 'L0_ffn_bo',
        'L0_ffn_router_w', 'L0_ffn_router_b', 'L0_ffn_W1', 'L0_ffn_b1', 'L0_ffn_W2', 'L0_ffn_b2',
        'L0_ffn_ln1_g', 'L0_ffn_ln1_b', 'L0_ffn_ln2_g', 'L0_ffn_ln2_b']


def kernel(**inputs):
    import numpy as np
    import concourse.bacc as bacc
    from concourse.bass_utils import run_bass_kernel_spmd

    nc = bacc.Bacc("TRN2", target_bir_lowering=False, num_devices=1)
    arrays, ins = {}, {}
    for name in _INS:
        a = np.ascontiguousarray(inputs[name])
        arrays["in_" + name] = a
        ins[name] = nc.dram_tensor("in_" + name, a.shape, mybir.dt.from_np(a.dtype), kind="ExternalInput").ap()
    out = nc.dram_tensor("out_0", (B, T, D), FP32, kind="ExternalOutput").ap()
    build(nc, ins, out)
    result = run_bass_kernel_spmd(nc, [arrays], core_ids=[0])
    return result.results[0]["out_0"]
```
